# Optimizing a Trainium2 kernel written in Bass

```python
import numpy as np
import jax
import jax.numpy as jnp

def _softmax(x, axis=-1):
    return jax.nn.softmax(x, axis=axis)

def _gelu(x):
    return jax.nn.gelu(x, approximate=True)

def _silu(x):
    return jax.nn.silu(x)

def _sigmoid(x):
    return jax.nn.sigmoid(x)

def _layernorm(x, axis=-1, eps=1e-05):
    m = jnp.mean(x, axis=axis, keepdims=True)
    v = jnp.var(x, axis=axis, keepdims=True)
    return (x - m) / jnp.sqrt(v + eps)

def _scatter_add(tgt, idx, src, axis=0):
    return tgt.at[idx].add(src)

def _segment_sum(src, seg, n):
    return jax.ops.segment_sum(src, seg, n)
kernel_name = 'mk_flamingo_gated_d2_seqx_r8_8a50b4'

def setup_inputs(seed: int=0):
    np.random.seed(seed)
    _w = jnp.asarray

    def _rec_inputs():
        import jax
        import jax.numpy as jnp
        _rk = jax.random.key(seed)
        x = 0.0002417 + 0.9998 * jax.random.normal(jax.random.fold_in(_rk, 1), (8, 128, 128), jnp.float32)
        _lenS = 128 - jax.random.randint(jax.random.fold_in(_rk, 7), (8,), 0, max(1, 128 // 4) + 1, jnp.int32)
        _lenS2 = 128 - jax.random.randint(jax.random.fold_in(_rk, 8), (8,), 0, max(1, 128 // 4) + 1, jnp.int32)
        _ctx_1024P = jax.random.normal(jax.random.fold_in(_rk, 11), (8, 16, 128), jnp.float32)
        _ctx_1024c = jax.random.dirichlet(jax.random.fold_in(_rk, 511), 0.3 * jnp.ones((16,), jnp.float32), (8, 128))
        _ctx_1024t = jnp.einsum('bsk,bkd->bsd', _ctx_1024c, _ctx_1024P)
        _ctx_1024t = _ctx_1024t * jax.lax.rsqrt(jnp.mean(jnp.square(_ctx_1024t)) + 1e-12) * 0.953939
        ctx_1024 = 7.22013e-05 + 1.00017 * (_ctx_1024t + 0.3 * jax.random.normal(jax.random.fold_in(_rk, 611), (8, 128, 128), jnp.float32))
        _validS = jnp.arange(128)[None, :] < _lenS[:, None]
        _validS2 = jnp.arange(128)[None, :] < _lenS2[:, None]
        _causal = jnp.tril(jnp.ones((128, 128), dtype=bool))
        mask_Bx1xSxS2_ik1 = jnp.where(jnp.broadcast_to(_validS2[:, None, None, :], (8, 1, 128, 128)), 1, 0).astype(jnp.int32)
        mask_BxS2_if1 = jnp.where(jnp.ones((8, 128), dtype=bool), 1, 0).astype(jnp.int32)
        _g = jax.random.normal(jax.random.fold_in(_rk, 9001), (2, 2), jnp.float32)
        _g = jnp.sign(_g) * jnp.maximum(jnp.abs(_g), 1.0) + (_g == 0) * 1.0
        g_xattn = _g[0]
        g_ffn = _g[1]
        return (x, ctx_1024, mask_Bx1xSxS2_ik1, mask_BxS2_if1, g_xattn, g_ffn)
    x, ctx_1024, mask_Bx1xSxS2_ik1, mask_BxS2_if1, g_xattn, g_ffn = _rec_inputs()

    def _L0_xattn_setup():
        import jax, jax.numpy as jnp
        import numpy as np
        HEADS = 16
        EMBED = 128
        HEAD_DIM = EMBED // HEADS
        key = jax.random.key(seed)
        ks = jax.random.split(key, 6)
        N, S, E = (4, 256, EMBED)
        return {'value': jax.random.normal(ks[0], (N, S, E), dtype=jnp.float32), 'key': jax.random.normal(ks[1], (N, S, E), dtype=jnp.float32), 'query': jax.random.normal(ks[2], (N, S, E), dtype=jnp.float32), 'mask': jax.random.randint(ks[3], (N, 1, S, S), 0, 2, dtype=jnp.int32), 'w_out': jax.random.normal(ks[4], (E, E), dtype=jnp.float32) * E ** (-0.5), 'b_out': jax.random.normal(ks[5], (E,), dtype=jnp.float32) * 0.01}
    _L0_xattn_all = _L0_xattn_setup()
    _L0_xattn_in = {k: v for k, v in _L0_xattn_all.items() if k in ('w_out', 'b_out')}
    del _L0_xattn_all

    def _L0_ffn_setup():
        import jax, jax.numpy as jnp
        import numpy as np
        B, S, H, F, E = (8, 256, 128, 512, 8)
        INIT_LAMBDA = 0.2
        key = jax.random.key(seed)
        ks = jax.random.split(key, 12)
        std = 0.02
        return {'hidden_states': jax.random.normal(ks[0], (B, S, H), jnp.float32), 'gate_w1': jax.random.normal(ks[1], (H, H), jnp.float32) * 0.01, 'gate_b1': jnp.zeros((H,), jnp.float32), 'gate_w2': jax.random.normal(ks[2], (E, H), jnp.float32) * 0.01, 'gate_b2': jnp.full((E,), INIT_LAMBDA, jnp.float32), 'W1': jax.random.normal(ks[3], (F, H), jnp.float32) * std, 'b1': jax.random.normal(ks[4], (F,), jnp.float32) * std, 'W2': jax.random.normal(ks[5], (H, F), jnp.float32) * std, 'b2': jax.random.normal(ks[6], (H,), jnp.float32) * std, 'TW1': jax.random.normal(ks[7], (E, F, H), jnp.float32) * std, 'Tb1': jax.random.normal(ks[8], (E, F), jnp.float32) * std, 'TW2': jax.random.normal(ks[9], (E, H, F), jnp.float32) * std, 'Tb2': jax.random.normal(ks[10], (E, H), jnp.float32) * std}
    _L0_ffn_all = _L0_ffn_setup()
    _L0_ffn_in = {k: v for k, v in _L0_ffn_all.items() if k in ('gate_w1', 'gate_b1', 'gate_w2', 'gate_b2', 'W1', 'b1', 'W2', 'b2', 'TW1', 'Tb1', 'TW2', 'Tb2')}
    del _L0_ffn_all

    def _L1_xattn_setup():
        import jax, jax.numpy as jnp
        import numpy as np
        M_DIM = 128
        H_DIM = 128
        NEG = -1000000000.0
        key = jax.random.key(seed)
        ks = jax.random.split(key, 9)
        B, S = (4, 256)
        q = jax.random.normal(ks[0], (B, S, M_DIM), dtype=jnp.float32)
        k = jax.random.normal(ks[1], (B, S, M_DIM), dtype=jnp.float32)
        v = jax.random.normal(ks[2], (B, S, M_DIM), dtype=jnp.float32)
        attention_mask = jnp.ones((B, S), dtype=jnp.int32)
        sc = 1.0 / np.sqrt(M_DIM)
        Wq_w = jax.random.normal(ks[3], (H_DIM, M_DIM), dtype=jnp.float32) * sc
        Wq_b = jnp.zeros((H_DIM,), dtype=jnp.float32)
        Wk_w = jax.random.normal(ks[4], (H_DIM, M_DIM), dtype=jnp.float32) * sc
        Wk_b = jnp.zeros((H_DIM,), dtype=jnp.float32)
        Wv_w = jax.random.normal(ks[5], (H_DIM, M_DIM), dtype=jnp.float32) * sc
        Wv_b = jnp.zeros((H_DIM,), dtype=jnp.float32)
        return {'q': q, 'k': k, 'v': v, 'attention_mask': attention_mask, 'Wq_w': Wq_w, 'Wq_b': Wq_b, 'Wk_w': Wk_w, 'Wk_b': Wk_b, 'Wv_w': Wv_w, 'Wv_b': Wv_b}
    _L1_xattn_all = _L1_xattn_setup()
    _L1_xattn_in = {k: v for k, v in _L1_xattn_all.items() if k in ('Wq_w', 'Wq_b', 'Wk_w', 'Wk_b', 'Wv_w', 'Wv_b')}
    del _L1_xattn_all

    def _L1_ffn_setup():
        import jax, jax.numpy as jnp
        import numpy as np
        E = 16
        H = 128
        F = 256
        TOP_K = 1
        B, S = (2, 128)
        key = jax.random.key(seed)
        ks = jax.random.split(key, 7)
        s = 0.02
        return {'hidden_states': jax.random.normal(ks[0], (B, S, H), jnp.float32), 'w_router': jax.random.normal(ks[1], (E, H), jnp.float32) * s, 'gate_up_proj': jax.random.normal(ks[2], (E, H, 2 * F), jnp.float32) * s, 'down_proj': jax.random.normal(ks[3], (E, F, H), jnp.float32) * s, 'w_gate': jax.random.normal(ks[4], (F, H), jnp.float32) * s, 'w_up': jax.random.normal(ks[5], (F, H), jnp.float32) * s, 'w_down': jax.random.normal(ks[6], (H, F), jnp.float32) * s}
    _L1_ffn_all = _L1_ffn_setup()
    _L1_ffn_in = {k: v for k, v in _L1_ffn_all.items() if k in ('w_router', 'gate_up_proj', 'down_proj', 'w_gate', 'w_up', 'w_down')}
    del _L1_ffn_all
    return {'x': x, 'ctx_1024': ctx_1024, 'mask_Bx1xSxS2_ik1': mask_Bx1xSxS2_ik1, 'mask_BxS2_if1': mask_BxS2_if1, 'g_xattn': g_xattn, 'g_ffn': g_ffn, 'L0_xattn_w_out': _L0_xattn_in['w_out'], 'L0_xattn_b_out': _L0_xattn_in['b_out'], 'L0_ffn_gate_w1': _L0_ffn_in['gate_w1'], 'L0_ffn_gate_b1': _L0_ffn_in['gate_b1'], 'L0_ffn_gate_w2': _L0_ffn_in['gate_w2'], 'L0_ffn_gate_b2': _L0_ffn_in['gate_b2'], 'L0_ffn_W1': _L0_ffn_in['W1'], 'L0_ffn_b1': _L0_ffn_in['b1'], 'L0_ffn_W2': _L0_ffn_in['W2'], 'L0_ffn_b2': _L0_ffn_in['b2'], 'L0_ffn_TW1': _L0_ffn_in['TW1'], 'L0_ffn_Tb1': _L0_ffn_in['Tb1'], 'L0_ffn_TW2': _L0_ffn_in['TW2'], 'L0_ffn_Tb2': _L0_ffn_in['Tb2'], 'L1_xattn_Wq_w': _L1_xattn_in['Wq_w'], 'L1_xattn_Wq_b': _L1_xattn_in['Wq_b'], 'L1_xattn_Wk_w': _L1_xattn_in['Wk_w'], 'L1_xattn_Wk_b': _L1_xattn_in['Wk_b'], 'L1_xattn_Wv_w': _L1_xattn_in['Wv_w'], 'L1_xattn_Wv_b': _L1_xattn_in['Wv_b'], 'L1_ffn_w_router': _L1_ffn_in['w_router'], 'L1_ffn_gate_up_proj': _L1_ffn_in['gate_up_proj'], 'L1_ffn_down_proj': _L1_ffn_in['down_proj'], 'L1_ffn_w_gate': _L1_ffn_in['w_gate'], 'L1_ffn_w_up': _L1_ffn_in['w_up'], 'L1_ffn_w_down': _L1_ffn_in['w_down']}

def reference(x, ctx_1024, mask_Bx1xSxS2_ik1, mask_BxS2_if1, g_xattn, g_ffn, L0_xattn_w_out, L0_xattn_b_out, L0_ffn_gate_w1, L0_ffn_gate_b1, L0_ffn_gate_w2, L0_ffn_gate_b2, L0_ffn_W1, L0_ffn_b1, L0_ffn_W2, L0_ffn_b2, L0_ffn_TW1, L0_ffn_Tb1, L0_ffn_TW2, L0_ffn_Tb2, L1_xattn_Wq_w, L1_xattn_Wq_b, L1_xattn_Wk_w, L1_xattn_Wk_b, L1_xattn_Wv_w, L1_xattn_Wv_b, L1_ffn_w_router, L1_ffn_gate_up_proj, L1_ffn_down_proj, L1_ffn_w_gate, L1_ffn_w_up, L1_ffn_w_down):
    import jax
    import jax.numpy as jnp

    def _L0_xattn_ref(value, key, query, mask, w_out, b_out):
        import jax, jax.numpy as jnp
        import numpy as np
        HEADS = 16
        EMBED = 128
        HEAD_DIM = EMBED // HEADS
        N, Q, E = query.shape
        K = key.shape[1]
        H, D = (HEADS, HEAD_DIM)
        q = query.reshape(N, Q, H, D)
        k = key.reshape(N, K, H, D)
        v = value.reshape(N, K, H, D)
        energy = jnp.einsum('nqhd,nkhd->nhqk', q, k)
        energy = jnp.where(mask == 0, jnp.float32(-1e+22), energy)
        attn = jax.nn.softmax(energy / jnp.sqrt(jnp.float32(E)), axis=-1)
        out = jnp.einsum('nhqk,nkhd->nqhd', attn, v).reshape(N, Q, H * D)
        return out @ w_out.T + b_out

    def _L0_ffn_ref(hidden_states, gate_w1, gate_b1, gate_w2, gate_b2, W1, b1, W2, b2, TW1, Tb1, TW2, Tb2):
        import jax, jax.numpy as jnp
        import numpy as np
        B, S, H, F, E = (8, 256, 128, 512, 8)
        INIT_LAMBDA = 0.2
        x = hidden_states
        h = jax.nn.relu(jnp.einsum('bsh,oh->bso', x, gate_w1) + gate_b1)
        g = jnp.einsum('bso,eo->bse', h, gate_w2) + gate_b2
        g = g.mean(axis=1)
        mW1 = W1 + jnp.einsum('be,efh->bfh', g, TW1)
        mb1 = b1 + g @ Tb1
        mW2 = W2 + jnp.einsum('be,ehf->bhf', g, TW2)
        mb2 = b2 + g @ Tb2
        u = jax.nn.gelu(jnp.einsum('bsh,bfh->bsf', x, mW1) + mb1[:, None, :])
        out = jnp.einsum('bsf,bhf->bsh', u, mW2) + mb2[:, None, :]
        return out

    def _L1_xattn_ref(q, k, v, attention_mask, Wq_w, Wq_b, Wk_w, Wk_b, Wv_w, Wv_b):
        import jax, jax.numpy as jnp
        import numpy as np
        M_DIM = 128
        H_DIM = 128
        NEG = -1000000000.0
        qh = jnp.einsum('bsm,hm->bsh', q, Wq_w) + Wq_b
        kh = jnp.einsum('bsm,hm->bsh', k, Wk_w) + Wk_b
        vh = jnp.einsum('bsm,hm->bsh', v, Wv_w) + Wv_b
        scores = jnp.einsum('bqh,bkh->bqk', qh, kh) / jnp.sqrt(jnp.float32(H_DIM))
        pad = attention_mask.astype(bool)[:, None, :]
        scores = jnp.where(pad, scores, NEG)
        Sq, Sk = (scores.shape[1], scores.shape[2])
        causal = jnp.tril(jnp.ones((Sq, Sk), dtype=bool))
        scores = jnp.where(causal[None, :, :], scores, NEG)
        attn = jax.nn.softmax(scores, axis=-1)
        out = jnp.einsum('bqk,bkh->bqh', attn, vh)
        return out

    def _L1_ffn_ref(hidden_states, w_router, gate_up_proj, down_proj, w_gate, w_up, w_down):
        import jax, jax.numpy as jnp
        import numpy as np
        E = 16
        H = 128
        F = 256
        TOP_K = 1
        B, S = (2, 128)
        b, s, h = hidden_states.shape
        x = hidden_states.reshape(-1, h)
        logits = x @ w_router.T
        _, top_idx = jax.lax.top_k(logits, TOP_K)
        mask = jax.nn.one_hot(top_idx, E, dtype=logits.dtype).sum(axis=1)
        scores = jax.nn.sigmoid(logits) * mask
        masked_inputs = scores.T[:, :, None] * x[None, :, :]
        gate_up = jnp.einsum('eth,ehf->etf', masked_inputs, gate_up_proj)
        gate, up = jnp.split(gate_up, 2, axis=-1)
        expert_out = jnp.einsum('etf,efh->eth', up * jax.nn.silu(gate), down_proj)
        shared = jax.nn.silu(x @ w_gate.T) * (x @ w_up.T) @ w_down.T
        out = shared + expert_out.sum(axis=0)
        return out.reshape(b, s, h)
    x = x + jnp.tanh(g_xattn[0]) * _L0_xattn_ref(ctx_1024, ctx_1024, _layernorm(x, axis=-1), mask_Bx1xSxS2_ik1, L0_xattn_w_out, L0_xattn_b_out)
    x = x + jnp.tanh(g_ffn[0]) * _L0_ffn_ref(_layernorm(x, axis=-1), L0_ffn_gate_w1, L0_ffn_gate_b1, L0_ffn_gate_w2, L0_ffn_gate_b2, L0_ffn_W1, L0_ffn_b1, L0_ffn_W2, L0_ffn_b2, L0_ffn_TW1, L0_ffn_Tb1, L0_ffn_TW2, L0_ffn_Tb2)
    x = x + jnp.tanh(g_xattn[1]) * _L1_xattn_ref(_layernorm(x, axis=-1), ctx_1024, ctx_1024, mask_BxS2_if1, L1_xattn_Wq_w, L1_xattn_Wq_b, L1_xattn_Wk_w, L1_xattn_Wk_b, L1_xattn_Wv_w, L1_xattn_Wv_b)
    x = x + jnp.tanh(g_ffn[1]) * _L1_ffn_ref(_layernorm(x, axis=-1), L1_ffn_w_router, L1_ffn_gate_up_proj, L1_ffn_down_proj, L1_ffn_w_gate, L1_ffn_w_up, L1_ffn_w_down)
    return x

_drawn_inputs = setup_inputs


def setup_inputs(seed=0):
    import zlib

    import numpy as np

    out = dict(_drawn_inputs(seed))
    spreads = {'g_ffn': (-1.0, 0.6),
     'L0_ffn_gate_b1': (0.0, 0.8),
     'L0_ffn_gate_b2': (0.20000000298023224, 0.6),
     'L1_xattn_Wq_b': (0.0, 0.336),
     'L1_xattn_Wk_b': (0.0, 0.8),
     'L1_xattn_Wv_b': (0.0, 0.1)}
    factors = {'L0_xattn_b_out': 7.454,
     'L0_ffn_gate_w1': 8.0,
     'L0_ffn_gate_w2': 8.0,
     'L0_ffn_b1': 8.0,
     'L0_ffn_b2': 4.071,
     'L0_ffn_Tb1': 8.0,
     'L0_ffn_Tb2': 8.0,
     'L1_ffn_w_router': 8.0,
     'L1_ffn_gate_up_proj': 8.0,
     'L1_ffn_down_proj': 8.0,
     'L1_ffn_w_gate': 8.0,
     'L1_ffn_w_up': 8.0,
     'L1_ffn_w_down': 8.0}
    for name, (base, spread) in spreads.items():
        noise = np.random.default_rng([zlib.crc32(name.encode()), seed]).standard_normal(out[name].shape)
        drawn = base * np.exp(spread * noise) if base else spread * noise
        out[name] = jnp.asarray(drawn.astype(out[name].dtype))
    for name, factor in factors.items():
        out[name] = (out[name] * factor).astype(out[name].dtype)
    return out
```

```python
from contextlib import ExitStack

import concourse.bass as bass
from concourse import mybir

ALU = mybir.AluOpType
ACT = mybir.ActivationFunctionType
F32 = mybir.dt.float32
BF16 = mybir.dt.bfloat16
I32 = mybir.dt.int32
U32 = mybir.dt.uint32
X = mybir.AxisListType.X

P = 128
MASKED_L0 = -1.0e22
MASKED_L1 = -1.0e30
EPS = 1e-5
LN_EXP_SET = "natural_log_exp_and_others"
NO_TOKEN = 1 << 20


def flamingo_gated_blocks(nc, a, out):
    B, S, D = a["x"].shape
    HEADS = 16
    HD = D // HEADS
    E0, F0, _ = a["L0_ffn_TW1"].shape
    FC = F0 // P
    RO = P // E0
    E1, _, F1X2 = a["L1_ffn_gate_up_proj"].shape
    F1 = F1X2 // 2
    C1 = F1 // P
    assert S == P and D == P and B == 8 and HD * HEADS == D
    SCALE = float(D) ** -0.5
    HG = 4
    UB = HEADS // HG
    UNITS = UB * B
    TILES = B * S // P + E1 - 1
    MIN_PAIRS = B * S // P // 2
    LOADED = TILES + 2
    ROW = D + 1

    ctx = ExitStack()
    with ctx:
        def sb(name, shape, dt=F32):
            return ctx.enter_context(nc.sbuf_tensor(name, shape, dt))

        bank = [ctx.enter_context(nc.psum_tensor(f"bank{i}", [P, 512], F32)) for i in range(8)]
        token_rows = nc.dram_tensor("token_rows", (B, S, D), F32, kind="Internal").ap()
        sorted_rows = nc.dram_tensor("sorted_rows", (LOADED * P, ROW), F32, kind="Internal").ap()

        x = sb("x", [P, B, D])
        c = sb("c", [P, B, D])
        early = sb("early", [P, 35, P])
        mask_i = early[:, 0:8, :].bitcast(I32)
        pad_i = early[:, 8:16, :].bitcast(I32)
        w_raw = early[:, 16:35, :]
        mW2T = early[:, 0:32, :].rearrange("p (b c) (q r) -> p b c q r", b=B, r=RO)
        w_t = sb("w_t", [P, 19, P])
        WO, GW1, WK, WV, W1, W2, WQ, WG, WU, WD = 0, 1, 2, 3, 4, 8, 12, 13, 15, 17
        w_small = sb("w_small", [P, 2, P])
        gate2T = sb("gate2T", [P, E0])
        routerT = sb("routerT", [P, E1])
        b_out = sb("b_out", [P, D])
        b_v = sb("b_v", [P, D])
        gates = sb("gates", [P, 4])
        tgate = sb("tgate", [P, 4])
        b_g1 = sb("b_g1", [P, 1])
        b_q = sb("b_q", [P, 1])
        b_k = sb("b_k", [P, 1])
        b_1 = sb("b_1", [P, FC])
        b_g2 = sb("b_g2", [E0, 1])
        tb1 = sb("tb1", [E0, F0])
        tb2 = sb("tb2", [E0 + 1, D])
        tw1 = sb("tw1", [P, F0 // RO, D])
        tw2 = sb("tw2", [P, D // RO, F0])
        gate_up = sb("gate_up", [P, E1, 2 * F1])
        down = sb("down", [P, E1, C1, D])

        ident = sb("ident", [P, P])
        ident_b = sb("ident_b", [P, P], BF16)
        before = sb("before", [P, P], BF16)
        ones_b = sb("ones_b", [P, P], BF16)
        head_of = sb("head_of", [P, HEADS])
        same_row = sb("same_row", [P, RO])
        spread = sb("spread", [E0, P])
        eps = sb("eps", [P, 1])
        minus_half = sb("minus_half", [P, 1])
        empty_row = sb("empty_row", [P, ROW])
        expert_no = sb("expert_no", [P, E1])
        tile_no = sb("tile_no", [P, LOADED])
        lower = sb("lower", [P, E1, E1])

        mask_b = sb("mask_b", [P, B, P], BF16)
        pad_f = sb("pad_f", [P, B, P], BF16)
        pad_b = sb("pad_b", [P, B, P], BF16)
        cT = sb("cT", [P, B, P])
        kT = sb("kT", [P, B, P])
        vh = sb("vh", [P, B, D])
        xn = sb("xn", [P, B, D])
        xnT = sb("xnT", [P, B, P])
        keys2 = sb("keys2", [P, 2 * HEADS, P])
        keys = [keys2[:, HEADS * i:HEADS * (i + 1), :] for i in range(2)]
        mW1T = keys2[:, :, :].rearrange("p (b c) (q r) -> p b (c q) r", b=B, r=RO)
        vals = [sb(f"vals{i}", [P, HEADS, 32]) for i in range(2)]
        probs = [sb(f"probs{i}", [P, HG, P]) for i in range(3)]
        probsT = [sb(f"probsT{i}", [P, HG, P]) for i in range(2)]
        neg_max = sb("neg_max", [P, UNITS, HG])
        rden = sb("rden", [P, B, HEADS])
        o_headsT = sb("o_headsT", [P, UB, P])
        o_rows = [sb(f"o_rows{i}", [P, HEADS, HD]) for i in range(2)]
        oT = sb("oT", [P, P])
        stats = sb("stats", [P, B, 6])
        mv = sb("mv", [P, 4, B, 2])
        var_ln = sb("var_ln", [P, B])
        var_eps = sb("var_eps", [P, B])
        rstd = sb("rstd", [P, 4, B])

        relu_out = sb("relu_out", [P, P])
        h_sum = sb("h_sum", [P, B])
        gT = sb("gT", [E0, B])
        g_rows = sb("g_rows", [E0 + 1, B, P])
        g_col = sb("g_col", [P, B])
        g_mix = sb("g_mix", [P, B, RO])
        mb1 = sb("mb1", [P, FC, B])
        uT = [sb(f"uT{i}", [P, FC, P]) for i in range(2)]

        q1T = [sb(f"q1T{i}", [P, P]) for i in range(2)]
        p1 = c
        routed_in = c
        p1T = [sb(f"p1T{i}", [P, P]) for i in range(2)]
        neg_max1 = sb("neg_max1", [P, B])
        den1 = sb("den1", [P, B])
        rden1 = sb("rden1", [P, B])

        logit_max = sb("logit_max", [P, B])
        score = sb("score", [P, B])
        tmp_be = sb("tmp_be", [P, B, E1])
        choice = sb("choice", [P, B])
        one_hot = sb("one_hot", [P, B, E1])
        one_hot_b = sb("one_hot_b", [P, B, E1], BF16)
        tiles_i = sb("tiles_i", [P, E1], I32)
        tiles_f = sb("tiles_f", [P, E1])
        tmp_ee = sb("tmp_ee", [P, E1, E1])
        first = sb("first", [P, E1])
        end_tile = sb("end_tile", [P, E1])
        tmp_te = sb("tmp_te", [P, LOADED, E1])
        tile_expert_f = sb("tile_expert_f", [P, LOADED])
        tile_expert = sb("tile_expert", [P, LOADED], I32)
        pairs_f = sb("pairs_f", [P, 1])
        pairs_i = sb("pairs_i", [P, 1], I32)
        slot_f = sb("slot_f", [P, B])
        slot_i = sb("slot_i", [P, B], I32)
        x_rows = sb("x_rows", [P, B, ROW])

        sharedT = tw1[:, 0:C1 * B, :].rearrange("p (c b) t -> p c b t", b=B)
        silu_sh = [tw1[:, 16 + 4 * i:20 + 4 * i, :].rearrange("p c t -> p (c t)") for i in range(2)]
        tail = tw2[:, :, :].rearrange("p q (c t) -> p (q c) t", t=P)
        xs_T = [tail[:, i, :] for i in range(2)]
        silu_g = [tail[:, 2 + 2 * i:4 + 2 * i, :].rearrange("p c t -> p (c t)") for i in range(2)]
        act_r = [tail[:, 6 + 2 * i:8 + 2 * i, :].rearrange("p c t -> p (c t)") for i in range(2)]
        act_T = [tail[:, 10 + 2 * i:12 + 2 * i, :] for i in range(2)]
        xs_in = [sb(f"xs_in{i}", [P, ROW]) for i in range(2)]
        tokens = sb("tokens", [P, LOADED], I32)
        token_of = [sb(f"token_of{i}", [P, 1], I32) for i in range(2)]
        y_out = [tail[:, 14 + i, :] for i in range(2)]

        names = """gates_loaded x_loaded c_loaded mask_loaded w_loaded small_loaded tw1_loaded tw2_loaded experts_loaded
            vector_step scalar_step pool_step
            ident_made consts_bf16 consts_made eps_made empty_made heads_made spread_made tanh_made
            bout_scaled wout_scaled x_plus_bout vh_scaled pad_copied pad_made mask_made
            var_ready rstd_ready xn_written rows_T rows_T_out_v rows_T_out_s
            pre_ready pre_out_v pre_out_s keys_made vals_made
            scores max_made probs_made probs_T probs_T_out heads_out heads_T_out heads_back o_normed o_T o_T_out
            projected x1_made xn2_made xn2_T xn2_T_out gate_hidden gate_summed
            gate_out g_made g_spread mix_inputs mixed mixed_out hidden gelu_made ffn_out x2_made
            var3_ready rstd3_ready xn3_made xn3_T xn3_T_out q_ready q_out scores1 max1_made probs1 probs1_T probs1_T_out
            attn1 x3_made var4_ready rstd4_ready xn4_made xn4_T xn4_T_out
            logits logit_max_made exp_made one_hot_made ranks slots_made tiles_made rows_scaled rows_filled rows_sorted
            shared_hidden shared_silu shared_act shared_out acc_made
            tile_loaded0 tile_loaded1 tile_T tile_T_out tile_hidden tile_silu tile_act act_T_ready act_T_out
            tile_y y_ready tokens_taken scatter_begun routed_loaded0 routed_loaded1 out_made out_stored y_scattered0 y_scattered1""".split()
        sem = {n: ctx.enter_context(nc.semaphore(n)) for n in names}
        tile_loaded = [sem["tile_loaded0"], sem["tile_loaded1"]]
        y_scattered = [sem["y_scattered0"], sem["y_scattered1"]]

        block = ctx.enter_context(nc.Block())

        def as_row(v):
            return v.rearrange("(a d) -> a d", a=1)

        def as_col(v):
            return v.rearrange("(d a) -> d a", a=1)

        def in_bank(i, n=4):
            return bank[i][:, 0:n * P].rearrange("p (b t) -> p b t", t=P)

        PRE = [("cT", 0, "s"), ("cT", 1, "s"), ("xn", 0, "v"), ("xn", 1, "s"), ("w", 0, "v"), ("w", 1, "s"),
               ("w", 2, "v"), ("w", 3, "s"), ("w", 4, "v"), ("small", 0, "v"),
               ("k", 0, "v"), ("k", 1, "v"), ("v", 0, "v"), ("v", 1, "v")]
        PB = 6
        W_GROUPS = [(0, 4), (4, 8), (8, 12), (12, 16), (16, 19)]

        def pre_emptied(n):
            e = PRE[n][2]
            return sem["pre_out_" + e], sum(1 for p in PRE[:n + 1] if p[2] == e)

        def chain_row(step, offset):
            b, r = divmod(step - offset, UB)
            return b if r == 0 and 0 <= b < B else None

        STEPS = UNITS + 9

        @block.sync
        def _(sp):
            def load(dst, src, s, **kw):
                sp.dma_start(dst, src, **kw).then_inc(sem[s], 16)

            load(gates[:, 0:2], as_row(a["g_xattn"]).partition_broadcast(P), "gates_loaded")
            load(gates[:, 2:4], as_row(a["g_ffn"]).partition_broadcast(P), "gates_loaded")
            load(x[:], a["x"].rearrange("b s d -> s b d"), "x_loaded")
            load(mask_i, a["mask_Bx1xSxS2_ik1"].rearrange("b o s k -> s (b o) k"), "mask_loaded")
            for slot, name in ((WO, "L0_xattn_w_out"), (GW1, "L0_ffn_gate_w1"), (WK, "L1_xattn_Wk_w"),
                               (WV, "L1_xattn_Wv_w"), (WQ, "L1_xattn_Wq_w")):
                load(w_raw[:, slot, :], a[name], "w_loaded")
            for slot, name, n in ((W1, "L0_ffn_W1", FC), (WG, "L1_ffn_w_gate", C1), (WU, "L1_ffn_w_up", C1)):
                load(w_raw[:, slot:slot + n, :], a[name].rearrange("(c f) h -> f c h", c=n), "w_loaded")
            load(w_raw[:, W2:W2 + FC, :], a["L0_ffn_W2"].rearrange("h (c f) -> h c f", c=FC), "w_loaded")
            load(w_raw[:, WD:WD + C1, :], a["L1_ffn_w_down"].rearrange("h (c f) -> h c f", c=C1), "w_loaded")
            load(w_small[0:E0, 0, :], a["L0_ffn_gate_w2"], "w_loaded")
            load(w_small[0:E1, 1, :], a["L1_ffn_w_router"], "w_loaded")
            load(b_out[:], as_row(a["L0_xattn_b_out"]).partition_broadcast(P), "small_loaded")
            load(b_v[:], as_row(a["L1_xattn_Wv_b"]).partition_broadcast(P), "small_loaded")
            for dst, name in ((b_g1, "L0_ffn_gate_b1"), (b_q, "L1_xattn_Wq_b"), (b_k, "L1_xattn_Wk_b"),
                              (b_g2, "L0_ffn_gate_b2")):
                load(dst[:], as_col(a[name]), "small_loaded")
            load(b_1[:], a["L0_ffn_b1"].rearrange("(c f) -> f c", c=FC), "small_loaded", allow_slow_non_contiguous=True)
            load(tb1[:], a["L0_ffn_Tb1"], "small_loaded")
            load(tb2[0:E0, :], a["L0_ffn_Tb2"], "small_loaded")
            load(tb2[E0:E0 + 1, :], as_row(a["L0_ffn_b2"]), "small_loaded")
            load(pad_i, a["mask_BxS2_if1"].rearrange("(o b) k -> o b k", o=1).partition_broadcast(P), "small_loaded")
            for e in range(E0):
                load(tw1[RO * e:RO * e + RO, :, :], a["L0_ffn_TW1"][e].rearrange("(q r) h -> r q h", r=RO), "tw1_loaded")
            for e in range(E0):
                load(tw2[RO * e:RO * e + RO, :, :], a["L0_ffn_TW2"][e].rearrange("(q r) f -> r q f", r=RO), "tw2_loaded")
            load(gate_up[:], a["L1_ffn_gate_up_proj"].rearrange("e h f -> h e f"), "experts_loaded")
            load(down[:], a["L1_ffn_down_proj"].rearrange("e (c f) h -> f e c h", c=C1), "experts_loaded")
            sp.wait_ge(sem["empty_made"], 2)
            load(sorted_rows.rearrange("(t p) r -> p t r", p=P),
                 empty_row[:, :].unsqueeze(1).to_broadcast([P, LOADED, ROW]), "rows_filled")
            sp.wait_ge(sem["rows_sorted"], 16 * B)
            sp.wait_ge(sem["tiles_made"], 1)
            pairs = sp.value_load(pairs_i[0:1, 0:1], min_val=MIN_PAIRS, max_val=TILES // 2)
            for t in range(3):
                if t == 2:
                    sp.wait_ge(sem["tokens_taken"], 1)
                    sp.wait_ge(sem["tile_T"], 1)
                load(xs_in[t % 2][:], sorted_rows[t * P:(t + 1) * P, :], f"tile_loaded{t % 2}")
            with sp.Fori(0, pairs) as i:
                for k in (1, 0):
                    t = 2 * i + 4 - k
                    sp.wait_ge(sem["tokens_taken"], t - 1)
                    sp.wait_ge(sem["tile_T"], t - 1)
                    load(xs_in[k][:], sorted_rows[bass.ds(t * P, P), :], f"tile_loaded{k}")
            sp.wait_ge(y_scattered[0], 16 * pairs + 16)
            sp.wait_ge(y_scattered[1], 16 * pairs)
            for h in range(2):
                load(routed_in[:, 4 * h:4 * h + 4, :], token_rows[4 * h:4 * h + 4].rearrange("b s d -> s b d"),
                     f"routed_loaded{h}")
            for h in range(2):
                sp.wait_ge(sem["out_made"], h + 1)
                sp.dma_start(out[4 * h:4 * h + 4].rearrange("b s d -> s b d"),
                             routed_in[:, 4 * h:4 * h + 4, :]).then_inc(sem["out_stored"], 16)
            sp.wait_ge(sem["out_stored"], 32)

        @block.gpsimd
        def _(pool):
            steps = [0]

            def step(i):
                steps[0] += 1
                i.then_inc(sem["pool_step"], 1)
                pool.wait_ge(sem["pool_step"], steps[0])

            pool.memset(eps[:], EPS).then_inc(sem["eps_made"], 1)
            step(pool.memset(ident[:], 0.0))
            pool.affine_select(out=ident[:], in_=ident[:], compare_op=ALU.not_equal, fill=1.0, base=0,
                               pattern=[[-1, P]], channel_multiplier=1).then_inc(sem["ident_made"], 1)
            pool.memset(vals[0][:], 0.0).then_inc(sem["pool_step"], 1)
            step(pool.memset(vals[1][:], 0.0))
            steps[0] += 1
            pool.wait_ge(sem["pool_step"], steps[0])
            for i in range(2):
                pool.memset(vals[i][:, :, HD:HD + 1], 1.0).then_inc(sem["consts_made"], 1)

            def make_vals(b):
                if b >= 2:
                    pool.wait_ge(sem["heads_out"], UB * (b - 1))
                pool.tensor_copy(vals[b % 2][:, :, 0:HD], c[:, b, :].rearrange("p (h d) -> p h d", d=HD)
                                 ).then_inc(sem["vals_made"], 1)

            def make_keys(b):
                pool.wait_ge(*pre_emptied(b // 4))
                if b >= 2:
                    pool.wait_ge(sem["scores"], UB * (b - 1))
                pool.tensor_tensor(keys[b % 2], cT[:, b:b + 1, :].to_broadcast([P, HEADS, P]),
                                   head_of[:, :].unsqueeze(2).to_broadcast([P, HEADS, P]), ALU.mult
                                   ).then_inc(sem["keys_made"], 1)

            pool.wait_ge(sem["c_loaded"], 16)
            pool.wait_ge(sem["heads_made"], 1)
            pool.wait_ge(*pre_emptied(0))
            make_keys(0)
            pool.wait_ge(sem["ident_made"], 1)
            pool.tensor_copy(ident_b[:], ident[:]).then_inc(sem["consts_bf16"], 1)
            make_vals(0)
            make_keys(1)
            make_vals(1)
            pool.wait_ge(sem["tanh_made"], 1)
            pool.wait_ge(*pre_emptied(4))
            pool.tensor_scalar(w_t[:, WO, :], w_t[:, WO, :], tgate[:, 0:1], None, ALU.mult).then_inc(sem["wout_scaled"], 1)
            pool.wait_ge(sem["small_loaded"], 11 * 16)
            step(pool.tensor_scalar(b_out[:], b_out[:], tgate[:, 0:1], None, ALU.mult))
            pool.wait_ge(sem["xn_written"], B)
            pool.tensor_tensor(x[:], x[:], b_out[:, :].unsqueeze(1).to_broadcast([P, B, D]), ALU.add
                               ).then_inc(sem["x_plus_bout"], 1)
            make_keys(2)
            make_vals(2)
            pool.memset(g_rows[:], 1.0).then_inc(sem["consts_made"], 1)
            pool.memset(minus_half[:], -0.5).then_inc(sem["consts_made"], 1)
            pool.memset(ones_b[:], 1.0).then_inc(sem["consts_bf16"], 1)
            step(pool.memset(before[:], 1.0))
            pool.affine_select(out=before[:], in_=before[:], compare_op=ALU.is_gt, fill=0.0, base=0,
                               pattern=[[1, P]], channel_multiplier=-1).then_inc(sem["consts_bf16"], 1)
            make_keys(3)
            make_vals(3)
            step(pool.memset(lower[:], 1.0))
            pool.affine_select(out=lower[:], in_=lower[:], compare_op=ALU.is_gt, fill=0.0, base=0,
                               pattern=[[1, E1], [-1, E1]], channel_multiplier=0).then_inc(sem["consts_made"], 1)
            pool.iota(expert_no[:], [[1, E1]], base=0, channel_multiplier=0,
                      allow_small_or_imprecise_dtypes=True).then_inc(sem["consts_made"], 1)
            pool.iota(tile_no[:], [[1, LOADED]], base=0, channel_multiplier=0,
                      allow_small_or_imprecise_dtypes=True).then_inc(sem["consts_made"], 1)
            pool.wait_ge(sem["pad_copied"], 1)
            pool.affine_select(out=pad_b[:], in_=pad_f[:], compare_op=ALU.is_ge, fill=MASKED_L1, base=0,
                               pattern=[[0, B], [-1, P]], channel_multiplier=1).then_inc(sem["pad_made"], 1)
            make_keys(4)
            make_vals(4)
            pool.memset(empty_row[:, 0:D], 0.0).then_inc(sem["empty_made"], 1)
            pool.iota(empty_row[:, D:ROW].bitcast(I32), [[0, 1]], base=NO_TOKEN, channel_multiplier=0
                      ).then_inc(sem["empty_made"], 1)
            pool.iota(x_rows[:, :, D:ROW].bitcast(I32), [[P, B], [0, 1]], base=0, channel_multiplier=1
                      ).then_inc(sem["consts_made"], 1)
            pool.wait_ge(*pre_emptied(13))
            pool.tensor_scalar(vh[:], vh[:], tgate[:, 1:2], None, ALU.mult).then_inc(sem["vh_scaled"], 1)
            for b in range(5, B):
                make_keys(b)
                make_vals(b)
            pool.wait_ge(sem["consts_made"], 4)
            for b in range(B):
                pool.wait_ge(sem["var3_ready"], b + 1)
                pool.tensor_tensor(rstd[:, 2, b:b + 1], var_eps[:, b:b + 1], minus_half[:], ALU.pow
                                   ).then_inc(sem["rstd3_ready"], 1)
            pool.wait_ge(sem["slots_made"], 1)
            pool.wait_ge(sem["rows_filled"], 16)
            for b in range(B):
                pool.wait_ge(sem["rows_scaled"], b + 1)
                pool.indirect_dma_start(
                    out=sorted_rows, in_=x_rows[:, b, :], in_offset=None,
                    out_offset=bass.IndirectOffsetOnAxis(ap=slot_i[:, b:b + 1].bitcast(U32), axis=0)
                ).then_inc(sem["rows_sorted"], 16)
            pool.wait_ge(sem["tiles_made"], 1)
            pairs = pool.value_load(pairs_i[0:1, 0:1], min_val=MIN_PAIRS, max_val=TILES // 2)

            def scatter_rows(k, t):
                pool.wait_ge(sem["y_ready"], 2 * t + 2)
                pool.sem_inc(sem["scatter_begun"], 1)
                pool.indirect_dma_start(
                    out=token_rows.rearrange("b s d -> (b s) d"), in_=y_out[k], in_offset=None, bounds_check=B * S - 1,
                    oob_is_err=False,
                    out_offset=bass.IndirectOffsetOnAxis(ap=token_of[k][:, 0:1].bitcast(U32), axis=0)
                ).then_inc(y_scattered[k], 16)

            scatter_rows(0, 0)
            with pool.Fori(0, pairs) as i:
                scatter_rows(1, 2 * i + 1)
                scatter_rows(0, 2 * i + 2)

        @block.scalar
        def _(act):
            A = nc.scalar.activation
            steps = [0]

            def step(i):
                steps[0] += 1
                i.then_inc(sem["scalar_step"], 1)
                act.wait_ge(sem["scalar_step"], steps[0])

            def inv_std(n, rows, done):
                step(A(var_ln[:, rows], mv[:, n, rows, 1], ACT.Ln, bias=eps[:, 0:1]))
                A(rstd[:, n, rows], var_ln[:, rows], ACT.Exp, scale=-0.5).then_inc(sem[done], 1)

            act.dma_start(c[:], a["ctx_1024"].rearrange("b s d -> s b d")).then_inc(sem["c_loaded"], 16)
            act.wait_ge(sem["gates_loaded"], 32)
            A(tgate[:], gates[:], ACT.Tanh).then_inc(sem["tanh_made"], 1)
            nc.scalar.preload_act_table_set(LN_EXP_SET)

            dst = {("cT", 0): cT[:, 0:4, :], ("cT", 1): cT[:, 4:8, :], ("xn", 1): xnT[:, 4:8, :],
                   ("w", 1): w_t[:, 4:8, :], ("w", 3): w_t[:, 12:16, :]}
            for i, (what, j, e) in enumerate(PRE):
                if (what, j) == ("xn", 1):
                    act.wait_ge(sem["var_ready"], 1)
                    act.wait_ge(sem["eps_made"], 1)
                    inv_std(0, slice(0, B), "rstd_ready")
                if e == "s":
                    act.wait_ge(sem["pre_ready"], i + 1)
                    A(dst[what, j], in_bank(i % PB), ACT.Copy, scale=SCALE if what == "xn" else 1.0
                      ).then_inc(sem["pre_out_s"], 1)

            for s in range(STEPS):
                b = chain_row(s, 2 * UB)
                if b is not None:
                    act.wait_ge(sem["o_T"], b + 1)
                    A(oT[:], bank[7][:, 0:P], ACT.Copy).then_inc(sem["o_T_out"], 1)
                b = chain_row(s, 2 * UB + 2)
                if b is not None:
                    act.wait_ge(sem["xn2_T"], b + 1)
                    A(xnT[:, b, :], bank[7][:, 0:P], ACT.Copy).then_inc(sem["xn2_T_out"], 1)
                if s < UNITS:
                    act.wait_ge(sem["max_made"], s + 1)
                    if s >= 3:
                        act.wait_ge(sem["probs_T"], s - 2)
                    for h in range(HG):
                        i = A(probs[s % 3][:, h, :], bank[s % 3][:, h * P:(h + 1) * P], ACT.Exp,
                              bias=neg_max[:, s, h:h + 1])
                    i.then_inc(sem["probs_made"], 1)
                b = chain_row(s, 2 * UB - 2)
                if b is not None:
                    act.wait_ge(sem["heads_out"], UB * (b + 1))
                    if b >= 1:
                        act.wait_ge(sem["heads_back"], b)
                    A(o_headsT[:], in_bank(5 + b % 2), ACT.Copy).then_inc(sem["heads_T_out"], 1)
                b = chain_row(s, 2 * UB)
                if b is not None:
                    act.wait_ge(sem["var_ready"], b + 2)
                    inv_std(1, slice(b, b + 1), "rstd_ready")
                b = chain_row(s, 2 * UB + 2)
                if b is not None:
                    act.wait_ge(sem["gate_hidden"], b + 1)
                    A(relu_out[:], bank[7][:, P:2 * P], ACT.Relu, bias=b_g1[:, 0:1], accum_out=h_sum[:, b:b + 1]
                      ).then_inc(sem["gate_summed"], 1)
                    act.wait_ge(sem["gate_summed"], b + 1)
            act.wait_ge(sem["gate_out"], 1)
            A(gT[:], bank[2][0:E0, 0:B], ACT.Identity, scale=1.0 / S, bias=b_g2[:, 0:1]).then_inc(sem["g_made"], 1)

            act.wait_ge(sem["mix_inputs"], 3)
            for s in range(B + 3):
                if s < B:
                    act.wait_ge(sem["hidden"], s + 1)
                    if s >= 2:
                        act.wait_ge(sem["ffn_out"], s - 1)
                    for f in range(FC):
                        i = A(uT[s % 2][:, f, :], bank[s % 2][:, f * P:(f + 1) * P], ACT.Gelu_apprx_tanh,
                              bias=mb1[:, f, s:s + 1])
                    i.then_inc(sem["gelu_made"], 1)
                if s >= 3:
                    b = s - 3
                    act.wait_ge(sem["xn3_T"], b + 1)
                    A(xnT[:, b, :], bank[4 + b % 2][:, 0:P], ACT.Copy).then_inc(sem["xn3_T_out"], 1)
            nc.scalar.preload_act_table_set(LN_EXP_SET)

            for s in range(B + 4):
                if s < B:
                    act.wait_ge(sem["max1_made"], s // 4 + 1)
                    A(p1[:, s, :], bank[6 + s // 4][:, (s % 4) * P:(s % 4 + 1) * P], ACT.Exp,
                      bias=neg_max1[:, s:s + 1], accum_out=den1[:, s:s + 1]).then_inc(sem["probs1"], 1)
                if 2 <= s < B + 2:
                    b = s - 2
                    act.wait_ge(sem["var4_ready"], b + 1)
                    inv_std(3, slice(b, b + 1), "rstd4_ready")
                if s >= 4:
                    b = s - 4
                    act.wait_ge(sem["xn4_T"], b + 1)
                    A(xnT[:, b, :], bank[4 + b % 2][:, 0:P], ACT.Copy).then_inc(sem["xn4_T_out"], 1)
            act.wait_ge(sem["logit_max_made"], 1)
            A(score[:], logit_max[:], ACT.Exp, scale=-1.0).then_inc(sem["exp_made"], 1)
            for i in range(4):
                act.wait_ge(sem["shared_hidden"], 2 * i + 1)
                if i >= 2:
                    act.wait_ge(sem["shared_act"], i - 1)
                A(silu_sh[i % 2], bank[3 + 2 * (i % 2)][:], ACT.Silu).then_inc(sem["shared_silu"], 1)

            act.wait_ge(sem["tiles_made"], 1)
            pairs = act.value_load(pairs_i[0:1, 0:1], min_val=MIN_PAIRS, max_val=TILES // 2)

            def tile_T_out(k, t, wait=True):
                act.wait_ge(sem["tile_T"], t + 1)
                if wait:
                    act.wait_ge(sem["tile_hidden"], t - 1)
                A(xs_T[k % 2], bank[k % 2][:, 0:P], ACT.Copy).then_inc(sem["tile_T_out"], 1)
                A(tokens[:, bass.ds(t, 1)], xs_in[k % 2][:, D:ROW].bitcast(I32), ACT.Copy).then_inc(sem["tokens_taken"], 1)

            def tile_silu(k, t, wait=True):
                act.wait_ge(sem["tile_hidden"], t + 1)
                if wait:
                    act.wait_ge(sem["tile_act"], t - 1)
                A(silu_g[k % 2], bank[2 + k % 2][:, 0:F1], ACT.Silu).then_inc(sem["tile_silu"], 1)

            tile_T_out(0, 0, wait=False)
            tile_T_out(1, 1, wait=False)
            tile_silu(0, 0, wait=False)
            tile_T_out(2, 2)
            tile_silu(1, 1, wait=False)
            with act.Fori(0, pairs) as i:
                for k in (1, 2):
                    tile_silu(k + 1, 2 * i + (k + 1))
                    tile_T_out(k + 2, 2 * i + (k + 2))

        @block.vector
        def _(v):
            steps = [0]

            def step(i):
                steps[0] += 1
                i.then_inc(sem["vector_step"], 1)
                v.wait_ge(sem["vector_step"], steps[0])

            def row_stats(n, b):
                step(v.bn_stats(stats[:, b, :], x[:, b, :]))
                return v.bn_aggr(mv[:, n, b, :], stats[:, b, :])

            def normed(n, b, done):
                v.tensor_scalar(xn[:, b, :], x[:, b, :], mv[:, n, b, 0:1], rstd[:, n, b:b + 1],
                                ALU.subtract, ALU.mult).then_inc(sem[done], 1)

            v.wait_ge(sem["ident_made"], 1)
            v.tensor_reduce(head_of[:], ident[:, :].rearrange("p (h d) -> p h d", d=HD), X, ALU.add
                            ).then_inc(sem["heads_made"], 1)
            v.tensor_reduce(same_row[:], ident[:, :].rearrange("p (e r) -> p r e", r=RO), X, ALU.add
                            ).then_inc(sem["vector_step"], 1)
            step(v.tensor_copy(spread[:, :].rearrange("p (e r) -> p e r", r=RO),
                               ident[0:E0, 0:E0].unsqueeze(2).to_broadcast([E0, E0, RO])))
            steps[0] += 1
            v.wait_ge(sem["vector_step"], steps[0])
            v.wait_ge(sem["x_loaded"], 16)
            for b in range(B):
                i = v.bn_stats(stats[:, b, :], x[:, b, :])
            step(i)
            for b in range(B):
                i = v.bn_aggr(mv[:, 0, b, :], stats[:, b, :])
            i.then_inc(sem["var_ready"], 1)
            v.wait_ge(sem["mask_loaded"], 16)
            v.tensor_scalar(mask_b[:], mask_i, 0.0, MASKED_L0, ALU.is_equal, ALU.mult).then_inc(sem["mask_made"], 1)
            v.wait_ge(sem["rstd_ready"], 1)
            for b in range(B):
                normed(0, b, "xn_written")

            dst = {("xn", 0): xnT[:, 0:4, :], ("w", 0): w_t[:, 0:4, :], ("w", 2): w_t[:, 8:12, :],
                   ("w", 4): w_t[:, 16:19, :], ("k", 0): kT[:, 0:4, :], ("k", 1): kT[:, 4:8, :],
                   ("v", 0): vh[:, 0:4, :], ("v", 1): vh[:, 4:8, :]}
            for i, (what, j, e) in enumerate(PRE):
                if e != "v":
                    continue
                v.wait_ge(sem["pre_ready"], i + 1)
                src = in_bank(i % PB)
                if what == "xn":
                    n = v.tensor_scalar(dst[what, j], src, SCALE, None, ALU.mult)
                elif what == "k":
                    v.wait_ge(sem["small_loaded"], 11 * 16)
                    n = v.tensor_scalar(dst[what, j], src, b_k[:, 0:1], None, ALU.add)
                elif what == "v":
                    n = v.tensor_tensor(dst[what, j], src, b_v[:, :].unsqueeze(1).to_broadcast([P, 4, D]), ALU.add)
                elif what == "small":
                    step(v.tensor_copy(gate2T[:], bank[i % PB][:, 0:E0]))
                    n = v.tensor_copy(routerT[:], bank[i % PB][:, E0:E0 + E1])
                else:
                    n = v.tensor_copy(dst[what, j], in_bank(i % PB, 3 if j == 4 else 4))
                n.then_inc(sem["pre_out_v"], 1)
            v.tensor_scalar(pad_f[:], pad_i, 0.0, MASKED_L1, ALU.is_equal, ALU.mult).then_inc(sem["pad_copied"], 1)

            for s in range(STEPS):
                if s < UNITS:
                    v.wait_ge(sem["scores"], s + 1)
                    v.tensor_reduce(neg_max[:, s, :], in_bank(s % 3), X, ALU.max, negate=True).then_inc(sem["max_made"], 1)
                if 2 <= s < UNITS + 2:
                    u = s - 2
                    v.wait_ge(sem["probs_T"], u + 1)
                    if u >= 2:
                        v.wait_ge(sem["heads_out"], u - 1)
                    v.tensor_copy(probsT[u % 2][:], in_bank(3 + u % 2)).then_inc(sem["probs_T_out"], 1)
                b = chain_row(s, 2 * UB - 1)
                if b is not None:
                    heads = bank[5 + b % 2][:, :].rearrange("p (h d) -> p h d", d=32)
                    v.wait_ge(sem["heads_back"], b + 1)
                    step(v.reciprocal(rden[:, b, :], heads[:, :, HD]))
                    if b >= 2:
                        v.wait_ge(sem["o_T"], b - 1)
                    v.tensor_tensor(o_rows[b % 2][:], heads[:, :, 0:HD],
                                    rden[:, b, :].unsqueeze(2).to_broadcast([P, HEADS, HD]), ALU.mult
                                    ).then_inc(sem["o_normed"], 1)
                b = chain_row(s, 2 * UB)
                if b is not None:
                    v.wait_ge(sem["projected"], b + 1)
                    v.wait_ge(sem["x_plus_bout"], 1)
                    v.tensor_tensor(x[:, b, :], bank[7][:, P:2 * P], x[:, b, :], ALU.add).then_inc(sem["x1_made"], 1)
                    v.wait_ge(sem["x1_made"], b + 1)
                    row_stats(1, b).then_inc(sem["var_ready"], 1)
                b = chain_row(s, 2 * UB + 1)
                if b is not None:
                    v.wait_ge(sem["rstd_ready"], b + 2)
                    normed(1, b, "xn2_made")

            v.wait_ge(sem["g_made"], 1)
            v.wait_ge(sem["consts_made"], 3)
            v.tensor_copy(g_rows[0:E0, :, :], gT[:, :].unsqueeze(2).to_broadcast([E0, B, P])).then_inc(sem["mix_inputs"], 1)
            v.wait_ge(sem["g_spread"], 1)
            step(v.tensor_copy(g_col[:], bank[2][:, 16:16 + B]))
            v.tensor_tensor(g_mix[:], g_col[:, :].unsqueeze(2).to_broadcast([P, B, RO]),
                            same_row[:, :].unsqueeze(1).to_broadcast([P, B, RO]), ALU.mult).then_inc(sem["mix_inputs"], 1)
            v.tensor_tensor(mb1[:], bank[2][:, 32:32 + FC * B].rearrange("p (c b) -> p c b", b=B),
                            b_1[:, :].unsqueeze(2).to_broadcast([P, FC, B]), ALU.add).then_inc(sem["mix_inputs"], 1)
            w1_rows = w_t[:, W1:W1 + FC, :].rearrange("p c (q r) -> p (c q) r", r=RO)
            for m in range(16):
                v.wait_ge(sem["mixed"], m + 1)
                src = bank[3 + m % 4][:, :].rearrange("p (j b r) -> p j b r", b=B, r=RO)
                if m < 8:
                    to = mW1T[:, :, 4 * m:4 * m + 4, :]
                    base = w1_rows[:, 4 * m:4 * m + 4, :]
                else:
                    f, h = divmod(m - 8, 2)
                    to = mW2T[:, :, f, 4 * h:4 * h + 4, :]
                    base = w_t[:, W2 + f, :].rearrange("p (q r) -> p q r", r=RO)[:, 4 * h:4 * h + 4, :]
                v.tensor_tensor(to.rearrange("p b j r -> p j b r"), src, base.unsqueeze(2).to_broadcast([P, 4, B, RO]),
                                ALU.add).then_inc(sem["mixed_out"], 1)

            for s in range(1, B + 6):
                if s <= B:
                    b = s - 1
                    v.wait_ge(sem["ffn_out"], b + 1)
                    v.scalar_tensor_tensor(out=x[:, b, :], in0=bank[2 + b % 2][:, 0:P], scalar=tgate[:, 2:3],
                                           in1=x[:, b, :], op0=ALU.mult, op1=ALU.add).then_inc(sem["x2_made"], 1)
                    v.wait_ge(sem["x2_made"], b + 1)
                    step(row_stats(2, b))
                    v.tensor_scalar(var_eps[:, b:b + 1], mv[:, 2, b, 1:2], EPS, None, ALU.add
                                    ).then_inc(sem["var3_ready"], 1)
                if 2 <= s <= B + 1:
                    b = s - 2
                    v.wait_ge(sem["rstd3_ready"], b + 1)
                    normed(2, b, "xn3_made")
                if 4 <= s <= B + 3:
                    b = s - 4
                    v.wait_ge(sem["q_ready"], b + 1)
                    if b >= 2:
                        v.wait_ge(sem["scores1"], b - 1)
                    v.tensor_scalar(q1T[b % 2][:], bank[4 + b % 2][:, P:2 * P], b_q[:, 0:1], SCALE, ALU.add, ALU.mult
                                    ).then_inc(sem["q_out"], 1)
                if s in (B // 2 + 5, B + 5):
                    h = 0 if s < B + 5 else 1
                    v.wait_ge(sem["scores1"], 4 * h + 4)
                    v.tensor_reduce(neg_max1[:, 4 * h:4 * h + 4], in_bank(6 + h), X, ALU.max, negate=True
                                    ).then_inc(sem["max1_made"], 1)

            for s in range(1, B + 4):
                if s <= B:
                    b = s - 1
                    v.wait_ge(sem["probs1_T"], b + 1)
                    if b >= 2:
                        v.wait_ge(sem["attn1"], b - 1)
                    v.tensor_copy(p1T[b % 2][:], bank[b % 2][:, 0:P]).then_inc(sem["probs1_T_out"], 1)
                    step(v.reciprocal(rden1[:, b:b + 1], den1[:, b:b + 1]))
                if 2 <= s <= B + 1:
                    b = s - 2
                    v.wait_ge(sem["attn1"], b + 1)
                    v.scalar_tensor_tensor(out=x[:, b, :], in0=bank[2 + b % 2][:, 0:P], scalar=rden1[:, b:b + 1],
                                           in1=x[:, b, :], op0=ALU.mult, op1=ALU.add).then_inc(sem["x3_made"], 1)
                    v.wait_ge(sem["x3_made"], b + 1)
                    row_stats(3, b).then_inc(sem["var4_ready"], 1)
                if s >= 3 and s - 3 < B:
                    b = s - 3
                    v.wait_ge(sem["rstd4_ready"], b + 1)
                    normed(3, b, "xn4_made")

            v.wait_ge(sem["logits"], 1)
            v.wait_ge(sem["consts_made"], 8)
            logits = bank[2][:, 0:B * E1].rearrange("p (b e) -> p b e", e=E1)
            experts = expert_no[:, :].unsqueeze(1).to_broadcast([P, B, E1])
            v.tensor_reduce(logit_max[:], logits, X, ALU.max).then_inc(sem["logit_max_made"], 1)
            v.wait_ge(sem["logit_max_made"], 1)
            step(v.tensor_tensor(tmp_be[:], logits, logit_max[:, :].unsqueeze(2).to_broadcast([P, B, E1]), ALU.is_equal))
            step(v.scalar_tensor_tensor(out=tmp_be[:], in0=tmp_be[:], scalar=-float(E1), in1=experts, op0=ALU.mult, op1=ALU.add))
            step(v.tensor_reduce(choice[:], tmp_be[:], X, ALU.min))
            step(v.tensor_scalar(choice[:], choice[:], float(E1), None, ALU.add))
            choices = choice[:, :].unsqueeze(2).to_broadcast([P, B, E1])
            v.tensor_tensor(one_hot_b[:], experts, choices, ALU.is_equal).then_inc(sem["one_hot_made"], 1)
            v.tensor_tensor(one_hot[:], experts, choices, ALU.is_equal).then_inc(sem["vector_step"], 1)
            steps[0] += 1
            v.wait_ge(sem["exp_made"], 1)
            step(v.tensor_scalar(score[:], score[:], 1.0, None, ALU.add))
            step(v.reciprocal(score[:], score[:]))
            for b in range(B // 2):
                v.tensor_scalar(x_rows[:, b, 0:D], xn[:, b, :], score[:, b:b + 1], None, ALU.mult
                                ).then_inc(sem["rows_scaled"], 1)
            v.wait_ge(sem["ranks"], 1)
            step(v.tensor_scalar(tiles_i[:], bank[2][:, 256:256 + E1], float(P - 1), None, ALU.add))
            step(v.tensor_scalar(tiles_i[:], tiles_i[:], 7, None, ALU.logical_shift_right))
            step(v.tensor_copy(tiles_f[:], tiles_i[:]))
            step(v.tensor_tensor(tmp_ee[:], lower[:], tiles_f[:, :].unsqueeze(1).to_broadcast([P, E1, E1]), ALU.mult))
            step(v.tensor_reduce(first[:], tmp_ee[:], X, ALU.add))
            ranks = bank[2][:, 128:128 + B * E1].rearrange("p (b e) -> p b e", e=E1)
            step(v.scalar_tensor_tensor(out=tmp_be[:], in0=first[:, :].unsqueeze(1).to_broadcast([P, B, E1]),
                                        scalar=float(P), in1=ranks, op0=ALU.mult, op1=ALU.add))
            step(v.tensor_tensor(tmp_be[:], tmp_be[:], one_hot[:], ALU.mult))
            step(v.tensor_reduce(slot_f[:], tmp_be[:], X, ALU.add))
            v.tensor_copy(slot_i[:], slot_f[:]).then_inc(sem["slots_made"], 1)
            for b in range(B // 2, B):
                v.tensor_scalar(x_rows[:, b, 0:D], xn[:, b, :], score[:, b:b + 1], None, ALU.mult
                                ).then_inc(sem["rows_scaled"], 1)
            step(v.tensor_tensor(end_tile[:], first[:], tiles_f[:], ALU.add))
            step(v.tensor_tensor(tmp_te[:], tile_no[:, :].unsqueeze(2).to_broadcast([P, LOADED, E1]),
                                 end_tile[:, :].unsqueeze(1).to_broadcast([P, LOADED, E1]), ALU.is_ge))
            step(v.tensor_reduce(tile_expert_f[:], tmp_te[:], X, ALU.add))
            step(v.tensor_scalar(tile_expert[:], tile_expert_f[:], float(E1 - 1), None, ALU.min))
            step(v.tensor_scalar(pairs_i[:], end_tile[:, E1 - 1:E1], 0.0, None, ALU.add))
            v.tensor_scalar(pairs_i[:], pairs_i[:], 1, None, ALU.logical_shift_right).then_inc(sem["tiles_made"], 1)

            for i in range(4):
                f, h = divmod(i, 2)
                v.wait_ge(sem["shared_hidden"], 2 * i + 2)
                v.wait_ge(sem["shared_silu"], i + 1)
                v.tensor_tensor(sharedT[:, f, 4 * h:4 * h + 4, :].rearrange("p b t -> p (b t)"),
                                bank[4 + 2 * (i % 2)][:], silu_sh[i % 2], ALU.mult).then_inc(sem["shared_act"], 1)
            for h in range(2):
                v.wait_ge(sem["shared_out"], h + 1)
                xh = x[:, 4 * h:4 * h + 4, :].rearrange("p b t -> p (b t)")
                v.scalar_tensor_tensor(out=xh, in0=bank[7 * (1 - h)][:], scalar=tgate[:, 3:4], in1=xh,
                                       op0=ALU.mult, op1=ALU.add).then_inc(sem["acc_made"], 1)

            v.wait_ge(sem["tiles_made"], 1)
            pairs = v.value_load(pairs_i[0:1, 0:1], min_val=MIN_PAIRS, max_val=TILES // 2)

            def tile_act(k, t, wait=True):
                v.wait_ge(sem["tile_silu"], t + 1)
                if wait:
                    v.wait_ge(sem["act_T_ready"], t - 1)
                v.tensor_tensor(act_r[k % 2], bank[2 + k % 2][:, F1:2 * F1], silu_g[k % 2], ALU.mult
                                ).then_inc(sem["tile_act"], 1)

            def act_T_out(k, t, wait=True):
                v.wait_ge(sem["act_T_ready"], t + 1)
                if wait:
                    v.wait_ge(sem["tile_y"], t - 1)
                v.tensor_copy(act_T[k % 2], in_bank(4 + k % 2, C1)).then_inc(sem["act_T_out"], 1)

            def y_scaled(k, t, scattered):
                if scattered is not None:
                    v.wait_ge(y_scattered[k % 2], scattered)
                v.tensor_copy(token_of[k % 2][:], tokens[:, bass.ds(t, 1)]).then_inc(sem["y_ready"], 1)
                v.wait_ge(sem["tile_y"], t + 1)
                v.tensor_scalar(y_out[k % 2], bank[6 + k % 2][:, 0:P], tgate[:, 3:4], None, ALU.mult
                                ).then_inc(sem["y_ready"], 1)

            tile_act(0, 0, wait=False)
            act_T_out(0, 0, wait=False)
            tile_act(1, 1, wait=False)

            def pair(i, first):
                for k in (1, 2):
                    t = 2 * i + k
                    tile_act(k + 1, t + 1)
                    y_scaled(k - 1, t - 1, None if first else 16 * i)
                    act_T_out(k, t, wait=not (first and k == 1))

            pair(0, True)
            with v.Fori(1, pairs) as i:
                pair(i, False)
            y_scaled(0, 2 * pairs, 16 * pairs)
            for h in range(2):
                v.wait_ge(sem[f"routed_loaded{h}"], 16)
                half = routed_in[:, 4 * h:4 * h + 4, :]
                v.tensor_tensor(half, half, x[:, 4 * h:4 * h + 4, :], ALU.add).then_inc(sem["out_made"], 1)

        @block.tensor
        def _(pe):
            mm = pe.matmul

            def transpose(to, rows):
                n = rows.shape[0]
                return pe.transpose(to, rows, ident[0:n, 0:n])

            def col(i, n=1):
                return slice(i * P, (i + n) * P)

            pe.wait_ge(sem["ident_made"], 1)
            for i, (what, j, e) in enumerate(PRE):
                if i >= PB:
                    pe.wait_ge(*pre_emptied(i - PB))
                to = bank[i % PB]
                if what == "cT":
                    pe.wait_ge(sem["c_loaded"], 16)
                    for m in range(4):
                        n = transpose(to[:, col(m)], c[:, 4 * j + m, :])
                elif what == "xn":
                    pe.wait_ge(sem["xn_written"], 4 * j + 4)
                    for m in range(4):
                        n = transpose(to[:, col(m)], xn[:, 4 * j + m, :])
                elif what == "w":
                    if j == 0:
                        pe.wait_ge(sem["w_loaded"], 12 * 16)
                    lo, hi = W_GROUPS[j]
                    for m in range(hi - lo):
                        n = transpose(to[:, col(m)], w_raw[:, lo + m, :])
                elif what == "small":
                    transpose(to[:, 0:E0], w_small[0:E0, 0, :])
                    n = transpose(to[:, E0:E0 + E1], w_small[0:E1, 1, :])
                elif what == "k":
                    pe.wait_ge(*pre_emptied(PRE.index(("w", 0, "v"))))
                    pe.wait_ge(*pre_emptied(1))
                    n = mm(to[:], w_t[:, WK, :], cT[:, 4 * j:4 * j + 4, :], start=True, stop=True)
                else:
                    for m in range(4):
                        n = mm(to[:, col(m)], cT[:, 4 * j + m, :], w_t[:, WV, :], start=True, stop=True)
                n.then_inc(sem["pre_ready"], 1)
            pe.wait_ge(sem["pre_out_v"], sum(p[2] == "v" for p in PRE))
            pe.wait_ge(sem["pre_out_s"], sum(p[2] == "s" for p in PRE))
            pe.wait_ge(sem["mask_made"], 1)
            pe.wait_ge(sem["consts_bf16"], 1)

            for s in range(STEPS):
                if s < UNITS:
                    b, g = divmod(s, UB)
                    pe.wait_ge(sem["keys_made"], b + 1)
                    if s >= 3:
                        pe.wait_ge(sem["probs_made"], s - 2)
                    mm(bank[s % 3][:], xnT[:, b, :], keys[b % 2][:, HG * g:HG * g + HG, :], start=True, stop=False)
                    mm(bank[s % 3][:], ident_b[:], mask_b[:, b:b + 1, :].to_broadcast([P, HG, P]), start=False,
                       stop=True).then_inc(sem["scores"], 1)
                b = chain_row(s, 2 * UB)
                if b is not None:
                    pe.wait_ge(sem["o_normed"], b + 1)
                    if b >= 1:
                        pe.wait_ge(sem["gate_summed"], b)
                    transpose(bank[7][:, 0:P], o_rows[b % 2][:, :, :].rearrange("p h d -> p (h d)")
                              ).then_inc(sem["o_T"], 1)
                b = chain_row(s, 2 * UB + 2)
                if b is not None:
                    pe.wait_ge(sem["xn2_made"], b + 1)
                    transpose(bank[7][:, 0:P], xn[:, b, :]).then_inc(sem["xn2_T"], 1)
                if 2 <= s < UNITS + 2:
                    u = s - 2
                    pe.wait_ge(sem["probs_made"], u + 1)
                    if u >= 2:
                        pe.wait_ge(sem["probs_T_out"], u - 1)
                    for h in range(HG):
                        n = transpose(bank[3 + u % 2][:, col(h)], probs[u % 3][:, h, :])
                    n.then_inc(sem["probs_T"], 1)
                b = chain_row(s, 2 * UB - 1)
                if b is not None:
                    pe.wait_ge(sem["heads_T_out"], b + 1)
                    for g in range(UB):
                        n = transpose(bank[5 + b % 2][:, col(g)], o_headsT[:, g, :])
                    n.then_inc(sem["heads_back"], 1)
                if 3 <= s < UNITS + 3:
                    u = s - 3
                    b, g = divmod(u, UB)
                    pe.wait_ge(sem["probs_T_out"], u + 1)
                    pe.wait_ge(sem["vals_made"], b + 1)
                    if g == 0 and b >= 2:
                        pe.wait_ge(sem["o_normed"], b - 1)
                    for h in range(HG):
                        n = mm(bank[5 + b % 2][32 * h:32 * h + 32, col(g)], vals[b % 2][:, HG * g + h, :],
                               probsT[u % 2][:, h, :], start=True, stop=True)
                    n.then_inc(sem["heads_out"], 1)
                b = chain_row(s, 2 * UB)
                if b is not None:
                    pe.wait_ge(sem["o_T_out"], b + 1)
                    pe.wait_ge(sem["wout_scaled"], 1)
                    mm(bank[7][:, col(1)], oT[:], w_t[:, WO, :], start=True, stop=True).then_inc(sem["projected"], 1)
                b = chain_row(s, 2 * UB + 2)
                if b is not None:
                    pe.wait_ge(sem["xn2_T_out"], b + 1)
                    mm(bank[7][:, col(1)], w_t[:, GW1, :], xnT[:, b, :], start=True, stop=True).then_inc(sem["gate_hidden"], 1)

            pe.wait_ge(sem["gate_summed"], B)
            mm(bank[2][0:E0, 0:B], gate2T[:], h_sum[:], start=True, stop=True).then_inc(sem["gate_out"], 1)
            pe.wait_ge(sem["g_made"], 1)
            mm(bank[2][:, 16:16 + B], spread[:], gT[:], start=True, stop=True)
            for f in range(FC):
                n = mm(bank[2][:, 32 + f * B:32 + (f + 1) * B], tb1[:, col(f)], gT[:], start=True, stop=True)
            n.then_inc(sem["g_spread"], 1)
            pe.wait_ge(sem["mix_inputs"], 3)
            pe.wait_ge(sem["tw1_loaded"], 16 * E0)
            pe.wait_ge(sem["tw2_loaded"], 16 * E0)
            for m in range(16):
                if m >= 4:
                    pe.wait_ge(sem["mixed_out"], m - 3)
                for j in range(4):
                    f, h = divmod(m - 8, 2)
                    w = tw1[:, 4 * m + j, :] if m < 8 else tw2[:, 4 * h + j, col(f)]
                    n = mm(bank[3 + m % 4][:, col(j)], w, g_mix[:], start=True, stop=True)
                n.then_inc(sem["mixed"], 1)
            pe.wait_ge(sem["mixed_out"], 16)

            for s in range(B + 5):
                if s < B:
                    if s >= 2:
                        pe.wait_ge(sem["gelu_made"], s - 1)
                    for f in range(FC):
                        n = mm(bank[s % 2][:, col(f)], mW1T[:, s, :, :].rearrange("p q r -> p (q r)")[:, col(f)],
                               xnT[:, s, :], start=True, stop=True)
                    n.then_inc(sem["hidden"], 1)
                if 3 <= s < B + 3:
                    b = s - 3
                    pe.wait_ge(sem["xn3_made"], b + 1)
                    if b >= 2:
                        pe.wait_ge(sem["q_out"], b - 1)
                    transpose(bank[4 + b % 2][:, 0:P], xn[:, b, :]).then_inc(sem["xn3_T"], 1)
                if 4 <= s < B + 4:
                    b = s - 4
                    pe.wait_ge(sem["xn3_T_out"], b + 1)
                    mm(bank[4 + b % 2][:, col(1)], w_t[:, WQ, :], xnT[:, b, :], start=True, stop=True).then_inc(sem["q_ready"], 1)
                if 5 <= s:
                    b = s - 5
                    pe.wait_ge(sem["q_out"], b + 1)
                    pe.wait_ge(sem["pad_made"], 1)
                    o = bank[6 + b // 4][:, col(b % 4)]
                    mm(o, q1T[b % 2][:], kT[:, b, :], start=True, stop=False)
                    mm(o, ident_b[:], pad_b[:, b, :], start=False, stop=True).then_inc(sem["scores1"], 1)
                if 1 <= s < B + 1:
                    b = s - 1
                    pe.wait_ge(sem["gelu_made"], b + 1)
                    if b >= 2:
                        pe.wait_ge(sem["x2_made"], b - 1)
                    o = bank[2 + b % 2][:, 0:P]
                    for f in range(FC):
                        mm(o, uT[b % 2][:, f, :], mW2T[:, b, f, :, :].rearrange("p q r -> p (q r)"), start=(f == 0), stop=False)
                    mm(o, g_rows[:, b, :], tb2[:], start=False, stop=True).then_inc(sem["ffn_out"], 1)

            for s in range(B + 4):
                if s < B:
                    pe.wait_ge(sem["probs1"], s + 1)
                    if s >= 2:
                        pe.wait_ge(sem["probs1_T_out"], s - 1)
                    transpose(bank[s % 2][:, 0:P], p1[:, s, :]).then_inc(sem["probs1_T"], 1)
                if 1 <= s < B + 1:
                    b = s - 1
                    pe.wait_ge(sem["probs1_T_out"], b + 1)
                    pe.wait_ge(sem["vh_scaled"], 1)
                    pe.wait_ge(sem["x2_made"], B)
                    if b >= 2:
                        pe.wait_ge(sem["x3_made"], b - 1)
                    mm(bank[2 + b % 2][:, 0:P], p1T[b % 2][:], vh[:, b, :], start=True, stop=True).then_inc(sem["attn1"], 1)
                if 4 <= s:
                    b = s - 4
                    pe.wait_ge(sem["xn4_made"], b + 1)
                    if b >= 2:
                        pe.wait_ge(sem["xn4_T_out"], b - 1)
                    transpose(bank[4 + b % 2][:, 0:P], xn[:, b, :]).then_inc(sem["xn4_T"], 1)
            pe.wait_ge(sem["xn4_T_out"], B)
            for b in range(B):
                n = mm(bank[2][:, b * E1:(b + 1) * E1], xnT[:, b, :], routerT[:], start=True, stop=True)
            n.then_inc(sem["logits"], 1)

            def shared(i):
                f, h = divmod(i, 2)
                if i >= 2:
                    pe.wait_ge(sem["shared_act"], i - 1)
                for w, at in ((WG, 3), (WU, 4)):
                    mm(bank[at + 2 * (i % 2)][:], w_t[:, w + f, :], xnT[:, 4 * h:4 * h + 4, :], start=True, stop=True
                       ).then_inc(sem["shared_hidden"], 1)

            shared(0)
            shared(1)
            pe.wait_ge(sem["one_hot_made"], 1)
            pe.wait_ge(sem["consts_bf16"], 3)
            mm(bank[2][:, P:P + B * E1], before[:], one_hot_b[:], start=True, stop=False, skip_group_check=True)
            for b in range(B - 1):
                mm(bank[2][:, P + (b + 1) * E1:P + B * E1], ones_b[:],
                   one_hot_b[:, b:b + 1, :].to_broadcast([P, B - 1 - b, E1]), start=False, stop=(b == B - 2),
                   skip_group_check=True)
            for b in range(B):
                n = mm(bank[2][:, 256:256 + E1], ones_b[:], one_hot_b[:, b, :], start=False, stop=(b == B - 1),
                       skip_group_check=True)
            n.then_inc(sem["ranks"], 1)
            shared(2)
            shared(3)
            pe.wait_ge(sem["shared_act"], 4)
            for b in range(B):
                for f in range(C1):
                    n = mm(bank[7 * (1 - b // 4)][:, col(b % 4)], sharedT[:, f, b, :], w_t[:, WD + f, :],
                           start=(f == 0), stop=(f == C1 - 1))
                if b % 4 == 3:
                    n.then_inc(sem["shared_out"], 1)

            pe.wait_ge(sem["experts_loaded"], 32)
            pe.wait_ge(sem["acc_made"], 2)
            pe.wait_ge(sem["tiles_made"], 1)
            pairs = pe.value_load(pairs_i[0:1, 0:1], min_val=MIN_PAIRS, max_val=TILES // 2)

            def tile_transpose(k, t, loads):
                pe.wait_ge(tile_loaded[k % 2], loads)
                if k >= 2:
                    pe.wait_ge(sem["tile_T_out"], t - 1)
                transpose(bank[k % 2][:, 0:P], xs_in[k % 2][:, 0:D]).then_inc(sem["tile_T"], 1)

            def tile_hidden(k, t, wait=True):
                e = pe.value_load(tile_expert[0:1, t:t + 1] if isinstance(t, int) else tile_expert[0:1, bass.ds(t, 1)],
                                  min_val=0, max_val=E1 - 1)
                pe.wait_ge(sem["tile_T_out"], t + 1)
                if wait:
                    pe.wait_ge(sem["tile_act"], t - 1)
                mm(bank[2 + k % 2][:], xs_T[k % 2], gate_up[:, bass.ds(e, 1), :].rearrange("p a f -> p (a f)"),
                   start=True, stop=True).then_inc(sem["tile_hidden"], 1)

            def act_transpose(k, t, wait=True):
                pe.wait_ge(sem["tile_act"], t + 1)
                if wait:
                    pe.wait_ge(sem["act_T_out"], t - 1)
                for f in range(C1):
                    n = transpose(bank[4 + k % 2][:, col(f)], act_r[k % 2][:, col(f)])
                n.then_inc(sem["act_T_ready"], 1)

            def tile_down(k, t, wait=True):
                e = pe.value_load(tile_expert[0:1, bass.ds(t, 1)], min_val=0, max_val=E1 - 1)
                pe.wait_ge(sem["act_T_out"], t + 1)
                if wait:
                    pe.wait_ge(sem["y_ready"], 2 * t)
                for f in range(C1):
                    n = mm(bank[6 + k % 2][:, 0:P], act_T[k % 2][:, f, :],
                           down[:, bass.ds(e, 1), f, :].rearrange("p a h -> p (a h)"), start=(f == 0), stop=(f == C1 - 1))
                n.then_inc(sem["tile_y"], 1)

            tile_transpose(0, 0, 16)
            tile_transpose(1, 1, 16)
            tile_hidden(0, 0, wait=False)
            tile_transpose(2, 2, 32)
            tile_hidden(1, 1, wait=False)
            act_transpose(0, 0, wait=False)

            def pair(i, first):
                for k in (1, 2):
                    t = 2 * i + k
                    tile_hidden(k + 1, t + 1)
                    tile_down(k - 1, t - 1, wait=not (first and k == 1))
                    act_transpose(k, t, wait=not (first and k == 1))
                    tile_transpose(k + 2, t + 2, 16 * i + 32 + 16 * (k - 1))

            pair(0, True)
            with pe.Fori(1, pairs) as i:
                pair(i, False)
            tile_down(0, 2 * pairs)


_INS = ['x', 'ctx_1024', 'mask_Bx1xSxS2_ik1', 'mask_BxS2_if1', 'g_xattn', 'g_ffn', 'L0_xattn_w_out', 'L0_xattn_b_out',
        'L0_ffn_gate_w1', 'L0_ffn_gate_b1', 'L0_ffn_gate_w2', 'L0_ffn_gate_b2', 'L0_ffn_W1', 'L0_ffn_b1', 'L0_ffn_W2',
        'L0_ffn_b2', 'L0_ffn_TW1', 'L0_ffn_Tb1', 'L0_ffn_TW2', 'L0_ffn_Tb2', 'L1_xattn_Wq_w', 'L1_xattn_Wq_b',
        'L1_xattn_Wk_w', 'L1_xattn_Wk_b', 'L1_xattn_Wv_w', 'L1_xattn_Wv_b', 'L1_ffn_w_router', 'L1_ffn_gate_up_proj',
        'L1_ffn_down_proj', 'L1_ffn_w_gate', 'L1_ffn_w_up', 'L1_ffn_w_down']


def kernel(**inputs):
    import numpy as _np
    import concourse.bacc as _bacc
    from concourse import mybir as _mybir
    from concourse.bass_utils import run_bass_kernel_spmd as _run

    nc = _bacc.Bacc("TRN2", target_bir_lowering=False, num_devices=1)
    arrays, args = {}, {}
    for name in _INS:
        arr = _np.ascontiguousarray(inputs[name])
        arrays[f"in_{name}"] = arr
        args[name] = nc.dram_tensor(f"in_{name}", arr.shape, _mybir.dt.from_np(arr.dtype), kind="ExternalInput").ap()
    out = nc.dram_tensor("out_x", inputs["x"].shape, _mybir.dt.float32, kind="ExternalOutput").ap()
    flamingo_gated_blocks(nc, args, out)
    r = _run(nc, [arrays], core_ids=[0])
    return r.results[0]["out_x"]
```

```python
from contextlib import ExitStack

import concourse.bass as bass
from concourse import mybir

ALU = mybir.AluOpType
ACT = mybir.ActivationFunctionType
F32 = mybir.dt.float32
BF16 = mybir.dt.bfloat16
I32 = mybir.dt.int32
U32 = mybir.dt.uint32
X = mybir.AxisListType.X

P = 128
MASKED_L0 = -1.0e22
MASKED_L1 = -1.0e30
EPS = 1e-5
LN_EXP_SET = "natural_log_exp_and_others"
NO_TOKEN = 1 << 20


def flamingo_gated_blocks(nc, a, out):
    B, S, D = a["x"].shape
    HEADS = 16
    HD = D // HEADS
    E0, F0, _ = a["L0_ffn_TW1"].shape
    FC = F0 // P
    RO = P // E0
    E1, _, F1X2 = a["L1_ffn_gate_up_proj"].shape
    F1 = F1X2 // 2
    C1 = F1 // P
    assert S == P and D == P and B == 8 and HD * HEADS == D
    SCALE = float(D) ** -0.5
    HG = 4
    UB = HEADS // HG
    UNITS = UB * B
    TILES = B * S // P + E1 - 1
    MIN_PAIRS = B * S // P // 2
    LOADED = TILES + 1
    ROW = D + 1

    ctx = ExitStack()
    with ctx:
        def sb(name, shape, dt=F32):
            return ctx.enter_context(nc.sbuf_tensor(name, shape, dt))

        bank = [ctx.enter_context(nc.psum_tensor(f"bank{i}", [P, 512], F32)) for i in range(8)]
        sorted_acc = nc.dram_tensor("sorted_acc", (LOADED * P, D), F32, kind="Internal").ap()
        sorted_rows = nc.dram_tensor("sorted_rows", (LOADED * P, ROW), F32, kind="Internal").ap()

        x = sb("x", [P, B, D])
        c = sb("c", [P, B, D])
        early = sb("early", [P, 35, P])
        mask_i = early[:, 0:8, :].bitcast(I32)
        pad_i = early[:, 8:16, :].bitcast(I32)
        w_raw = early[:, 16:35, :]
        mW2T = early[:, 0:32, :].rearrange("p (b c) (q r) -> p b c q r", b=B, r=RO)
        w_t = sb("w_t", [P, 19, P])
        WO, GW1, WK, WV, W1, W2, WQ, WG, WU, WD = 0, 1, 2, 3, 4, 8, 12, 13, 15, 17
        w_small = sb("w_small", [P, 2, P])
        gate2T = sb("gate2T", [P, E0])
        routerT = sb("routerT", [P, E1])
        b_out = sb("b_out", [P, D])
        b_v = sb("b_v", [P, D])
        gates = sb("gates", [P, 4])
        tgate = sb("tgate", [P, 4])
        b_g1 = sb("b_g1", [P, 1])
        b_q = sb("b_q", [P, 1])
        b_k = sb("b_k", [P, 1])
        b_1 = sb("b_1", [P, FC])
        b_g2 = sb("b_g2", [E0, 1])
        tb1 = sb("tb1", [E0, F0])
        tb2 = sb("tb2", [E0 + 1, D])
        tw1 = sb("tw1", [P, F0 // RO, D])
        tw2 = sb("tw2", [P, D // RO, F0])
        gate_up = sb("gate_up", [P, E1, 2 * F1])
        down = sb("down", [P, E1, C1, D])

        ident = sb("ident", [P, P])
        ident_b = sb("ident_b", [P, P], BF16)
        before = sb("before", [P, P], BF16)
        ones_b = sb("ones_b", [P, P], BF16)
        head_of = sb("head_of", [P, HEADS])
        same_row = sb("same_row", [P, RO])
        spread = sb("spread", [E0, P])
        eps = sb("eps", [P, 1])
        empty_row = sb("empty_row", [P, ROW])
        expert_no = sb("expert_no", [P, E1])
        expert_low = sb("expert_low", [P, E1])
        tile_no = sb("tile_no", [P, LOADED])
        lower = sb("lower", [P, E1, E1])

        mask_b = sb("mask_b", [P, B, P], BF16)
        pad_f = sb("pad_f", [P, B, P], BF16)
        pad_b = sb("pad_b", [P, B, P], BF16)
        cT = sb("cT", [P, B, P])
        kT = sb("kT", [P, B, P])
        vh = sb("vh", [P, B, D])
        xn = sb("xn", [P, B, D])
        xnT = sb("xnT", [P, B, P])
        keys2 = sb("keys2", [P, 2 * HEADS, P])
        keys = [keys2[:, HEADS * i:HEADS * (i + 1), :] for i in range(2)]
        mW1T = keys2[:, :, :].rearrange("p (b c) (q r) -> p b (c q) r", b=B, r=RO)
        vals = [sb(f"vals{i}", [P, HEADS, 32]) for i in range(2)]
        probs = [sb(f"probs{i}", [P, HG, P]) for i in range(3)]
        probsT = [sb(f"probsT{i}", [P, HG, P]) for i in range(2)]
        neg_max = sb("neg_max", [P, UNITS, HG])
        rden = sb("rden", [P, B, HEADS])
        o_headsT = sb("o_headsT", [P, UB, P])
        o_rows = [sb(f"o_rows{i}", [P, HEADS, HD]) for i in range(2)]
        oT = sb("oT", [P, P])
        stats = sb("stats", [P, B, 6])
        mv = sb("mv", [P, 4, B, 2])
        var_ln = sb("var_ln", [P, B])
        rstd = sb("rstd", [P, 4, B])

        relu_out = sb("relu_out", [P, P])
        h_sum = sb("h_sum", [P, B])
        gT = sb("gT", [E0, B])
        g_rows = sb("g_rows", [E0 + 1, B, P])
        g_col = sb("g_col", [P, B])
        g_mix = sb("g_mix", [P, B, RO])
        mb1 = sb("mb1", [P, FC, B])
        uT = tw1[:, :, :].rearrange("p (b c) t -> p b c t", b=B)


        q1T = [sb(f"q1T{i}", [P, P]) for i in range(2)]
        p1 = c
        p1T = [sb(f"p1T{i}", [P, P]) for i in range(2)]
        neg_max1 = sb("neg_max1", [P, B])
        den1 = sb("den1", [P, B])
        rden1 = sb("rden1", [P, B])

        logit_max = sb("logit_max", [P, B])
        score = sb("score", [P, B])
        tmp_be = sb("tmp_be", [P, B, E1])
        choice = sb("choice", [P, B])
        one_hot = sb("one_hot", [P, B, E1])
        one_hot_b = sb("one_hot_b", [P, B, E1], BF16)
        tiles_i = sb("tiles_i", [P, E1], I32)
        tmp_ee = sb("tmp_ee", [P, E1, E1])
        first = sb("first", [P, E1])
        end_tile = sb("end_tile", [P, E1])
        tmp_te = sb("tmp_te", [P, LOADED, E1])
        tile_expert_f = sb("tile_expert_f", [P, LOADED])
        tile_expert = sb("tile_expert", [P, LOADED], I32)
        inner_i = sb("inner_i", [P, 1], I32)
        slot_i = sb("slot_i", [P, B], I32)
        x_rows = sb("x_rows", [P, B, ROW])

        sharedT = tw1[:, 0:C1 * B, :].rearrange("p (c b) t -> p c b t", b=B)
        silu_sh = [tw1[:, 16 + 4 * i:20 + 4 * i, :].rearrange("p c t -> p (c t)") for i in range(2)]
        tail = tw2[:, :, :].rearrange("p q (c t) -> p (q c) t", t=P)
        xs_T = [tail[:, i, :] for i in range(2)]
        silu_g = [tail[:, 2 + 2 * i:4 + 2 * i, :].rearrange("p c t -> p (c t)") for i in range(2)]
        act_r = [tail[:, 6 + 2 * i:8 + 2 * i, :].rearrange("p c t -> p (c t)") for i in range(2)]
        act_T = [tail[:, 10 + 2 * i:12 + 2 * i, :] for i in range(2)]
        sorted_in = early[:, :, :].rearrange("p c t -> p (c t)")[:, 0:LOADED * ROW].rearrange("p (t r) -> p t r", r=ROW)
        LOADS = [(0, 2), (2, 5), (5, LOADED)]
        acc_in = keys2
        ACC_LOADS = [(0, 2), (2, 6), (6, LOADED)]
        SHARED = [(0, 0, 0, 1), (1, 0, 2, 3), (0, 1, 4, 5), (1, 1, 0, 1)]
        xs_in = [sb(f"xs_in{i}", [P, D]) for i in range(2)]
        token_of = [sb(f"token_of{i}", [P, 1], I32) for i in range(2)]
        y_out = [tail[:, 14 + i, :] for i in range(2)]

        names = """gates_loaded x_loaded0 x_loaded1 c_loaded0 c_loaded1 mask_loaded0 mask_loaded1 w_loaded small_loaded tw1_loaded tw2_loaded experts_loaded
            vector_step scalar_step pool_step
            ident_made consts_bf16 consts_made eps_made empty_made heads_made spread_made tanh_made
            bq_scaled wout_scaled x_plus_bout vh_scaled pad_copied pad_made mask_made
            var_ready rstd_ready xn_written rows_T rows_T_out_v rows_T_out_s
            pre_ready pre_out_v pre_out_s keys_made vals_made
            scores max_made probs_made probs_T probs_T_out heads_out heads_T_out heads_back o_normed o_T o_T_out
            projected x1_made xn2_made xn2_T xn2_T_out gate_hidden gate_summed
            gate_out g_made g_spread g_mixed mb1_made g_rows_made mixed mixed_out hidden gelu_made ffn_out x2_made
            var3_ready rstd3_ready xn3_made xn3_T xn3_T_out q_ready q_out scores1 max1_made probs1 rden1_made probs1_T probs1_T_out
            attn1 x3_made var4_ready rstd4_ready xn4_made xn4_T xn4_T_out
            logits logit_max_made exp_made one_hot_made ranks slots_made tiles_made rows_scaled rows_filled rows_sorted
            acc_filled acc_sorted acc_loaded0 acc_loaded1 acc_loaded2
            shared_hidden shared_silu shared_act shared_out acc_made
            tiles_loaded0 tiles_loaded1 tiles_loaded2 tile_copied tile_T tile_T_out tile_hidden tile_silu tile_act act_T_ready act_T_out
            tile_y y_ready last_scattered pairs_scattered scatter_begun y_scattered0 y_scattered1""".split()
        sem = {n: ctx.enter_context(nc.semaphore(n)) for n in names}
        y_scattered = [sem["y_scattered0"], sem["y_scattered1"]]

        block = ctx.enter_context(nc.Block())

        def as_row(v):
            return v.rearrange("(a d) -> a d", a=1)

        def as_col(v):
            return v.rearrange("(d a) -> d a", a=1)

        def in_bank(i, n=4):
            return bank[i][:, 0:n * P].rearrange("p (b t) -> p b t", t=P)

        END = UNITS + 9
        GROUPS = [(-1, "cT", 0, 0, "s"), (-1, "cT", 1, 2, "s"), (-1, "xn", 0, 1, "v"),
                  (2, "w", 0, 7, "s"), (4, "xn", 1, 7, "v"),
                  (UNITS + 1, "small", 0, 0, "v"), (UNITS + 2, "w", 1, 1, "s"), (UNITS + 3, "k", 0, 0, "s"),
                  (UNITS + 4, "k", 1, 1, "v"), (UNITS + 5, "v", 0, 0, "v"), (UNITS + 6, "v", 1, 1, "v"),
                  (END, "w", 2, 0, "s"), (END, "w", 3, 1, "v"), (END + 1, "w", 4, 0, "s"), (END + 1, "w", 5, 1, "s")]
        W_GROUPS = [(0, 2), (2, 4), (4, 8), (8, 12), (12, 16), (16, 19)]

        def group(what, j):
            return [g[1:3] for g in GROUPS].index((what, j))

        def pre_emptied(what, j):
            n = group(what, j)
            e = GROUPS[n][4]
            return sem["pre_out_" + e], sum(g[4] == e for g in GROUPS[:n + 1])

        def groups_at(s, engine=None):
            return [(n, *g[1:]) for n, g in enumerate(GROUPS) if g[0] == s and engine in (None, g[4])]

        def chain_row(step, offset):
            b, r = divmod(step - offset, UB)
            return b if r == 0 and 0 <= b < B else None

        STEPS = END

        @block.sync
        def _(sp):
            def load(dst, src, s, **kw):
                sp.dma_start(dst, src, **kw).then_inc(sem[s], 16)

            for h in range(2):
                rows = slice(4 * h, 4 * h + 4)
                load(x[:, rows, :], a["x"][rows].rearrange("b s d -> s b d"), f"x_loaded{h}")
                if h == 0:
                    load(c[:, 4:8, :], a["ctx_1024"][4:8].rearrange("b s d -> s b d"), "c_loaded1")
                load(mask_i[:, rows, :], a["mask_Bx1xSxS2_ik1"][rows].rearrange("b o s k -> s (b o) k"),
                     f"mask_loaded{h}")
            for slot, name in ((WO, "L0_xattn_w_out"), (GW1, "L0_ffn_gate_w1"), (WK, "L1_xattn_Wk_w"),
                               (WV, "L1_xattn_Wv_w"), (WQ, "L1_xattn_Wq_w")):
                load(w_raw[:, slot, :], a[name], "w_loaded")
            for slot, name, n in ((W1, "L0_ffn_W1", FC), (WG, "L1_ffn_w_gate", C1), (WU, "L1_ffn_w_up", C1)):
                load(w_raw[:, slot:slot + n, :], a[name].rearrange("(c f) h -> f c h", c=n), "w_loaded")
            load(w_raw[:, W2:W2 + FC, :], a["L0_ffn_W2"].rearrange("h (c f) -> h c f", c=FC), "w_loaded")
            load(w_raw[:, WD:WD + C1, :], a["L1_ffn_w_down"].rearrange("h (c f) -> h c f", c=C1), "w_loaded")
            load(w_small[0:E0, 0, :], a["L0_ffn_gate_w2"], "w_loaded")
            load(w_small[0:E1, 1, :], a["L1_ffn_w_router"], "w_loaded")
            load(b_out[:], as_row(a["L0_xattn_b_out"]).partition_broadcast(P), "small_loaded")
            load(b_v[:], as_row(a["L1_xattn_Wv_b"]).partition_broadcast(P), "small_loaded")
            for dst, name in ((b_g1, "L0_ffn_gate_b1"), (b_q, "L1_xattn_Wq_b"), (b_k, "L1_xattn_Wk_b"),
                              (b_g2, "L0_ffn_gate_b2")):
                load(dst[:], as_col(a[name]), "small_loaded")
            load(b_1[:], a["L0_ffn_b1"].rearrange("(c f) -> f c", c=FC), "small_loaded", allow_slow_non_contiguous=True)
            load(tb1[:], a["L0_ffn_Tb1"], "small_loaded")
            load(tb2[0:E0, :], a["L0_ffn_Tb2"], "small_loaded")
            load(tb2[E0:E0 + 1, :], as_row(a["L0_ffn_b2"]), "small_loaded")
            load(pad_i, a["mask_BxS2_if1"].rearrange("(o b) k -> o b k", o=1).partition_broadcast(P), "small_loaded")
            for e in range(E0):
                load(tw1[RO * e:RO * e + RO, :, :], a["L0_ffn_TW1"][e].rearrange("(q r) h -> r q h", r=RO), "tw1_loaded")
            for e in range(E0):
                load(tw2[RO * e:RO * e + RO, :, :], a["L0_ffn_TW2"][e].rearrange("(q r) f -> r q f", r=RO), "tw2_loaded")
            load(gate_up[:], a["L1_ffn_gate_up_proj"].rearrange("e h f -> h e f"), "experts_loaded")
            load(down[:], a["L1_ffn_down_proj"].rearrange("e (c f) h -> f e c h", c=C1), "experts_loaded")
            sp.wait_ge(sem["empty_made"], 2)
            load(sorted_rows.rearrange("(t p) r -> p t r", p=P),
                 empty_row[:, :].unsqueeze(1).to_broadcast([P, LOADED, ROW]), "rows_filled")
            load(sorted_acc.rearrange("(t p) r -> p t r", p=P),
                 empty_row[:, 0:D].unsqueeze(1).to_broadcast([P, LOADED, D]), "acc_filled")
            sp.wait_ge(sem["rows_sorted"], 16 * B)
            for i, (lo, hi) in enumerate(LOADS):
                load(sorted_in[:, lo:hi, :], sorted_rows[lo * P:hi * P, :].rearrange("(t p) r -> p t r", p=P),
                     f"tiles_loaded{i}")
            sp.wait_ge(sem["acc_sorted"], 16 * B)
            for i, (lo, hi) in enumerate(ACC_LOADS):
                load(acc_in[:, lo:hi, :], sorted_acc[lo * P:hi * P, :].rearrange("(t p) d -> p t d", p=P),
                     f"acc_loaded{i}")
            sp.wait_ge(sem["tiles_made"], 1)
            inner = sp.value_load(inner_i[0:1, 0:1], min_val=MIN_PAIRS - 1, max_val=TILES // 2 - 1)
            pair_tiles = 16 * inner + 16
            sp.wait_ge(y_scattered[0], pair_tiles)
            sp.wait_ge(y_scattered[1], pair_tiles)
            sp.sem_inc(sem["pairs_scattered"], 1)
            sp.wait_ge(sem["last_scattered"], 16)

        @block.gpsimd
        def _(pool):
            steps = [0]

            def step(i):
                steps[0] += 1
                i.then_inc(sem["pool_step"], 1)
                pool.wait_ge(sem["pool_step"], steps[0])

            pool.memset(eps[:], EPS).then_inc(sem["eps_made"], 1)
            step(pool.memset(ident[:], 0.0))
            pool.affine_select(out=ident[:], in_=ident[:], compare_op=ALU.not_equal, fill=1.0, base=0,
                               pattern=[[-1, P]], channel_multiplier=1).then_inc(sem["ident_made"], 1)
            pool.wait_ge(sem["ident_made"], 1)
            pool.tensor_copy(ident_b[:], ident[:]).then_inc(sem["consts_bf16"], 1)
            pool.memset(vals[0][:], 0.0).then_inc(sem["pool_step"], 1)
            step(pool.memset(vals[1][:], 0.0))
            steps[0] += 1
            pool.wait_ge(sem["pool_step"], steps[0])
            for i in range(2):
                pool.memset(vals[i][:, :, HD:HD + 1], 1.0).then_inc(sem["consts_made"], 1)

            def make_vals(b):
                if b >= 2:
                    pool.wait_ge(sem["heads_out"], UB * (b - 1))
                pool.tensor_copy(vals[b % 2][:, :, 0:HD], c[:, b, :].rearrange("p (h d) -> p h d", d=HD)
                                 ).then_inc(sem["vals_made"], 1)

            def make_keys(b):
                pool.wait_ge(*pre_emptied("cT", b // 4))
                if b >= 2:
                    pool.wait_ge(sem["scores"], UB * (b - 1))
                n = HG if b == 0 else HEADS
                for h in range(0, HEADS, n):
                    pool.tensor_tensor(keys[b % 2][:, h:h + n, :], cT[:, b:b + 1, :].to_broadcast([P, n, P]),
                                       head_of[:, h:h + n].unsqueeze(2).to_broadcast([P, n, P]), ALU.mult
                                       ).then_inc(sem["keys_made"], 1)

            pool.wait_ge(sem["heads_made"], 1)
            make_keys(0)
            pool.wait_ge(sem["c_loaded0"], 16)
            make_vals(0)
            make_keys(1)
            make_vals(1)
            make_keys(2)
            pool.wait_ge(sem["tanh_made"], 1)
            pool.wait_ge(*pre_emptied("w", 0))
            pool.tensor_scalar(w_t[:, WO, :], w_t[:, WO, :], tgate[:, 0:1], None, ALU.mult).then_inc(sem["wout_scaled"], 1)
            pool.wait_ge(sem["small_loaded"], 11 * 16)
            step(pool.tensor_scalar(b_out[:], b_out[:], tgate[:, 0:1], None, ALU.mult))
            pool.tensor_scalar(b_q[:], b_q[:], SCALE, None, ALU.mult).then_inc(sem["bq_scaled"], 1)
            pool.wait_ge(sem["xn_written"], B)
            pool.tensor_tensor(x[:], x[:], b_out[:, :].unsqueeze(1).to_broadcast([P, B, D]), ALU.add
                               ).then_inc(sem["x_plus_bout"], 1)
            make_vals(2)
            pool.memset(g_rows[:], 1.0).then_inc(sem["consts_made"], 1)
            pool.memset(ones_b[:], 1.0).then_inc(sem["consts_bf16"], 1)
            step(pool.memset(before[:], 1.0))
            pool.affine_select(out=before[:], in_=before[:], compare_op=ALU.is_gt, fill=0.0, base=0,
                               pattern=[[1, P]], channel_multiplier=-1).then_inc(sem["consts_bf16"], 1)
            make_keys(3)
            make_vals(3)
            step(pool.memset(lower[:], 1.0))
            pool.affine_select(out=lower[:], in_=lower[:], compare_op=ALU.is_gt, fill=0.0, base=0,
                               pattern=[[1, E1], [-1, E1]], channel_multiplier=0).then_inc(sem["consts_made"], 1)
            pool.iota(expert_no[:], [[1, E1]], base=0, channel_multiplier=0,
                      allow_small_or_imprecise_dtypes=True).then_inc(sem["consts_made"], 1)
            pool.iota(expert_low[:], [[1, E1]], base=-E1, channel_multiplier=0,
                      allow_small_or_imprecise_dtypes=True).then_inc(sem["consts_made"], 1)
            pool.iota(tile_no[:], [[1, LOADED]], base=0, channel_multiplier=0,
                      allow_small_or_imprecise_dtypes=True).then_inc(sem["consts_made"], 1)
            pool.wait_ge(sem["pad_copied"], 1)
            pool.affine_select(out=pad_b[:], in_=pad_f[:], compare_op=ALU.is_ge, fill=MASKED_L1, base=0,
                               pattern=[[0, B], [-1, P]], channel_multiplier=1).then_inc(sem["pad_made"], 1)
            make_keys(4)
            pool.wait_ge(sem["c_loaded1"], 16)
            make_vals(4)
            pool.memset(empty_row[:, 0:D], 0.0).then_inc(sem["empty_made"], 1)
            pool.iota(empty_row[:, D:ROW].bitcast(I32), [[0, 1]], base=NO_TOKEN, channel_multiplier=0
                      ).then_inc(sem["empty_made"], 1)
            pool.iota(x_rows[:, :, D:ROW].bitcast(I32), [[P, B], [0, 1]], base=0, channel_multiplier=1
                      ).then_inc(sem["consts_made"], 1)
            for b in range(5, B):
                make_keys(b)
                make_vals(b)
            pool.wait_ge(*pre_emptied("v", 1))
            pool.tensor_scalar(vh[:], vh[:], tgate[:, 1:2], None, ALU.mult).then_inc(sem["vh_scaled"], 1)
            pool.wait_ge(sem["g_made"], 1)
            pool.wait_ge(sem["consts_made"], 3)
            pool.tensor_copy(g_rows[0:E0, :, :], gT[:, :].unsqueeze(2).to_broadcast([E0, B, P])
                             ).then_inc(sem["g_rows_made"], 1)
            pool.wait_ge(sem["slots_made"], 1)
            pool.wait_ge(sem["rows_filled"], 16)
            for b in range(B):
                pool.wait_ge(sem["rows_scaled"], b + 1)
                pool.indirect_dma_start(
                    out=sorted_rows, in_=x_rows[:, b, :], in_offset=None,
                    out_offset=bass.IndirectOffsetOnAxis(ap=slot_i[:, b:b + 1].bitcast(U32), axis=0)
                ).then_inc(sem["rows_sorted"], 16)
            pool.wait_ge(sem["acc_filled"], 16)
            for b in range(B):
                pool.wait_ge(sem["acc_made"], b // 4 + 1)
                pool.indirect_dma_start(
                    out=sorted_acc, in_=x[:, b, :], in_offset=None,
                    out_offset=bass.IndirectOffsetOnAxis(ap=slot_i[:, b:b + 1].bitcast(U32), axis=0)
                ).then_inc(sem["acc_sorted"], 16)
            pool.wait_ge(sem["tiles_made"], 1)
            inner = pool.value_load(inner_i[0:1, 0:1], min_val=MIN_PAIRS - 1, max_val=TILES // 2 - 1)

            def scatter_rows(k, t, done=None):
                pool.wait_ge(sem["y_ready"], 2 * t + 2)
                pool.sem_inc(sem["scatter_begun"], 1)
                pool.indirect_dma_start(
                    out=out.rearrange("b s d -> (b s) d"), in_=y_out[k], in_offset=None, bounds_check=B * S - 1,
                    oob_is_err=False,
                    out_offset=bass.IndirectOffsetOnAxis(ap=token_of[k][:, 0:1].bitcast(U32), axis=0)
                ).then_inc(done or y_scattered[k], 16)

            scatter_rows(0, 0)
            scatter_rows(1, 1)
            with pool.Fori(1, inner + 1) as i:
                scatter_rows(0, 2 * i)
                scatter_rows(1, 2 * i + 1)
            scatter_rows(0, 2 * inner + 2, sem["last_scattered"])

        @block.scalar
        def _(act):
            A = nc.scalar.activation
            steps = [0]

            def step(i):
                steps[0] += 1
                i.then_inc(sem["scalar_step"], 1)
                act.wait_ge(sem["scalar_step"], steps[0])

            def inv_std(n, rows, done):
                step(A(var_ln[:, rows], mv[:, n, rows, 1], ACT.Ln, bias=eps[:, 0:1]))
                A(rstd[:, n, rows], var_ln[:, rows], ACT.Exp, scale=-0.5).then_inc(sem[done], 1)

            act.dma_start(gates[:, 0:2], as_row(a["g_xattn"]).partition_broadcast(P)).then_inc(sem["gates_loaded"], 16)
            act.dma_start(gates[:, 2:4], as_row(a["g_ffn"]).partition_broadcast(P)).then_inc(sem["gates_loaded"], 16)
            act.dma_start(c[:, 0:4, :], a["ctx_1024"][0:4].rearrange("b s d -> s b d")).then_inc(sem["c_loaded0"], 16)
            act.wait_ge(sem["gates_loaded"], 32)
            A(tgate[:], gates[:], ACT.Tanh).then_inc(sem["tanh_made"], 1)
            nc.scalar.preload_act_table_set(LN_EXP_SET)

            def empty_groups(s):
                for n, what, j, at, e in groups_at(s, "s"):
                    act.wait_ge(sem["pre_ready"], n + 1)
                    if what == "k":
                        act.wait_ge(sem["small_loaded"], 11 * 16)
                        i = A(kT[:, 4 * j:4 * j + 4, :], in_bank(at), ACT.Identity, bias=b_k[:, 0:1])
                    elif what == "cT":
                        i = A(cT[:, 4 * j:4 * j + 4, :], in_bank(at), ACT.Copy)
                    else:
                        lo, hi = W_GROUPS[j]
                        i = A(w_t[:, lo:hi, :], in_bank(at, hi - lo), ACT.Copy)
                    i.then_inc(sem["pre_out_s"], 1)

            def first_inv_std(h):
                act.wait_ge(sem["var_ready"], h + 1)
                inv_std(0, slice(4 * h, 4 * h + 4), "rstd_ready")

            act.wait_ge(sem["eps_made"], 1)
            first_inv_std(0)
            empty_groups(-1)
            for s in range(STEPS):
                b = chain_row(s, 2 * UB)
                if b is not None:
                    act.wait_ge(sem["o_T"], b + 1)
                    A(oT[:], bank[7][:, 0:P], ACT.Copy).then_inc(sem["o_T_out"], 1)
                b = chain_row(s, 2 * UB + 2)
                if b is not None:
                    act.wait_ge(sem["xn2_T"], b + 1)
                    A(xnT[:, b, :], bank[7][:, 0:P], ACT.Copy).then_inc(sem["xn2_T_out"], 1)
                if s < UNITS:
                    act.wait_ge(sem["max_made"], s + 1)
                    if s >= 3:
                        act.wait_ge(sem["probs_T"], s - 2)
                    for h in range(HG):
                        i = A(probs[s % 3][:, h, :], bank[s % 3][:, h * P:(h + 1) * P], ACT.Exp,
                              bias=neg_max[:, s, h:h + 1])
                    i.then_inc(sem["probs_made"], 1)
                b = chain_row(s, 2 * UB - 2)
                if b is not None:
                    act.wait_ge(sem["heads_out"], UB * (b + 1))
                    if b >= 1:
                        act.wait_ge(sem["heads_back"], b)
                    A(o_headsT[:], in_bank(5 + b % 2), ACT.Copy).then_inc(sem["heads_T_out"], 1)
                b = chain_row(s, 2 * UB)
                if b is not None:
                    act.wait_ge(sem["var_ready"], b + 3)
                    inv_std(1, slice(b, b + 1), "rstd_ready")
                b = chain_row(s, 2 * UB + 2)
                if b is not None:
                    act.wait_ge(sem["gate_hidden"], b + 1)
                    A(relu_out[:], bank[7][:, P:2 * P], ACT.Relu, bias=b_g1[:, 0:1], accum_out=h_sum[:, b:b + 1]
                      ).then_inc(sem["gate_summed"], 1)
                    act.wait_ge(sem["gate_summed"], b + 1)
                if s == 0:
                    first_inv_std(1)
                empty_groups(s)
            act.wait_ge(sem["gate_out"], 1)
            A(gT[:], bank[2][0:E0, 0:B], ACT.Identity, scale=1.0 / S, bias=b_g2[:, 0:1]).then_inc(sem["g_made"], 1)

            empty_groups(END)
            empty_groups(END + 1)
            nc.scalar.preload_act_table_set("gelu_apprx_tanh_and_others")

            act.wait_ge(sem["mb1_made"], 1)
            for b in range(B):
                act.wait_ge(sem["hidden"], b + 1)
                for f in range(FC):
                    i = A(uT[:, b, f, :], bank[b % 2][:, f * P:(f + 1) * P], ACT.Gelu_apprx_tanh, bias=mb1[:, f, b:b + 1])
                i.then_inc(sem["gelu_made"], 1)
            nc.scalar.preload_act_table_set(LN_EXP_SET)

            act.wait_ge(sem["bq_scaled"], 1)
            for s in range(B + 6):
                if 3 <= s < B + 3:
                    b = s - 3
                    act.wait_ge(sem["max1_made"], b + 1)
                    A(p1[:, b, :], bank[4 + b % 2][:, 0:P], ACT.Exp, bias=neg_max1[:, b:b + 1],
                      accum_out=den1[:, b:b + 1]).then_inc(sem["probs1"], 1)
                if 2 <= s < B + 2:
                    b = s - 2
                    act.wait_ge(sem["q_ready"], b + 1)
                    if b >= 2:
                        act.wait_ge(sem["scores1"], b - 1)
                    A(q1T[b % 2][:], bank[2 + b % 2][:, P:2 * P], ACT.Identity, scale=SCALE, bias=b_q[:, 0:1]
                      ).then_inc(sem["q_out"], 1)
                if 5 <= s < B + 5:
                    b = s - 5
                    act.wait_ge(sem["var4_ready"], b + 1)
                    inv_std(3, slice(b, b + 1), "rstd4_ready")
                if 3 <= s < B + 3:
                    b = s - 3
                    act.wait_ge(sem["probs1_T"], b + 1)
                    if b >= 2:
                        act.wait_ge(sem["attn1"], b - 1)
                    A(p1T[b % 2][:], bank[6][:, 0:P], ACT.Copy).then_inc(sem["probs1_T_out"], 1)
                if 1 <= s < B + 1:
                    b = s - 1
                    act.wait_ge(sem["xn3_T"], b + 1)
                    A(xnT[:, b, :], bank[2 + b % 2][:, 0:P], ACT.Copy).then_inc(sem["xn3_T_out"], 1)
                if s < B:
                    act.wait_ge(sem["var3_ready"], s + 1)
                    inv_std(2, slice(s, s + 1), "rstd3_ready")
                if 6 <= s:
                    b = s - 6
                    act.wait_ge(sem["xn4_T"], b + 1)
                    A(xnT[:, b, :], bank[7][:, 0:P], ACT.Copy).then_inc(sem["xn4_T_out"], 1)
            act.wait_ge(sem["logit_max_made"], 1)
            A(score[:], logit_max[:], ACT.Exp, scale=-1.0).then_inc(sem["exp_made"], 1)
            for i, (f, h, gate_bank, up_bank) in enumerate(SHARED):
                act.wait_ge(sem["shared_hidden"], 2 * i + 1)
                if i >= 2:
                    act.wait_ge(sem["shared_act"], i - 1)
                A(silu_sh[i % 2], bank[gate_bank][:], ACT.Silu).then_inc(sem["shared_silu"], 1)

            act.wait_ge(sem["tiles_made"], 1)
            inner = act.value_load(inner_i[0:1, 0:1], min_val=MIN_PAIRS - 1, max_val=TILES // 2 - 1)

            def tile_T_out(k, t):
                act.wait_ge(sem["tile_T"], t + 1)
                A(xs_T[k % 2], bank[k % 2][:, 0:P], ACT.Copy).then_inc(sem["tile_T_out"], 1)

            def tile_copy(k, t):
                A(xs_in[k % 2][:], sorted_in[:, bass.ds(t, 1), 0:D].rearrange("p a d -> p (a d)"), ACT.Copy
                  ).then_inc(sem["tile_copied"], 1)

            def tile_silu(k, t):
                act.wait_ge(sem["tile_hidden"], t + 1)
                A(silu_g[k % 2], bank[2 + k % 2][:, 0:F1], ACT.Silu).then_inc(sem["tile_silu"], 1)

            def pair(i):
                for k in (0, 1):
                    t = 2 * i + k
                    tile_T_out(k + 3, t + 3)
                    tile_copy(k + 4, t + 4)
                    tile_silu(k + 2, t + 2)

            act.wait_ge(sem["tiles_loaded0"], 16)
            tile_copy(0, 0)
            tile_copy(1, 1)
            tile_T_out(0, 0)
            act.wait_ge(sem["tiles_loaded1"], 16)
            tile_copy(2, 2)
            tile_T_out(1, 1)
            tile_copy(3, 3)
            tile_silu(0, 0)
            tile_T_out(2, 2)
            tile_silu(1, 1)
            act.wait_ge(sem["tiles_loaded2"], 16)
            pair(0)
            with act.Fori(1, inner) as i:
                pair(i)
            tile_silu(0, 2 * inner + 2)

        @block.vector
        def _(v):
            steps = [0]

            def step(i):
                steps[0] += 1
                i.then_inc(sem["vector_step"], 1)
                v.wait_ge(sem["vector_step"], steps[0])

            def row_stats(n, b):
                step(v.bn_stats(stats[:, b, :], x[:, b, :]))
                return v.bn_aggr(mv[:, n, b, :], stats[:, b, :])

            def normed(n, b, done):
                v.tensor_scalar(xn[:, b, :], x[:, b, :], mv[:, n, b, 0:1], rstd[:, n, b:b + 1],
                                ALU.subtract, ALU.mult).then_inc(sem[done], 1)

            v.wait_ge(sem["ident_made"], 1)
            v.tensor_reduce(head_of[:], ident[:, :].rearrange("p (h d) -> p h d", d=HD), X, ALU.add
                            ).then_inc(sem["heads_made"], 1)
            v.tensor_reduce(same_row[:], ident[:, :].rearrange("p (e r) -> p r e", r=RO), X, ALU.add
                            ).then_inc(sem["vector_step"], 1)
            step(v.tensor_copy(spread[:, :].rearrange("p (e r) -> p e r", r=RO),
                               ident[0:E0, 0:E0].unsqueeze(2).to_broadcast([E0, E0, RO])))
            steps[0] += 1
            v.wait_ge(sem["vector_step"], steps[0])

            def first_stats(h):
                v.wait_ge(sem[f"x_loaded{h}"], 16)
                for b in range(4 * h, 4 * h + 4):
                    i = v.bn_stats(stats[:, b, :], x[:, b, :])
                step(i)
                for b in range(4 * h, 4 * h + 4):
                    i = v.bn_aggr(mv[:, 0, b, :], stats[:, b, :])
                i.then_inc(sem["var_ready"], 1)

            def make_mask(h):
                rows = slice(4 * h, 4 * h + 4)
                v.wait_ge(sem[f"mask_loaded{h}"], 16)
                v.tensor_scalar(mask_b[:, rows, :], mask_i[:, rows, :], 0.0, MASKED_L0, ALU.is_equal, ALU.mult
                                ).then_inc(sem["mask_made"], 1)

            def first_normed(h):
                v.wait_ge(sem["rstd_ready"], h + 1)
                for b in range(4 * h, 4 * h + 4):
                    normed(0, b, "xn_written")

            def empty_groups(s):
                for n, what, j, at, e in groups_at(s, "v"):
                    v.wait_ge(sem["pre_ready"], n + 1)
                    rows = slice(4 * j, 4 * j + 4)
                    if what == "xn":
                        i = v.tensor_scalar(xnT[:, rows, :], in_bank(at), SCALE, None, ALU.mult)
                    elif what == "k":
                        v.wait_ge(sem["small_loaded"], 11 * 16)
                        i = v.tensor_scalar(kT[:, rows, :], in_bank(at), b_k[:, 0:1], None, ALU.add)
                    elif what == "v":
                        v.wait_ge(sem["small_loaded"], 11 * 16)
                        i = v.tensor_tensor(vh[:, rows, :], in_bank(at), b_v[:, :].unsqueeze(1).to_broadcast([P, 4, D]),
                                            ALU.add)
                    elif what == "small":
                        step(v.tensor_copy(gate2T[:], bank[at][:, 0:E0]))
                        i = v.tensor_copy(routerT[:], bank[at][:, E0:E0 + E1])
                    else:
                        lo, hi = W_GROUPS[j]
                        i = v.tensor_copy(w_t[:, lo:hi, :], in_bank(at, hi - lo))
                    i.then_inc(sem["pre_out_v"], 1)

            first_stats(0)
            make_mask(0)
            first_normed(0)
            empty_groups(-1)

            for s in range(STEPS):
                if s < UNITS:
                    v.wait_ge(sem["scores"], s + 1)
                    v.tensor_reduce(neg_max[:, s, :], in_bank(s % 3), X, ALU.max, negate=True).then_inc(sem["max_made"], 1)
                if 2 <= s < UNITS + 2:
                    u = s - 2
                    v.wait_ge(sem["probs_T"], u + 1)
                    if u >= 2:
                        v.wait_ge(sem["heads_out"], u - 1)
                    v.tensor_copy(probsT[u % 2][:], in_bank(3 + u % 2)).then_inc(sem["probs_T_out"], 1)
                b = chain_row(s, 2 * UB - 1)
                if b is not None:
                    heads = bank[5 + b % 2][:, :].rearrange("p (h d) -> p h d", d=32)
                    v.wait_ge(sem["heads_back"], b + 1)
                    step(v.reciprocal(rden[:, b, :], heads[:, :, HD]))
                    if b >= 2:
                        v.wait_ge(sem["o_T"], b - 1)
                    v.tensor_tensor(o_rows[b % 2][:], heads[:, :, 0:HD],
                                    rden[:, b, :].unsqueeze(2).to_broadcast([P, HEADS, HD]), ALU.mult
                                    ).then_inc(sem["o_normed"], 1)
                b = chain_row(s, 2 * UB)
                if b is not None:
                    v.wait_ge(sem["projected"], b + 1)
                    v.wait_ge(sem["x_plus_bout"], 1)
                    v.tensor_tensor(x[:, b, :], bank[7][:, P:2 * P], x[:, b, :], ALU.add).then_inc(sem["x1_made"], 1)
                    v.wait_ge(sem["x1_made"], b + 1)
                    row_stats(1, b).then_inc(sem["var_ready"], 1)
                b = chain_row(s, 2 * UB + 1)
                if b is not None:
                    v.wait_ge(sem["rstd_ready"], b + 3)
                    normed(1, b, "xn2_made")
                if s == 0:
                    first_stats(1)
                if s == 1:
                    make_mask(1)
                    first_normed(1)
                if s == 6:
                    v.wait_ge(sem["small_loaded"], 11 * 16)
                    v.tensor_scalar(pad_f[:], pad_i, 0.0, MASKED_L1, ALU.is_equal, ALU.mult
                                    ).then_inc(sem["pad_copied"], 1)
                empty_groups(s)

            v.wait_ge(sem["g_spread"], 1)
            step(v.tensor_copy(g_col[:], bank[2][:, 16:16 + B]))
            v.tensor_tensor(g_mix[:], g_col[:, :].unsqueeze(2).to_broadcast([P, B, RO]),
                            same_row[:, :].unsqueeze(1).to_broadcast([P, B, RO]), ALU.mult).then_inc(sem["g_mixed"], 1)
            empty_groups(END)
            v.wait_ge(sem["g_spread"], 2)
            v.tensor_tensor(mb1[:], bank[7][:, 0:FC * B].rearrange("p (c b) -> p c b", b=B),
                            b_1[:, :].unsqueeze(2).to_broadcast([P, FC, B]), ALU.add).then_inc(sem["mb1_made"], 1)
            w1_rows = w_t[:, W1:W1 + FC, :].rearrange("p c (q r) -> p (c q) r", r=RO)
            for m in range(16):
                v.wait_ge(sem["mixed"], m + 1)
                src = bank[3 + m % 4][:, :].rearrange("p (j b r) -> p j b r", b=B, r=RO)
                if m < 8:
                    to = mW1T[:, :, 4 * m:4 * m + 4, :]
                    base = w1_rows[:, 4 * m:4 * m + 4, :]
                else:
                    f, h = divmod(m - 8, 2)
                    to = mW2T[:, :, f, 4 * h:4 * h + 4, :]
                    base = w_t[:, W2 + f, :].rearrange("p (q r) -> p q r", r=RO)[:, 4 * h:4 * h + 4, :]
                v.tensor_tensor(to.rearrange("p b j r -> p j b r"), src, base.unsqueeze(2).to_broadcast([P, 4, B, RO]),
                                ALU.add).then_inc(sem["mixed_out"], 1)

            for s in range(B + 6):
                if s < B:
                    v.wait_ge(sem["ffn_out"], s + 1)
                    v.scalar_tensor_tensor(out=x[:, s, :], in0=bank[s % 2][:, 0:P], scalar=tgate[:, 2:3],
                                           in1=x[:, s, :], op0=ALU.mult, op1=ALU.add).then_inc(sem["x2_made"], 1)
                if 3 <= s < B + 3:
                    b = s - 3
                    v.wait_ge(sem["scores1"], b + 1)
                    v.tensor_reduce(neg_max1[:, b:b + 1], bank[4 + b % 2][:, 0:P], X, ALU.max, negate=True
                                    ).then_inc(sem["max1_made"], 1)
                if 6 <= s:
                    b = s - 6
                    v.wait_ge(sem["rstd4_ready"], b + 1)
                    normed(3, b, "xn4_made")
                if 4 <= s < B + 4:
                    b = s - 4
                    v.wait_ge(sem["rden1_made"], b + 1)
                    v.wait_ge(sem["attn1"], b + 1)
                    v.scalar_tensor_tensor(out=x[:, b, :], in0=bank[6][:, P:2 * P], scalar=rden1[:, b:b + 1],
                                           in1=x[:, b, :], op0=ALU.mult, op1=ALU.add).then_inc(sem["x3_made"], 1)
                if 1 <= s < B + 1:
                    b = s - 1
                    v.wait_ge(sem["rstd3_ready"], b + 1)
                    normed(2, b, "xn3_made")
                if s < B:
                    v.wait_ge(sem["x2_made"], s + 1)
                    row_stats(2, s).then_inc(sem["var3_ready"], 1)
                if 3 <= s < B + 3:
                    b = s - 3
                    v.wait_ge(sem["probs1"], b + 1)
                    v.reciprocal(rden1[:, b:b + 1], den1[:, b:b + 1]).then_inc(sem["rden1_made"], 1)
                if 4 <= s < B + 4:
                    b = s - 4
                    v.wait_ge(sem["x3_made"], b + 1)
                    row_stats(3, b).then_inc(sem["var4_ready"], 1)

            v.wait_ge(sem["logits"], 1)
            v.wait_ge(sem["consts_made"], 8)
            logits = bank[7][:, P:P + B * E1].rearrange("p (b e) -> p b e", e=E1)
            experts = expert_no[:, :].unsqueeze(1).to_broadcast([P, B, E1])
            v.tensor_reduce(logit_max[:], logits, X, ALU.max).then_inc(sem["logit_max_made"], 1)
            v.wait_ge(sem["logit_max_made"], 1)
            step(v.tensor_tensor(tmp_be[:], logits, logit_max[:, :].unsqueeze(2).to_broadcast([P, B, E1]), ALU.is_equal))
            step(v.scalar_tensor_tensor(out=tmp_be[:], in0=tmp_be[:], scalar=-float(E1), in1=experts, op0=ALU.mult, op1=ALU.add))
            step(v.tensor_reduce(choice[:], tmp_be[:], X, ALU.min))
            choices = choice[:, :].unsqueeze(2).to_broadcast([P, B, E1])
            numbers = expert_low[:, :].unsqueeze(1).to_broadcast([P, B, E1])
            v.tensor_tensor(one_hot_b[:], numbers, choices, ALU.is_equal).then_inc(sem["one_hot_made"], 1)
            v.tensor_tensor(one_hot[:], numbers, choices, ALU.is_equal).then_inc(sem["vector_step"], 1)
            steps[0] += 1
            v.wait_ge(sem["exp_made"], 1)
            step(v.tensor_scalar(score[:], score[:], 1.0, None, ALU.add))
            step(v.reciprocal(score[:], score[:]))
            for b in range(B // 2):
                v.tensor_scalar(x_rows[:, b, 0:D], xn[:, b, :], score[:, b:b + 1], None, ALU.mult
                                ).then_inc(sem["rows_scaled"], 1)
            v.wait_ge(sem["ranks"], 1)
            step(v.tensor_scalar(tiles_i[:], bank[6][:, 256:256 + E1], float(P - 1), None, ALU.add))
            step(v.tensor_scalar(tiles_i[:], tiles_i[:], 7, None, ALU.logical_shift_right))
            step(v.tensor_tensor(tmp_ee[:], lower[:], tiles_i[:, :].unsqueeze(1).to_broadcast([P, E1, E1]), ALU.mult))
            step(v.tensor_reduce(first[:], tmp_ee[:], X, ALU.add))
            ranks = bank[6][:, 128:128 + B * E1].rearrange("p (b e) -> p b e", e=E1)
            step(v.scalar_tensor_tensor(out=tmp_be[:], in0=first[:, :].unsqueeze(1).to_broadcast([P, B, E1]),
                                        scalar=float(P), in1=ranks, op0=ALU.mult, op1=ALU.add))
            step(v.tensor_tensor(tmp_be[:], tmp_be[:], one_hot[:], ALU.mult))
            with nc.allow_low_precision("whole numbers"):
                v.tensor_reduce(slot_i[:], tmp_be[:], X, ALU.add).then_inc(sem["slots_made"], 1)

            def shared_act(i):
                f, h, gate_bank, up_bank = SHARED[i]
                v.wait_ge(sem["shared_hidden"], 2 * i + 2)
                v.wait_ge(sem["shared_silu"], i + 1)
                v.tensor_tensor(sharedT[:, f, 4 * h:4 * h + 4, :].rearrange("p b t -> p (b t)"),
                                bank[up_bank][:], silu_sh[i % 2], ALU.mult).then_inc(sem["shared_act"], 1)

            def add_shared(h):
                v.wait_ge(sem["shared_out"], h + 1)
                xh = x[:, 4 * h:4 * h + 4, :].rearrange("p b t -> p (b t)")
                v.scalar_tensor_tensor(out=xh, in0=bank[(7, 3)[h]][:], scalar=tgate[:, 3:4], in1=xh,
                                       op0=ALU.mult, op1=ALU.add).then_inc(sem["acc_made"], 1)

            shared_act(0)
            shared_act(1)
            for b in range(B // 2, B):
                v.tensor_scalar(x_rows[:, b, 0:D], xn[:, b, :], score[:, b:b + 1], None, ALU.mult
                                ).then_inc(sem["rows_scaled"], 1)
            shared_act(2)
            add_shared(0)
            step(v.tensor_tensor(end_tile[:], first[:], tiles_i[:], ALU.add))
            step(v.tensor_tensor(tmp_te[:], tile_no[:, :].unsqueeze(2).to_broadcast([P, LOADED, E1]),
                                 end_tile[:, :].unsqueeze(1).to_broadcast([P, LOADED, E1]), ALU.is_ge))
            step(v.tensor_reduce(tile_expert_f[:], tmp_te[:], X, ALU.add))
            step(v.tensor_scalar(tile_expert[:], tile_expert_f[:], float(E1 - 1), None, ALU.min))
            step(v.tensor_scalar(inner_i[:], end_tile[:, E1 - 1:E1], -2.0, None, ALU.add))
            v.tensor_scalar(inner_i[:], inner_i[:], 1, None, ALU.logical_shift_right).then_inc(sem["tiles_made"], 1)
            shared_act(3)
            add_shared(1)

            v.wait_ge(sem["tiles_made"], 1)
            inner = v.value_load(inner_i[0:1, 0:1], min_val=MIN_PAIRS - 1, max_val=TILES // 2 - 1)

            def tile_act(k, t):
                v.wait_ge(sem["tile_silu"], t + 1)
                v.tensor_tensor(act_r[k % 2], bank[2 + k % 2][:, F1:2 * F1], silu_g[k % 2], ALU.mult
                                ).then_inc(sem["tile_act"], 1)

            def act_T_out(k, t):
                v.wait_ge(sem["act_T_ready"], t + 1)
                v.tensor_copy(act_T[k % 2], in_bank(4 + k % 2, C1)).then_inc(sem["act_T_out"], 1)

            def y_scaled(k, t, scattered):
                if scattered is not None:
                    v.wait_ge(y_scattered[k % 2], scattered)
                v.tensor_copy(token_of[k % 2][:], sorted_in[:, bass.ds(t, 1), D:ROW].rearrange("p a d -> p (a d)").bitcast(I32)).then_inc(sem["y_ready"], 1)
                v.wait_ge(sem["tile_y"], t + 1)
                v.scalar_tensor_tensor(out=y_out[k % 2], in0=bank[6 + k % 2][:, 0:P], scalar=tgate[:, 3:4],
                                       in1=acc_in[:, bass.ds(t, 1), :].rearrange("p a d -> p (a d)"),
                                       op0=ALU.mult, op1=ALU.add).then_inc(sem["y_ready"], 1)

            tile_act(0, 0)

            def pair(i, first=False):
                for k in (0, 1):
                    t = 2 * i + k
                    act_T_out(k, t)
                    tile_act(k + 1, t + 1)
                    if first and k == 0:
                        v.wait_ge(sem["acc_loaded0"], 16)
                    y_scaled(k, t, None if first else 16 * i)

            pair(0, first=True)
            v.wait_ge(sem["acc_loaded1"], 16)
            pair(1)
            pair(2)
            v.wait_ge(sem["acc_loaded2"], 16)
            with v.Fori(3, inner + 1) as i:
                pair(i)
            act_T_out(0, 2 * inner + 2)
            y_scaled(0, 2 * inner + 2, 16 * inner + 16)

        @block.tensor
        def _(pe):
            mm = pe.matmul

            def transpose(to, rows):
                n = rows.shape[0]
                return pe.transpose(to, rows, ident[0:n, 0:n])

            def col(i, n=1):
                return slice(i * P, (i + n) * P)

            def run_groups(s):
                for n, what, j, at, e in groups_at(s):
                    before_it = [g for g in GROUPS[:n] if g[3] == at]
                    if at == 7 and before_it:
                        pe.wait_ge(*pre_emptied(*before_it[-1][1:3]))
                    if at < 7 and s > 0:
                        if before_it[-1][0] > 0:
                            pe.wait_ge(*pre_emptied(*before_it[-1][1:3]))
                        else:
                            pe.wait_ge(sem["probs_made"], UNITS)
                    to = bank[at]
                    if what == "cT":
                        pe.wait_ge(sem[f"c_loaded{j}"], 16)
                        for m in range(4):
                            i = transpose(to[:, col(m)], c[:, 4 * j + m, :])
                    elif what == "xn":
                        pe.wait_ge(sem["xn_written"], 4 * j + 4)
                        for m in range(4):
                            i = transpose(to[:, col(m)], xn[:, 4 * j + m, :])
                    elif what == "w":
                        pe.wait_ge(sem["w_loaded"], 12 * 16)
                        lo, hi = W_GROUPS[j]
                        for m in range(hi - lo):
                            i = transpose(to[:, col(m)], w_raw[:, lo + m, :])
                    elif what == "small":
                        transpose(to[:, 0:E0], w_small[0:E0, 0, :])
                        i = transpose(to[:, E0:E0 + E1], w_small[0:E1, 1, :])
                    elif what == "k":
                        pe.wait_ge(*pre_emptied("w", 1))
                        i = mm(to[:], w_t[:, WK, :], cT[:, 4 * j:4 * j + 4, :], start=True, stop=True)
                    else:
                        for m in range(4):
                            i = mm(to[:, col(m)], cT[:, 4 * j + m, :], w_t[:, WV, :], start=True, stop=True)
                    i.then_inc(sem["pre_ready"], 1)

            pe.wait_ge(sem["ident_made"], 1)
            run_groups(-1)
            pe.wait_ge(*pre_emptied("cT", 1))
            pe.wait_ge(*pre_emptied("xn", 0))
            pe.wait_ge(sem["mask_made"], 1)
            pe.wait_ge(sem["consts_bf16"], 1)

            for s in range(STEPS):
                if s < UNITS:
                    b, g = divmod(s, UB)
                    pe.wait_ge(sem["keys_made"], g + 1 if b == 0 else UB + b)
                    if s == UNITS // 2:
                        pe.wait_ge(*pre_emptied("xn", 1))
                        pe.wait_ge(sem["mask_made"], 2)
                    if s >= 3:
                        pe.wait_ge(sem["probs_made"], s - 2)
                    mm(bank[s % 3][:], xnT[:, b, :], keys[b % 2][:, HG * g:HG * g + HG, :], start=True, stop=False)
                    mm(bank[s % 3][:], ident_b[:], mask_b[:, b:b + 1, :].to_broadcast([P, HG, P]), start=False,
                       stop=True).then_inc(sem["scores"], 1)
                b = chain_row(s, 2 * UB)
                if b is not None:
                    pe.wait_ge(sem["o_normed"], b + 1)
                    if b == 0:
                        pe.wait_ge(*pre_emptied("xn", 1))
                    else:
                        pe.wait_ge(sem["gate_summed"], b)
                    transpose(bank[7][:, 0:P], o_rows[b % 2][:, :, :].rearrange("p h d -> p (h d)")
                              ).then_inc(sem["o_T"], 1)
                b = chain_row(s, 2 * UB + 2)
                if b is not None:
                    pe.wait_ge(sem["xn2_made"], b + 1)
                    transpose(bank[7][:, 0:P], xn[:, b, :]).then_inc(sem["xn2_T"], 1)
                if 2 <= s < UNITS + 2:
                    u = s - 2
                    pe.wait_ge(sem["probs_made"], u + 1)
                    if u >= 2:
                        pe.wait_ge(sem["probs_T_out"], u - 1)
                    for h in range(HG):
                        n = transpose(bank[3 + u % 2][:, col(h)], probs[u % 3][:, h, :])
                    n.then_inc(sem["probs_T"], 1)
                b = chain_row(s, 2 * UB - 1)
                if b is not None:
                    pe.wait_ge(sem["heads_T_out"], b + 1)
                    for g in range(UB):
                        n = transpose(bank[5 + b % 2][:, col(g)], o_headsT[:, g, :])
                    n.then_inc(sem["heads_back"], 1)
                if 3 <= s < UNITS + 3:
                    u = s - 3
                    b, g = divmod(u, UB)
                    pe.wait_ge(sem["probs_T_out"], u + 1)
                    pe.wait_ge(sem["vals_made"], b + 1)
                    if g == 0 and b >= 2:
                        pe.wait_ge(sem["o_normed"], b - 1)
                    for h in range(HG):
                        n = mm(bank[5 + b % 2][32 * h:32 * h + 32, col(g)], vals[b % 2][:, HG * g + h, :],
                               probsT[u % 2][:, h, :], start=True, stop=True)
                    n.then_inc(sem["heads_out"], 1)
                b = chain_row(s, 2 * UB)
                if b is not None:
                    pe.wait_ge(sem["o_T_out"], b + 1)
                    pe.wait_ge(sem["wout_scaled"], 1)
                    mm(bank[7][:, col(1)], oT[:], w_t[:, WO, :], start=True, stop=True).then_inc(sem["projected"], 1)
                b = chain_row(s, 2 * UB + 2)
                if b is not None:
                    pe.wait_ge(sem["xn2_T_out"], b + 1)
                    mm(bank[7][:, col(1)], w_t[:, GW1, :], xnT[:, b, :], start=True, stop=True).then_inc(sem["gate_hidden"], 1)

                run_groups(s)

            pe.wait_ge(sem["gate_summed"], B)
            mm(bank[2][0:E0, 0:B], gate2T[:], h_sum[:], start=True, stop=True).then_inc(sem["gate_out"], 1)
            run_groups(END)
            pe.wait_ge(sem["g_made"], 1)
            mm(bank[2][:, 16:16 + B], spread[:], gT[:], start=True, stop=True).then_inc(sem["g_spread"], 1)
            for f in range(FC):
                n = mm(bank[7][:, f * B:(f + 1) * B], tb1[:, col(f)], gT[:], start=True, stop=True)
            n.then_inc(sem["g_spread"], 1)
            run_groups(END + 1)
            pe.wait_ge(sem["g_mixed"], 1)
            pe.wait_ge(sem["tw1_loaded"], 16 * E0)
            pe.wait_ge(sem["tw2_loaded"], 16 * E0)

            def mix(m):
                if m >= 4:
                    pe.wait_ge(sem["mixed_out"], m - 3)
                for j in range(4):
                    f, h = divmod(m - 8, 2)
                    w = tw1[:, 4 * m + j, :] if m < 8 else tw2[:, 4 * h + j, col(f)]
                    n = mm(bank[3 + m % 4][:, col(j)], w, g_mix[:], start=True, stop=True)
                n.then_inc(sem["mixed"], 1)

            for m in range(10):
                mix(m)
            pe.wait_ge(*pre_emptied("w", 5))
            pe.wait_ge(sem["mixed_out"], 8)
            for b in range(B):
                if b >= 2:
                    pe.wait_ge(sem["gelu_made"], b - 1)
                for f in range(FC):
                    n = mm(bank[b % 2][:, col(f)], mW1T[:, b, :, :].rearrange("p q r -> p (q r)")[:, col(f)],
                           xnT[:, b, :], start=True, stop=True)
                n.then_inc(sem["hidden"], 1)
                if b < B - 2:
                    mix(10 + b)
            pe.wait_ge(sem["mixed_out"], 16)
            pe.wait_ge(sem["pad_made"], 1)
            pe.wait_ge(sem["vh_scaled"], 1)
            pe.wait_ge(sem["g_rows_made"], 1)

            def shared_part(w, h, at):
                mm(bank[at][:], w_t[:, w, :], xnT[:, 4 * h:4 * h + 4, :], start=True, stop=True
                   ).then_inc(sem["shared_hidden"], 1)

            for s in range(B + 8):
                if s < B:
                    pe.wait_ge(sem["gelu_made"], B - 1 + s if s < 2 else s + 1)
                    if s >= 2:
                        pe.wait_ge(sem["x2_made"], s - 1)
                    o = bank[s % 2][:, 0:P]
                    for f in range(FC):
                        mm(o, uT[:, s, f, :], mW2T[:, s, f, :, :].rearrange("p q r -> p (q r)"), start=(f == 0), stop=False)
                    mm(o, g_rows[:, s, :], tb2[:], start=False, stop=True).then_inc(sem["ffn_out"], 1)
                if 8 <= s:
                    b = s - 8
                    pe.wait_ge(sem["xn4_T_out"], b + 1)
                    n = mm(bank[7][:, P + b * E1:P + (b + 1) * E1], xnT[:, b, :], routerT[:], start=True, stop=True)
                    if b == B - 1:
                        n.then_inc(sem["logits"], 1)
                if 4 <= s < B + 4:
                    b = s - 4
                    pe.wait_ge(sem["probs1"], b + 1)
                    if b >= 1:
                        pe.wait_ge(sem["x3_made"], b)
                    transpose(bank[6][:, 0:P], p1[:, b, :]).then_inc(sem["probs1_T"], 1)
                if 2 <= s < B + 2:
                    b = s - 2
                    pe.wait_ge(sem["xn3_made"], b + 1)
                    if b >= 2:
                        pe.wait_ge(sem["q_out"], b - 1)
                    transpose(bank[2 + b % 2][:, 0:P], xn[:, b, :]).then_inc(sem["xn3_T"], 1)
                if 3 <= s < B + 3:
                    b = s - 3
                    pe.wait_ge(sem["q_out"], b + 1)
                    if b >= 2:
                        pe.wait_ge(sem["probs1"], b - 1)
                    o = bank[4 + b % 2][:, 0:P]
                    mm(o, q1T[b % 2][:], kT[:, b, :], start=True, stop=False)
                    mm(o, ident_b[:], pad_b[:, b, :], start=False, stop=True).then_inc(sem["scores1"], 1)
                if 7 <= s < B + 7:
                    b = s - 7
                    pe.wait_ge(sem["xn4_made"], b + 1)
                    transpose(bank[7][:, 0:P], xn[:, b, :]).then_inc(sem["xn4_T"], 1)
                if 4 <= s < B + 4:
                    b = s - 4
                    pe.wait_ge(sem["probs1_T_out"], b + 1)
                    mm(bank[6][:, col(1)], p1T[b % 2][:], vh[:, b, :], start=True, stop=True).then_inc(sem["attn1"], 1)
                if 2 <= s < B + 2:
                    b = s - 2
                    pe.wait_ge(sem["xn3_T_out"], b + 1)
                    mm(bank[2 + b % 2][:, col(1)], w_t[:, WQ, :], xnT[:, b, :], start=True, stop=True
                       ).then_inc(sem["q_ready"], 1)
                if s == B + 4:
                    pe.wait_ge(sem["x2_made"], B)
                    shared_part(WG, 0, 0)
                if s == B + 6:
                    shared_part(WU, 0, 1)

            def shared(i):
                f, h, gate_bank, up_bank = SHARED[i]
                for w, at in ((WG, gate_bank), (WU, up_bank)):
                    shared_part(w + f, h, at)

            pe.wait_ge(sem["q_out"], B)
            shared_part(WG + 1, 0, 2)
            pe.wait_ge(sem["one_hot_made"], 1)
            pe.wait_ge(sem["consts_bf16"], 3)
            mm(bank[6][:, P:P + B * E1], before[:], one_hot_b[:], start=True, stop=False, skip_group_check=True)
            for b in range(B - 1):
                mm(bank[6][:, P + (b + 1) * E1:P + B * E1], ones_b[:],
                   one_hot_b[:, b:b + 1, :].to_broadcast([P, B - 1 - b, E1]), start=False, stop=(b == B - 2),
                   skip_group_check=True)
            for b in range(B):
                n = mm(bank[6][:, 256:256 + E1], ones_b[:], one_hot_b[:, b, :], start=False, stop=(b == B - 1),
                       skip_group_check=True)
            n.then_inc(sem["ranks"], 1)

            def shared_down(h):
                for b in range(4 * h, 4 * h + 4):
                    for f in range(C1):
                        n = mm(bank[(7, 3)[h]][:, col(b % 4)], sharedT[:, f, b, :], w_t[:, WD + f, :],
                               start=(f == 0), stop=(f == C1 - 1))
                n.then_inc(sem["shared_out"], 1)

            shared_part(WU + 1, 0, 3)
            shared(2)
            pe.wait_ge(sem["shared_act"], 2)
            shared_down(0)
            shared(3)
            pe.wait_ge(sem["shared_act"], 4)
            shared_down(1)

            pe.wait_ge(sem["experts_loaded"], 32)
            pe.wait_ge(sem["acc_made"], 2)
            pe.wait_ge(sem["tiles_made"], 1)
            inner = pe.value_load(inner_i[0:1, 0:1], min_val=MIN_PAIRS - 1, max_val=TILES // 2 - 1)

            def experts_of(t, n):
                _, e = nc.values_load_multi_w_load_instructions(
                    tile_expert[0:1, bass.ds(t, n)], engines=(mybir.EngineType.PE,), min_val=0, max_val=E1 - 1,
                    skip_runtime_bounds_check_because="a count, and clamped to the last expert where it is computed")
                return e

            def tile_transpose(k, t):
                pe.wait_ge(sem["tile_copied"], t + 1)
                transpose(bank[k % 2][:, 0:P], xs_in[k % 2][:]).then_inc(sem["tile_T"], 1)

            def tile_hidden(k, t, e):
                pe.wait_ge(sem["tile_T_out"], t + 1)
                mm(bank[2 + k % 2][:], xs_T[k % 2], gate_up[:, bass.ds(e, 1), :].rearrange("p a f -> p (a f)"),
                   start=True, stop=True).then_inc(sem["tile_hidden"], 1)

            def act_transpose(k, t):
                pe.wait_ge(sem["tile_act"], t + 1)
                for f in range(C1):
                    n = transpose(bank[4 + k % 2][:, col(f)], act_r[k % 2][:, col(f)])
                n.then_inc(sem["act_T_ready"], 1)

            def tile_down(k, t, e, first=False):
                pe.wait_ge(sem["act_T_out"], t + 1)
                if not first:
                    pe.wait_ge(sem["y_ready"], 2 * t)
                for f in range(C1):
                    n = mm(bank[6 + k % 2][:, 0:P], act_T[k % 2][:, f, :],
                           down[:, bass.ds(e, 1), f, :].rearrange("p a h -> p (a h)"), start=(f == 0), stop=(f == C1 - 1))
                n.then_inc(sem["tile_y"], 1)

            e = experts_of(0, 3)
            tile_transpose(0, 0)
            tile_transpose(1, 1)
            tile_hidden(0, 0, e[0])
            tile_transpose(2, 2)
            tile_hidden(1, 1, e[1])
            tile_transpose(3, 3)
            act_transpose(0, 0)
            tile_hidden(0, 2, e[2])

            def pair(i, first=False, last=False):
                e = experts_of(2 * i, 3 if last else 5)
                for k in (0, 1):
                    t = 2 * i + k
                    tile_down(k, t, e[k], first and k == 0)
                    if not last:
                        tile_transpose(k + 4, t + 4)
                    act_transpose(k + 1, t + 1)
                    if not last:
                        tile_hidden(k + 3, t + 3, e[k + 3])
                if last:
                    tile_down(0, t + 1, e[2])

            pair(0, first=True)
            with pe.Fori(1, inner) as i:
                pair(i)
            pair(inner, last=True)


_INS = ['x', 'ctx_1024', 'mask_Bx1xSxS2_ik1', 'mask_BxS2_if1', 'g_xattn', 'g_ffn', 'L0_xattn_w_out', 'L0_xattn_b_out',
        'L0_ffn_gate_w1', 'L0_ffn_gate_b1', 'L0_ffn_gate_w2', 'L0_ffn_gate_b2', 'L0_ffn_W1', 'L0_ffn_b1', 'L0_ffn_W2',
        'L0_ffn_b2', 'L0_ffn_TW1', 'L0_ffn_Tb1', 'L0_ffn_TW2', 'L0_ffn_Tb2', 'L1_xattn_Wq_w', 'L1_xattn_Wq_b',
        'L1_xattn_Wk_w', 'L1_xattn_Wk_b', 'L1_xattn_Wv_w', 'L1_xattn_Wv_b', 'L1_ffn_w_router', 'L1_ffn_gate_up_proj',
        'L1_ffn_down_proj', 'L1_ffn_w_gate', 'L1_ffn_w_up', 'L1_ffn_w_down']


def kernel(**inputs):
    import numpy as _np
    import concourse.bacc as _bacc
    from concourse import mybir as _mybir
    from concourse.bass_utils import run_bass_kernel_spmd as _run

    nc = _bacc.Bacc("TRN2", target_bir_lowering=False, num_devices=1)
    arrays, args = {}, {}
    for name in _INS:
        arr = _np.ascontiguousarray(inputs[name])
        arrays[f"in_{name}"] = arr
        args[name] = nc.dram_tensor(f"in_{name}", arr.shape, _mybir.dt.from_np(arr.dtype), kind="ExternalInput").ap()
    out = nc.dram_tensor("out_x", inputs["x"].shape, _mybir.dt.float32, kind="ExternalOutput").ap()
    flamingo_gated_blocks(nc, args, out)
    r = _run(nc, [arrays], core_ids=[0])
    return r.results[0]["out_x"]
```

```python
from contextlib import ExitStack

import concourse.bass as bass
from concourse import mybir

ALU = mybir.AluOpType
ACT = mybir.ActivationFunctionType
F32 = mybir.dt.float32
BF16 = mybir.dt.bfloat16
I32 = mybir.dt.int32
U32 = mybir.dt.uint32
X = mybir.AxisListType.X

P = 128
MASKED_L0 = -1.0e22
MASKED_L1 = -1.0e30
EPS = 1e-5
LN_EXP_SET = "natural_log_exp_and_others"
NO_TOKEN = 1 << 20


def flamingo_gated_blocks(nc, a, out):
    B, S, D = a["x"].shape
    HEADS = 16
    HD = D // HEADS
    E0, F0, _ = a["L0_ffn_TW1"].shape
    FC = F0 // P
    RO = P // E0
    E1, _, F1X2 = a["L1_ffn_gate_up_proj"].shape
    F1 = F1X2 // 2
    C1 = F1 // P
    assert S == P and D == P and B == 8 and HD * HEADS == D
    SCALE = float(D) ** -0.5
    HG = 4
    UB = HEADS // HG
    UNITS = UB * B
    TILES = B * S // P + E1 - 1
    MAX_INNER = (TILES - 2) // 4
    MIN_INNER = 2
    LOADED = 4 * MAX_INNER + 5
    ROW = D + 1
    RECORD = ROW + D

    ctx = ExitStack()
    with ctx:
        def sb(name, shape, dt=F32):
            return ctx.enter_context(nc.sbuf_tensor(name, shape, dt))

        bank = [ctx.enter_context(nc.psum_tensor(f"bank{i}", [P, 512], F32)) for i in range(8)]
        sorted_rows = nc.dram_tensor("sorted_rows", (LOADED * P, RECORD), F32, kind="Internal").ap()

        x = sb("x", [P, B, D])
        c = sb("c", [P, B, D])
        early = sb("early", [P, 35, P])
        mask_i = early[:, 0:8, :].bitcast(I32)
        pad_i = early[:, 8:16, :].bitcast(I32)
        w_raw = early[:, 16:35, :]
        mW2T = early[:, 0:32, :].rearrange("p (b c) (q r) -> p b c q r", b=B, r=RO)
        w_t = sb("w_t", [P, 19, P])
        WO, GW1, WK, WV, W1, W2, WQ, WG, WU, WD = 0, 1, 2, 3, 4, 8, 12, 13, 15, 17
        w_small = sb("w_small", [P, 2, P])
        gate2T = sb("gate2T", [P, E0])
        routerT = sb("routerT", [P, E1])
        b_out = sb("b_out", [P, D])
        b_v = sb("b_v", [P, D])
        gates = sb("gates", [P, 4])
        tgate = sb("tgate", [P, 4])
        b_g1 = sb("b_g1", [P, 1])
        b_q = sb("b_q", [P, 1])
        b_k = sb("b_k", [P, 1])
        b_1 = sb("b_1", [P, FC])
        b_g2 = sb("b_g2", [E0, 1])
        tb1 = sb("tb1", [E0, F0])
        tb2 = sb("tb2", [E0 + 1, D])
        tw1 = sb("tw1", [P, F0 // RO, D])
        tw2 = sb("tw2", [P, D // RO, F0])
        gate_up = sb("gate_up", [P, E1, 2 * F1])
        down = sb("down", [P, E1, C1, D])

        ident = sb("ident", [P, P])
        ident_b = sb("ident_b", [P, P], BF16)
        before = sb("before", [P, P], BF16)
        ones_b = sb("ones_b", [P, P], BF16)
        head_of = sb("head_of", [P, HEADS])
        same_row = sb("same_row", [P, RO])
        spread = sb("spread", [E0, P])
        eps = sb("eps", [P, 1])
        empty_row = sb("empty_row", [P, RECORD])
        expert_no = sb("expert_no", [P, E1])
        expert_low = sb("expert_low", [P, E1])
        tile_no = sb("tile_no", [P, LOADED])
        lower = sb("lower", [P, E1, E1])

        mask_b = sb("mask_b", [P, B, P], BF16)
        pad_f = sb("pad_f", [P, B, P], BF16)
        pad_b = sb("pad_b", [P, B, P], BF16)
        cT = sb("cT", [P, B, P])
        kT = sb("kT", [P, B, P])
        vh = sb("vh", [P, B, D])
        xn = sb("xn", [P, B, D])
        xnT = sb("xnT", [P, B, P])
        keys2 = sb("keys2", [P, 2 * HEADS, P])
        keys = [keys2[:, HEADS * i:HEADS * (i + 1), :] for i in range(2)]
        mW1T = keys2[:, :, :].rearrange("p (b c) (q r) -> p b (c q) r", b=B, r=RO)
        vals = [sb(f"vals{i}", [P, HEADS, 32]) for i in range(2)]
        probs = [sb(f"probs{i}", [P, HG, P]) for i in range(3)]
        probsT = [sb(f"probsT{i}", [P, HG, P]) for i in range(2)]
        neg_max = sb("neg_max", [P, UNITS, HG])
        rden = sb("rden", [P, B, HEADS])
        o_headsT = sb("o_headsT", [P, UB, P])
        o_rows = [sb(f"o_rows{i}", [P, HEADS, HD]) for i in range(2)]
        oT = sb("oT", [P, P])
        stats = sb("stats", [P, B, 6])
        mv = sb("mv", [P, 4, B, 2])
        var_ln = sb("var_ln", [P, B])
        rstd = sb("rstd", [P, 4, B])

        relu_out = sb("relu_out", [P, P])
        h_sum = sb("h_sum", [P, B])
        gT = sb("gT", [E0, B])
        g_rows = sb("g_rows", [E0 + 1, B, P])
        g_col = sb("g_col", [P, B])
        g_mix = sb("g_mix", [P, B, RO])
        mb1 = sb("mb1", [P, FC, B])
        uT = tw1[:, :, :].rearrange("p (b c) t -> p b c t", b=B)


        q1T = [sb(f"q1T{i}", [P, P]) for i in range(2)]
        p1 = c
        p1T = [sb(f"p1T{i}", [P, P]) for i in range(2)]
        neg_max1 = sb("neg_max1", [P, B])
        den1 = sb("den1", [P, B])
        rden1 = sb("rden1", [P, B])

        logit_max = sb("logit_max", [P, B])
        score = sb("score", [P, B])
        tmp_be = sb("tmp_be", [P, B, E1])
        choice = sb("choice", [P, B])
        one_hot = sb("one_hot", [P, B, E1])
        one_hot_b = sb("one_hot_b", [P, B, E1], BF16)
        tiles_i = sb("tiles_i", [P, E1], I32)
        tmp_ee = sb("tmp_ee", [P, E1, E1])
        first = sb("first", [P, E1])
        end_tile = sb("end_tile", [P, E1])
        tmp_te = sb("tmp_te", [P, LOADED, E1])
        tile_expert_f = sb("tile_expert_f", [P, LOADED])
        tile_expert = sb("tile_expert", [P, LOADED], I32)
        inner_i = sb("inner_i", [P, 1], I32)
        slot_i = sb("slot_i", [P, B], I32)
        x_rows = sb("x_rows", [P, B, RECORD])

        sharedT = tw1[:, 0:C1 * B, :].rearrange("p (c b) t -> p c b t", b=B)
        silu_sh = [tw1[:, 16 + 4 * i:20 + 4 * i, :].rearrange("p c t -> p (c t)") for i in range(4)]
        tail = tw2[:, :, :].rearrange("p q (c t) -> p (q c) t", t=P)
        xs_T = [tail[:, i, :] for i in range(2)]
        silu_g = [tail[:, 2 + 2 * i:4 + 2 * i, :].rearrange("p c t -> p (c t)") for i in range(2)]
        act_T = [tail[:, 6 + 2 * i:8 + 2 * i, :] for i in range(2)]
        y_out = [tail[:, 10 + i, :] for i in range(4)]
        w_tile = [tail[:, 14 + 4 * i:18 + 4 * i, :] for i in range(2)]
        sorted_in = early[:, :, :].rearrange("p c t -> p (c t)")[:, 0:LOADED * ROW].rearrange("p (t r) -> p t r", r=ROW)
        LOADS = [(0, 2), (2, 5), (5, LOADED)]
        acc_in = keys2
        ACC_LOADS = [(0, 2), (2, 6), (6, LOADED)]
        OUT_BANKS = (7, 2, 3, 6)
        SHARED = [(0, 0, 0, 1), (1, 0, 2, 3), (0, 1, 4, 5), (1, 1, 0, 1)]
        xs_in = [sb(f"xs_in{i}", [P, D]) for i in range(2)]
        token_of = [sb(f"token_of{i}", [P, 1], I32) for i in range(4)]

        names = """gates_loaded x_loaded0 x_loaded1 c_loaded0 c_loaded1 mask_loaded0 mask_loaded1 w_loaded small_loaded tw1_loaded tw2_loaded experts_loaded
            vector_step scalar_step pool_step
            ident_made consts_bf16 consts_made eps_made empty_made heads_made tanh_made
            bq_scaled wout_scaled x_plus_bout vh_scaled pad_copied pad_made mask_made
            var_ready rstd_ready xn_written
            pre_ready pre_out_v pre_out_s keys_made vals_made
            scores max_made probs_made probs_T probs_T_out heads_out heads_T_out heads_back o_normed o_T o_T_out
            projected x1_made xn2_made xn2_T xn2_T_out gate_hidden gate_summed
            gate_out g_made g_spread g_mixed mb1_made g_rows_made mixed mixed_out hidden gelu_made ffn_out x2_made
            var3_ready rstd3_ready xn3_made xn3_T xn3_T_out q_ready q_out scores1 max1_made probs1 rden1_made probs1_T probs1_T_out
            attn1 x3_made var4_ready rstd4_ready xn4_made xn4_T xn4_T_out
            logits logit_max_made exp_made score_made one_hot_made ranks slots_made tiles_made rows_scaled rows_filled rows_sorted
            acc_loaded0 acc_loaded1 acc_loaded2
            shared_hidden shared_silu shared_act shared_out acc_made
            tiles_loaded0 tiles_loaded1 tiles_loaded2 tile_copied w_copied tile_T tile_T_out tile_gate tile_up tile_silu tile_act
            tile_y y_ready last_scattered fours_scattered scatter_begun y_scattered0 y_scattered1 y_scattered2 y_scattered3""".split()
        sem = {n: ctx.enter_context(nc.semaphore(n)) for n in names}
        y_scattered = [sem[f"y_scattered{i}"] for i in range(4)]

        block = ctx.enter_context(nc.Block())

        def as_row(v):
            return v.rearrange("(a d) -> a d", a=1)

        def as_col(v):
            return v.rearrange("(d a) -> d a", a=1)

        def in_bank(i, n=4):
            return bank[i][:, 0:n * P].rearrange("p (b t) -> p b t", t=P)

        END = UNITS + 9
        GROUPS = [(-1, "cT", 0, 0, "s"), (-1, "cT", 1, 2, "s"), (-1, "xn", 0, 1, "v"),
                  (2, "w", 0, 7, "s"), (4, "xn", 1, 7, "v"),
                  (UNITS + 1, "small", 0, 0, "v"), (UNITS + 1, "w", 1, 1, "s"), (UNITS + 2, "w", 2, 3, "s"),
                  (UNITS + 3, "k", 0, 0, "s"), (UNITS + 4, "k", 1, 1, "v"), (UNITS + 4, "w", 3, 4, "s"),
                  (UNITS + 5, "v", 0, 0, "v"), (UNITS + 6, "v", 1, 1, "v"),
                  (END, "w", 4, 0, "s"), (END + 1, "w", 5, 1, "s")]
        W_GROUPS = [(0, 2), (2, 4), (4, 8), (8, 12), (12, 16), (16, 19)]

        def group(what, j):
            return [g[1:3] for g in GROUPS].index((what, j))

        def pre_emptied(what, j):
            n = group(what, j)
            e = GROUPS[n][4]
            return sem["pre_out_" + e], sum(g[4] == e for g in GROUPS[:n + 1])

        def groups_at(s, engine=None):
            return [(n, *g[1:]) for n, g in enumerate(GROUPS) if g[0] == s and engine in (None, g[4])]

        def chain_row(step, offset):
            b, r = divmod(step - offset, UB)
            return b if r == 0 and 0 <= b < B else None

        STEPS = END

        @block.sync
        def _(sp):
            def load(dst, src, s, **kw):
                sp.dma_start(dst, src, **kw).then_inc(sem[s], 16)

            for h in range(2):
                rows = slice(4 * h, 4 * h + 4)
                load(x[:, rows, :], a["x"][rows].rearrange("b s d -> s b d"), f"x_loaded{h}")
                if h == 0:
                    load(c[:, 4:8, :], a["ctx_1024"][4:8].rearrange("b s d -> s b d"), "c_loaded1")
                load(mask_i[:, rows, :], a["mask_Bx1xSxS2_ik1"][rows].rearrange("b o s k -> s (b o) k"),
                     f"mask_loaded{h}")
            for slot, name in ((WO, "L0_xattn_w_out"), (GW1, "L0_ffn_gate_w1"), (WK, "L1_xattn_Wk_w"),
                               (WV, "L1_xattn_Wv_w"), (WQ, "L1_xattn_Wq_w")):
                load(w_raw[:, slot, :], a[name], "w_loaded")
            for slot, name, n in ((W1, "L0_ffn_W1", FC), (WG, "L1_ffn_w_gate", C1), (WU, "L1_ffn_w_up", C1)):
                load(w_raw[:, slot:slot + n, :], a[name].rearrange("(c f) h -> f c h", c=n), "w_loaded")
            load(w_raw[:, W2:W2 + FC, :], a["L0_ffn_W2"].rearrange("h (c f) -> h c f", c=FC), "w_loaded")
            load(w_raw[:, WD:WD + C1, :], a["L1_ffn_w_down"].rearrange("h (c f) -> h c f", c=C1), "w_loaded")
            load(w_small[0:E0, 0, :], a["L0_ffn_gate_w2"], "w_loaded")
            load(w_small[0:E1, 1, :], a["L1_ffn_w_router"], "w_loaded")
            load(b_out[:], as_row(a["L0_xattn_b_out"]).partition_broadcast(P), "small_loaded")
            load(b_v[:], as_row(a["L1_xattn_Wv_b"]).partition_broadcast(P), "small_loaded")
            for dst, name in ((b_g1, "L0_ffn_gate_b1"), (b_q, "L1_xattn_Wq_b"), (b_k, "L1_xattn_Wk_b"),
                              (b_g2, "L0_ffn_gate_b2")):
                load(dst[:], as_col(a[name]), "small_loaded")
            load(b_1[:], a["L0_ffn_b1"].rearrange("(c f) -> f c", c=FC), "small_loaded", allow_slow_non_contiguous=True)
            load(tb1[:], a["L0_ffn_Tb1"], "small_loaded")
            load(tb2[0:E0, :], a["L0_ffn_Tb2"], "small_loaded")
            load(tb2[E0:E0 + 1, :], as_row(a["L0_ffn_b2"]), "small_loaded")
            load(pad_i, a["mask_BxS2_if1"].rearrange("(o b) k -> o b k", o=1).partition_broadcast(P), "small_loaded")
            for e in range(E0):
                load(tw1[RO * e:RO * e + RO, :, :], a["L0_ffn_TW1"][e].rearrange("(q r) h -> r q h", r=RO), "tw1_loaded")
            for e in range(E0):
                load(tw2[RO * e:RO * e + RO, :, :], a["L0_ffn_TW2"][e].rearrange("(q r) f -> r q f", r=RO), "tw2_loaded")
            load(gate_up[:], a["L1_ffn_gate_up_proj"].rearrange("e h f -> h e f"), "experts_loaded")
            load(down[:], a["L1_ffn_down_proj"].rearrange("e (c f) h -> f e c h", c=C1), "experts_loaded")
            sp.wait_ge(sem["empty_made"], 3)
            load(sorted_rows.rearrange("(t p) r -> p t r", p=P),
                 empty_row[:, :].unsqueeze(1).to_broadcast([P, LOADED, RECORD]), "rows_filled")
            sp.wait_ge(sem["rows_sorted"], 16 * B)
            for i in range(len(LOADS)):
                lo, hi = LOADS[i]
                load(sorted_in[:, lo:hi, :], sorted_rows[lo * P:hi * P, 0:ROW].rearrange("(t p) r -> p t r", p=P),
                     f"tiles_loaded{i}")
                lo, hi = ACC_LOADS[i]
                load(acc_in[:, lo:hi, :], sorted_rows[lo * P:hi * P, ROW:RECORD].rearrange("(t p) d -> p t d", p=P),
                     f"acc_loaded{i}")
            sp.wait_ge(sem["tiles_made"], 1)
            inner = sp.value_load(inner_i[0:1, 0:1], min_val=MIN_INNER, max_val=MAX_INNER)
            for slot in y_scattered:
                sp.wait_ge(slot, 16 * inner + 16)
            sp.sem_inc(sem["fours_scattered"], 1)
            sp.wait_ge(sem["last_scattered"], 16)

        @block.gpsimd
        def _(pool):
            steps = [0]

            def step(i):
                steps[0] += 1
                i.then_inc(sem["pool_step"], 1)
                pool.wait_ge(sem["pool_step"], steps[0])

            pool.memset(eps[:], EPS).then_inc(sem["eps_made"], 1)
            step(pool.memset(ident[:], 0.0))
            pool.affine_select(out=ident[:], in_=ident[:], compare_op=ALU.not_equal, fill=1.0, base=0,
                               pattern=[[-1, P]], channel_multiplier=1).then_inc(sem["ident_made"], 1)
            pool.wait_ge(sem["ident_made"], 1)
            pool.tensor_copy(ident_b[:], ident[:]).then_inc(sem["consts_bf16"], 1)
            pool.memset(vals[0][:], 0.0).then_inc(sem["pool_step"], 1)
            step(pool.memset(vals[1][:], 0.0))
            steps[0] += 1
            pool.wait_ge(sem["pool_step"], steps[0])
            for i in range(2):
                pool.memset(vals[i][:, :, HD:HD + 1], 1.0).then_inc(sem["consts_made"], 1)

            def make_vals(b):
                if b >= 2:
                    pool.wait_ge(sem["heads_out"], UB * (b - 1))
                pool.tensor_copy(vals[b % 2][:, :, 0:HD], c[:, b, :].rearrange("p (h d) -> p h d", d=HD)
                                 ).then_inc(sem["vals_made"], 1)

            def make_keys(b):
                pool.wait_ge(*pre_emptied("cT", b // 4))
                if b >= 2:
                    pool.wait_ge(sem["scores"], UB * (b - 1))
                n = HG if b == 0 else HEADS
                for h in range(0, HEADS, n):
                    pool.tensor_tensor(keys[b % 2][:, h:h + n, :], cT[:, b:b + 1, :].to_broadcast([P, n, P]),
                                       head_of[:, h:h + n].unsqueeze(2).to_broadcast([P, n, P]), ALU.mult
                                       ).then_inc(sem["keys_made"], 1)

            pool.wait_ge(sem["heads_made"], 1)
            make_keys(0)
            pool.wait_ge(sem["c_loaded0"], 16)
            make_vals(0)
            make_keys(1)
            make_vals(1)
            make_keys(2)
            pool.wait_ge(sem["tanh_made"], 1)
            pool.wait_ge(*pre_emptied("w", 0))
            pool.tensor_scalar(w_t[:, WO, :], w_t[:, WO, :], tgate[:, 0:1], None, ALU.mult).then_inc(sem["wout_scaled"], 1)
            pool.wait_ge(sem["small_loaded"], 11 * 16)
            step(pool.tensor_scalar(b_out[:], b_out[:], tgate[:, 0:1], None, ALU.mult))
            pool.tensor_scalar(b_q[:], b_q[:], SCALE, None, ALU.mult).then_inc(sem["bq_scaled"], 1)
            pool.wait_ge(sem["xn_written"], B)
            pool.tensor_tensor(x[:], x[:], b_out[:, :].unsqueeze(1).to_broadcast([P, B, D]), ALU.add
                               ).then_inc(sem["x_plus_bout"], 1)
            make_vals(2)
            pool.memset(g_rows[:], 1.0).then_inc(sem["consts_made"], 1)
            pool.memset(ones_b[:], 1.0).then_inc(sem["consts_bf16"], 1)
            step(pool.memset(before[:], 1.0))
            pool.affine_select(out=before[:], in_=before[:], compare_op=ALU.is_gt, fill=0.0, base=0,
                               pattern=[[1, P]], channel_multiplier=-1).then_inc(sem["consts_bf16"], 1)
            make_keys(3)
            make_vals(3)
            step(pool.memset(lower[:], 1.0))
            pool.affine_select(out=lower[:], in_=lower[:], compare_op=ALU.is_gt, fill=0.0, base=0,
                               pattern=[[1, E1], [-1, E1]], channel_multiplier=0).then_inc(sem["consts_made"], 1)
            pool.iota(expert_no[:], [[1, E1]], base=0, channel_multiplier=0,
                      allow_small_or_imprecise_dtypes=True).then_inc(sem["consts_made"], 1)
            pool.iota(expert_low[:], [[1, E1]], base=-E1, channel_multiplier=0,
                      allow_small_or_imprecise_dtypes=True).then_inc(sem["consts_made"], 1)
            pool.iota(tile_no[:], [[1, LOADED]], base=0, channel_multiplier=0,
                      allow_small_or_imprecise_dtypes=True).then_inc(sem["consts_made"], 1)
            pool.wait_ge(sem["pad_copied"], 1)
            pool.affine_select(out=pad_b[:], in_=pad_f[:], compare_op=ALU.is_ge, fill=MASKED_L1, base=0,
                               pattern=[[0, B], [-1, P]], channel_multiplier=1).then_inc(sem["pad_made"], 1)
            make_keys(4)
            pool.wait_ge(sem["c_loaded1"], 16)
            make_vals(4)
            pool.memset(empty_row[:, 0:D], 0.0).then_inc(sem["empty_made"], 1)
            pool.memset(empty_row[:, ROW:RECORD], 0.0).then_inc(sem["empty_made"], 1)
            pool.iota(empty_row[:, D:ROW].bitcast(I32), [[0, 1]], base=NO_TOKEN, channel_multiplier=0
                      ).then_inc(sem["empty_made"], 1)
            pool.iota(x_rows[:, :, D:ROW].bitcast(I32), [[P, B], [0, 1]], base=0, channel_multiplier=1
                      ).then_inc(sem["consts_made"], 1)
            for b in range(5, B):
                make_keys(b)
                make_vals(b)
            pool.wait_ge(*pre_emptied("v", 1))
            pool.tensor_scalar(vh[:], vh[:], tgate[:, 1:2], None, ALU.mult).then_inc(sem["vh_scaled"], 1)
            pool.wait_ge(sem["g_made"], 1)
            pool.wait_ge(sem["consts_made"], 3)
            pool.tensor_copy(g_rows[0:E0, :, :], gT[:, :].unsqueeze(2).to_broadcast([E0, B, P])
                             ).then_inc(sem["g_rows_made"], 1)
            pool.wait_ge(sem["slots_made"], 1)
            pool.wait_ge(sem["rows_filled"], 16)
            for b in range(B):
                pool.wait_ge(sem["rows_scaled"], b + 1)
                pool.wait_ge(sem["acc_made"], b + 1)
                pool.indirect_dma_start(
                    out=sorted_rows, in_=x_rows[:, b, :], in_offset=None,
                    out_offset=bass.IndirectOffsetOnAxis(ap=slot_i[:, b:b + 1].bitcast(U32), axis=0)
                ).then_inc(sem["rows_sorted"], 16)
            pool.wait_ge(sem["tiles_made"], 1)
            inner = pool.value_load(inner_i[0:1, 0:1], min_val=MIN_INNER, max_val=MAX_INNER)

            def scatter_rows(k, t, done=None):
                pool.wait_ge(sem["y_ready"], 2 * t + 2)
                pool.sem_inc(sem["scatter_begun"], 1)
                pool.indirect_dma_start(
                    out=out.rearrange("b s d -> (b s) d"), in_=y_out[k], in_offset=None, bounds_check=B * S - 1,
                    oob_is_err=False,
                    out_offset=bass.IndirectOffsetOnAxis(ap=token_of[k][:, 0:1].bitcast(U32), axis=0)
                ).then_inc(done or y_scattered[k], 16)

            for k in range(4):
                scatter_rows(k, k)
            with pool.Fori(1, inner + 1) as i:
                for k in range(4):
                    scatter_rows(k, 4 * i + k)
            scatter_rows(0, 4 * inner + 4, sem["last_scattered"])

        @block.scalar
        def _(act):
            A = nc.scalar.activation
            steps = [0]

            def step(i):
                steps[0] += 1
                i.then_inc(sem["scalar_step"], 1)
                act.wait_ge(sem["scalar_step"], steps[0])

            def inv_std(n, rows, done):
                step(A(var_ln[:, rows], mv[:, n, rows, 1], ACT.Ln, bias=eps[:, 0:1]))
                A(rstd[:, n, rows], var_ln[:, rows], ACT.Exp, scale=-0.5).then_inc(sem[done], 1)

            act.dma_start(gates[:, 0:2], as_row(a["g_xattn"]).partition_broadcast(P)).then_inc(sem["gates_loaded"], 16)
            act.dma_start(gates[:, 2:4], as_row(a["g_ffn"]).partition_broadcast(P)).then_inc(sem["gates_loaded"], 16)
            act.dma_start(c[:, 0:4, :], a["ctx_1024"][0:4].rearrange("b s d -> s b d")).then_inc(sem["c_loaded0"], 16)
            act.wait_ge(sem["gates_loaded"], 32)
            A(tgate[:], gates[:], ACT.Tanh).then_inc(sem["tanh_made"], 1)
            nc.scalar.preload_act_table_set(LN_EXP_SET)

            def empty_groups(s):
                for n, what, j, at, e in groups_at(s, "s"):
                    act.wait_ge(sem["pre_ready"], n + 1)
                    if what == "k":
                        act.wait_ge(sem["small_loaded"], 11 * 16)
                        i = A(kT[:, 4 * j:4 * j + 4, :], in_bank(at), ACT.Identity, bias=b_k[:, 0:1])
                    elif what == "cT":
                        i = A(cT[:, 4 * j:4 * j + 4, :], in_bank(at), ACT.Copy)
                    else:
                        lo, hi = W_GROUPS[j]
                        i = A(w_t[:, lo:hi, :], in_bank(at, hi - lo), ACT.Copy)
                    i.then_inc(sem["pre_out_s"], 1)

            def first_inv_std(h):
                act.wait_ge(sem["var_ready"], h + 1)
                inv_std(0, slice(4 * h, 4 * h + 4), "rstd_ready")

            act.wait_ge(sem["eps_made"], 1)
            first_inv_std(0)
            empty_groups(-1)
            for s in range(STEPS):
                b = chain_row(s, 2 * UB)
                if b is not None:
                    act.wait_ge(sem["o_T"], b + 1)
                    A(oT[:], bank[7][:, 0:P], ACT.Copy).then_inc(sem["o_T_out"], 1)
                b = chain_row(s, 2 * UB + 2)
                if b is not None:
                    act.wait_ge(sem["xn2_T"], b + 1)
                    A(xnT[:, b, :], bank[7][:, 0:P], ACT.Copy).then_inc(sem["xn2_T_out"], 1)
                if s < UNITS:
                    act.wait_ge(sem["max_made"], s + 1)
                    if s >= 3:
                        act.wait_ge(sem["probs_T"], s - 2)
                    for h in range(HG):
                        i = A(probs[s % 3][:, h, :], bank[s % 3][:, h * P:(h + 1) * P], ACT.Exp,
                              bias=neg_max[:, s, h:h + 1])
                    i.then_inc(sem["probs_made"], 1)
                b = chain_row(s, 2 * UB - 2)
                if b is not None:
                    act.wait_ge(sem["heads_out"], UB * (b + 1))
                    if b >= 1:
                        act.wait_ge(sem["heads_back"], b)
                    A(o_headsT[:], in_bank(5 + b % 2), ACT.Copy).then_inc(sem["heads_T_out"], 1)
                b = chain_row(s, 2 * UB)
                if b is not None:
                    act.wait_ge(sem["var_ready"], b + 3)
                    inv_std(1, slice(b, b + 1), "rstd_ready")
                b = chain_row(s, 2 * UB + 2)
                if b is not None:
                    act.wait_ge(sem["gate_hidden"], b + 1)
                    A(relu_out[:], bank[7][:, P:2 * P], ACT.Relu, bias=b_g1[:, 0:1], accum_out=h_sum[:, b:b + 1]
                      ).then_inc(sem["gate_summed"], 1)
                    act.wait_ge(sem["gate_summed"], b + 1)
                if s == 0:
                    first_inv_std(1)
                empty_groups(s)
            act.wait_ge(sem["gate_out"], 1)
            A(gT[:], bank[2][0:E0, 0:B], ACT.Identity, scale=1.0 / S, bias=b_g2[:, 0:1]).then_inc(sem["g_made"], 1)

            empty_groups(END)
            empty_groups(END + 1)
            nc.scalar.preload_act_table_set("gelu_apprx_tanh_and_others")

            act.wait_ge(sem["mb1_made"], 1)
            for b in range(B):
                act.wait_ge(sem["hidden"], b + 1)
                for f in range(FC):
                    i = A(uT[:, b, f, :], bank[b % 2][:, f * P:(f + 1) * P], ACT.Gelu_apprx_tanh, bias=mb1[:, f, b:b + 1])
                i.then_inc(sem["gelu_made"], 1)
            nc.scalar.preload_act_table_set(LN_EXP_SET)

            act.wait_ge(sem["bq_scaled"], 1)
            for s in range(B + 6):
                if 3 <= s < B + 3:
                    b = s - 3
                    act.wait_ge(sem["max1_made"], b + 1)
                    A(p1[:, b, :], bank[4 + b % 2][:, 0:P], ACT.Exp, bias=neg_max1[:, b:b + 1],
                      accum_out=den1[:, b:b + 1]).then_inc(sem["probs1"], 1)
                if 2 <= s < B + 2:
                    b = s - 2
                    act.wait_ge(sem["q_ready"], b + 1)
                    if b >= 2:
                        act.wait_ge(sem["scores1"], b - 1)
                    A(q1T[b % 2][:], bank[2 + b % 2][:, P:2 * P], ACT.Identity, scale=SCALE, bias=b_q[:, 0:1]
                      ).then_inc(sem["q_out"], 1)
                if 5 <= s < B + 5:
                    b = s - 5
                    act.wait_ge(sem["var4_ready"], b + 1)
                    inv_std(3, slice(b, b + 1), "rstd4_ready")
                if 3 <= s < B + 3:
                    b = s - 3
                    act.wait_ge(sem["probs1_T"], b + 1)
                    if b >= 2:
                        act.wait_ge(sem["attn1"], b - 1)
                    A(p1T[b % 2][:], bank[6][:, 0:P], ACT.Copy).then_inc(sem["probs1_T_out"], 1)
                if 1 <= s < B + 1:
                    b = s - 1
                    act.wait_ge(sem["xn3_T"], b + 1)
                    A(xnT[:, b, :], bank[2 + b % 2][:, 0:P], ACT.Copy).then_inc(sem["xn3_T_out"], 1)
                if s < B:
                    act.wait_ge(sem["var3_ready"], s + 1)
                    inv_std(2, slice(s, s + 1), "rstd3_ready")
                if 6 <= s:
                    b = s - 6
                    act.wait_ge(sem["xn4_T"], b + 1)
                    A(xnT[:, b, :], bank[7][:, 0:P], ACT.Copy).then_inc(sem["xn4_T_out"], 1)
            act.wait_ge(sem["logit_max_made"], 1)
            A(score[:], logit_max[:], ACT.Exp, scale=-1.0).then_inc(sem["exp_made"], 1)

            def shared_silu(i):
                act.wait_ge(sem["shared_hidden"], 2 * i + 1)
                A(silu_sh[i], bank[SHARED[i][2]][:], ACT.Silu).then_inc(sem["shared_silu"], 1)

            def scale_rows(lo, hi):
                for b in range(lo, hi):
                    A(x_rows[:, b, 0:D], xn[:, b, :], ACT.Copy, scale=score[:, b:b + 1]).then_inc(sem["rows_scaled"], 1)

            shared_silu(0)
            shared_silu(1)
            act.wait_ge(sem["score_made"], 1)
            scale_rows(0, 4)
            shared_silu(2)
            scale_rows(4, B)
            shared_silu(3)

            act.wait_ge(sem["tiles_made"], 1)
            inner = act.value_load(inner_i[0:1, 0:1], min_val=MIN_INNER, max_val=MAX_INNER)

            def tile_T_out(k, t):
                act.wait_ge(sem["tile_T"], t + 1)
                A(xs_T[k % 2], bank[k % 2][:, 0:P], ACT.Copy).then_inc(sem["tile_T_out"], 1)

            def w_copy(k, t, e):
                if t is not None:
                    act.wait_ge(sem["tile_up"], t - 1)
                A(w_tile[k % 2].rearrange("p c f -> p (c f)"),
                  gate_up[:, bass.ds(e, 1), :].rearrange("p a f -> p (a f)"), ACT.Copy).then_inc(sem["w_copied"], 1)

            def tile_silu(k, t):
                act.wait_ge(sem["tile_gate"], t + 1)
                A(silu_g[k % 2], bank[2 + k % 2][:, 0:F1], ACT.Silu).then_inc(sem["tile_silu"], 1)

            def experts_of(t, n):
                _, e = nc.values_load_multi_w_load_instructions(
                    tile_expert[0:1, bass.ds(t, n)], engines=(mybir.EngineType.Activation,), min_val=0, max_val=E1 - 1,
                    skip_runtime_bounds_check_because="a count, and clamped to the last expert where it is computed")
                return e

            def four(i, n=4):
                e = experts_of(4 * i + 3, n)
                for k in range(n):
                    t = 4 * i + k
                    w_copy(k + 3, t + 3, e[k])
                    tile_T_out(k + 3, t + 3)
                    tile_silu(k + 2, t + 2)

            act.wait_ge(sem["experts_loaded"], 32)
            e = experts_of(0, 3)
            w_copy(0, None, e[0])
            w_copy(1, None, e[1])
            tile_T_out(0, 0)
            tile_T_out(1, 1)
            tile_silu(0, 0)
            w_copy(2, 2, e[2])
            tile_T_out(2, 2)
            tile_silu(1, 1)
            four(0)
            with act.Fori(1, inner) as i:
                four(i)
            four(inner, 2)
            tile_silu(0, 4 * inner + 4)

        @block.vector
        def _(v):
            steps = [0]

            def step(i):
                steps[0] += 1
                i.then_inc(sem["vector_step"], 1)
                v.wait_ge(sem["vector_step"], steps[0])

            def row_stats(n, b):
                step(v.bn_stats(stats[:, b, :], x[:, b, :]))
                return v.bn_aggr(mv[:, n, b, :], stats[:, b, :])

            def normed(n, b, done):
                v.tensor_scalar(xn[:, b, :], x[:, b, :], mv[:, n, b, 0:1], rstd[:, n, b:b + 1],
                                ALU.subtract, ALU.mult).then_inc(sem[done], 1)

            v.wait_ge(sem["ident_made"], 1)
            v.tensor_reduce(head_of[:], ident[:, :].rearrange("p (h d) -> p h d", d=HD), X, ALU.add
                            ).then_inc(sem["heads_made"], 1)
            v.tensor_reduce(same_row[:], ident[:, :].rearrange("p (e r) -> p r e", r=RO), X, ALU.add
                            ).then_inc(sem["vector_step"], 1)
            step(v.tensor_copy(spread[:, :].rearrange("p (e r) -> p e r", r=RO),
                               ident[0:E0, 0:E0].unsqueeze(2).to_broadcast([E0, E0, RO])))
            steps[0] += 1
            v.wait_ge(sem["vector_step"], steps[0])

            def first_stats(h):
                v.wait_ge(sem[f"x_loaded{h}"], 16)
                for b in range(4 * h, 4 * h + 4):
                    i = v.bn_stats(stats[:, b, :], x[:, b, :])
                step(i)
                for b in range(4 * h, 4 * h + 4):
                    i = v.bn_aggr(mv[:, 0, b, :], stats[:, b, :])
                i.then_inc(sem["var_ready"], 1)

            def make_mask(h):
                rows = slice(4 * h, 4 * h + 4)
                v.wait_ge(sem[f"mask_loaded{h}"], 16)
                v.tensor_scalar(mask_b[:, rows, :], mask_i[:, rows, :], 0.0, MASKED_L0, ALU.is_equal, ALU.mult
                                ).then_inc(sem["mask_made"], 1)

            def first_normed(h):
                v.wait_ge(sem["rstd_ready"], h + 1)
                for b in range(4 * h, 4 * h + 4):
                    normed(0, b, "xn_written")

            def empty_groups(s):
                for n, what, j, at, e in groups_at(s, "v"):
                    v.wait_ge(sem["pre_ready"], n + 1)
                    rows = slice(4 * j, 4 * j + 4)
                    if what == "xn":
                        i = v.tensor_scalar(xnT[:, rows, :], in_bank(at), SCALE, None, ALU.mult)
                    elif what == "k":
                        v.wait_ge(sem["small_loaded"], 11 * 16)
                        i = v.tensor_scalar(kT[:, rows, :], in_bank(at), b_k[:, 0:1], None, ALU.add)
                    elif what == "v":
                        v.wait_ge(sem["small_loaded"], 11 * 16)
                        i = v.tensor_tensor(vh[:, rows, :], in_bank(at), b_v[:, :].unsqueeze(1).to_broadcast([P, 4, D]),
                                            ALU.add)
                    elif what == "small":
                        step(v.tensor_copy(gate2T[:], bank[at][:, 0:E0]))
                        i = v.tensor_copy(routerT[:], bank[at][:, E0:E0 + E1])
                    else:
                        lo, hi = W_GROUPS[j]
                        i = v.tensor_copy(w_t[:, lo:hi, :], in_bank(at, hi - lo))
                    i.then_inc(sem["pre_out_v"], 1)

            first_stats(0)
            make_mask(0)
            first_normed(0)
            empty_groups(-1)

            for s in range(STEPS):
                if s < UNITS:
                    v.wait_ge(sem["scores"], s + 1)
                    v.tensor_reduce(neg_max[:, s, :], in_bank(s % 3), X, ALU.max, negate=True).then_inc(sem["max_made"], 1)
                if 2 <= s < UNITS + 2:
                    u = s - 2
                    v.wait_ge(sem["probs_T"], u + 1)
                    if u >= 2:
                        v.wait_ge(sem["heads_out"], u - 1)
                    v.tensor_copy(probsT[u % 2][:], in_bank(3 + u % 2)).then_inc(sem["probs_T_out"], 1)
                b = chain_row(s, 2 * UB - 1)
                if b is not None:
                    heads = bank[5 + b % 2][:, :].rearrange("p (h d) -> p h d", d=32)
                    v.wait_ge(sem["heads_back"], b + 1)
                    step(v.reciprocal(rden[:, b, :], heads[:, :, HD]))
                    if b >= 2:
                        v.wait_ge(sem["o_T"], b - 1)
                    v.tensor_tensor(o_rows[b % 2][:], heads[:, :, 0:HD],
                                    rden[:, b, :].unsqueeze(2).to_broadcast([P, HEADS, HD]), ALU.mult
                                    ).then_inc(sem["o_normed"], 1)
                b = chain_row(s, 2 * UB)
                if b is not None:
                    v.wait_ge(sem["projected"], b + 1)
                    v.wait_ge(sem["x_plus_bout"], 1)
                    v.tensor_tensor(x[:, b, :], bank[7][:, P:2 * P], x[:, b, :], ALU.add).then_inc(sem["x1_made"], 1)
                    v.wait_ge(sem["x1_made"], b + 1)
                    row_stats(1, b).then_inc(sem["var_ready"], 1)
                b = chain_row(s, 2 * UB + 1)
                if b is not None:
                    v.wait_ge(sem["rstd_ready"], b + 3)
                    normed(1, b, "xn2_made")
                if s == 0:
                    first_stats(1)
                if s == 1:
                    make_mask(1)
                    first_normed(1)
                if s == 6:
                    v.wait_ge(sem["small_loaded"], 11 * 16)
                    v.tensor_scalar(pad_f[:], pad_i, 0.0, MASKED_L1, ALU.is_equal, ALU.mult
                                    ).then_inc(sem["pad_copied"], 1)
                empty_groups(s)

            v.wait_ge(sem["g_spread"], 1)
            step(v.tensor_copy(g_col[:], bank[2][:, 16:16 + B]))
            v.tensor_tensor(g_mix[:], g_col[:, :].unsqueeze(2).to_broadcast([P, B, RO]),
                            same_row[:, :].unsqueeze(1).to_broadcast([P, B, RO]), ALU.mult).then_inc(sem["g_mixed"], 1)
            empty_groups(END)
            v.wait_ge(sem["g_spread"], 2)
            v.tensor_tensor(mb1[:], bank[7][:, 0:FC * B].rearrange("p (c b) -> p c b", b=B),
                            b_1[:, :].unsqueeze(2).to_broadcast([P, FC, B]), ALU.add).then_inc(sem["mb1_made"], 1)
            w1_rows = w_t[:, W1:W1 + FC, :].rearrange("p c (q r) -> p (c q) r", r=RO)
            for m in range(16):
                v.wait_ge(sem["mixed"], m + 1)
                src = bank[3 + m % 4][:, :].rearrange("p (j b r) -> p j b r", b=B, r=RO)
                if m < 8:
                    to = mW1T[:, :, 4 * m:4 * m + 4, :]
                    base = w1_rows[:, 4 * m:4 * m + 4, :]
                else:
                    f, h = divmod(m - 8, 2)
                    to = mW2T[:, :, f, 4 * h:4 * h + 4, :]
                    base = w_t[:, W2 + f, :].rearrange("p (q r) -> p q r", r=RO)[:, 4 * h:4 * h + 4, :]
                v.tensor_tensor(to.rearrange("p b j r -> p j b r"), src, base.unsqueeze(2).to_broadcast([P, 4, B, RO]),
                                ALU.add).then_inc(sem["mixed_out"], 1)

            for s in range(B + 6):
                if s < B:
                    v.wait_ge(sem["ffn_out"], s + 1)
                    v.scalar_tensor_tensor(out=x[:, s, :], in0=bank[s % 2][:, 0:P], scalar=tgate[:, 2:3],
                                           in1=x[:, s, :], op0=ALU.mult, op1=ALU.add).then_inc(sem["x2_made"], 1)
                if 3 <= s < B + 3:
                    b = s - 3
                    v.wait_ge(sem["scores1"], b + 1)
                    v.tensor_reduce(neg_max1[:, b:b + 1], bank[4 + b % 2][:, 0:P], X, ALU.max, negate=True
                                    ).then_inc(sem["max1_made"], 1)
                if 6 <= s:
                    b = s - 6
                    v.wait_ge(sem["rstd4_ready"], b + 1)
                    normed(3, b, "xn4_made")
                if 4 <= s < B + 4:
                    b = s - 4
                    v.wait_ge(sem["rden1_made"], b + 1)
                    v.wait_ge(sem["attn1"], b + 1)
                    v.scalar_tensor_tensor(out=x[:, b, :], in0=bank[6][:, P:2 * P], scalar=rden1[:, b:b + 1],
                                           in1=x[:, b, :], op0=ALU.mult, op1=ALU.add).then_inc(sem["x3_made"], 1)
                if 1 <= s < B + 1:
                    b = s - 1
                    v.wait_ge(sem["rstd3_ready"], b + 1)
                    normed(2, b, "xn3_made")
                if s < B:
                    v.wait_ge(sem["x2_made"], s + 1)
                    row_stats(2, s).then_inc(sem["var3_ready"], 1)
                if 3 <= s < B + 3:
                    b = s - 3
                    v.wait_ge(sem["probs1"], b + 1)
                    v.reciprocal(rden1[:, b:b + 1], den1[:, b:b + 1]).then_inc(sem["rden1_made"], 1)
                if 4 <= s < B + 4:
                    b = s - 4
                    v.wait_ge(sem["x3_made"], b + 1)
                    row_stats(3, b).then_inc(sem["var4_ready"], 1)

            v.wait_ge(sem["logits"], 1)
            v.wait_ge(sem["consts_made"], 8)
            logits = bank[7][:, P:P + B * E1].rearrange("p (b e) -> p b e", e=E1)
            experts = expert_no[:, :].unsqueeze(1).to_broadcast([P, B, E1])
            v.tensor_reduce(logit_max[:], logits, X, ALU.max).then_inc(sem["logit_max_made"], 1)
            v.wait_ge(sem["logit_max_made"], 1)
            step(v.tensor_tensor(tmp_be[:], logits, logit_max[:, :].unsqueeze(2).to_broadcast([P, B, E1]), ALU.is_equal))
            step(v.scalar_tensor_tensor(out=tmp_be[:], in0=tmp_be[:], scalar=-float(E1), in1=experts, op0=ALU.mult, op1=ALU.add))
            step(v.tensor_reduce(choice[:], tmp_be[:], X, ALU.min))
            choices = choice[:, :].unsqueeze(2).to_broadcast([P, B, E1])
            numbers = expert_low[:, :].unsqueeze(1).to_broadcast([P, B, E1])
            v.tensor_tensor(one_hot_b[:], numbers, choices, ALU.is_equal).then_inc(sem["one_hot_made"], 1)
            v.tensor_tensor(one_hot[:], numbers, choices, ALU.is_equal).then_inc(sem["vector_step"], 1)
            steps[0] += 1
            v.wait_ge(sem["exp_made"], 1)
            step(v.tensor_scalar(score[:], score[:], 1.0, None, ALU.add))
            v.reciprocal(score[:], score[:]).then_inc(sem["score_made"], 1)

            def shared_act(i):
                f, h, gate_bank, up_bank = SHARED[i]
                v.wait_ge(sem["shared_hidden"], 2 * i + 2)
                v.wait_ge(sem["shared_silu"], i + 1)
                v.tensor_tensor(sharedT[:, f, 4 * h:4 * h + 4, :].rearrange("p b t -> p (b t)"),
                                bank[up_bank][:], silu_sh[i], ALU.mult).then_inc(sem["shared_act"], 1)

            def add_shared(b):
                v.wait_ge(sem["shared_out"], b + 1)
                v.scalar_tensor_tensor(out=x_rows[:, b, ROW:RECORD], in0=bank[OUT_BANKS[b % 4]][:, 0:P],
                                       scalar=tgate[:, 3:4], in1=x[:, b, :], op0=ALU.mult, op1=ALU.add
                                       ).then_inc(sem["acc_made"], 1)

            shared_act(0)
            v.wait_ge(sem["ranks"], 1)
            step(v.tensor_scalar(tiles_i[:], bank[6][:, 256:256 + E1], float(P - 1), None, ALU.add))
            step(v.tensor_scalar(tiles_i[:], tiles_i[:], 7, None, ALU.logical_shift_right))
            step(v.tensor_tensor(tmp_ee[:], lower[:], tiles_i[:, :].unsqueeze(1).to_broadcast([P, E1, E1]), ALU.mult))
            shared_act(1)
            step(v.tensor_reduce(first[:], tmp_ee[:], X, ALU.add))
            ranks = bank[6][:, 128:128 + B * E1].rearrange("p (b e) -> p b e", e=E1)
            step(v.scalar_tensor_tensor(out=tmp_be[:], in0=first[:, :].unsqueeze(1).to_broadcast([P, B, E1]),
                                        scalar=float(P), in1=ranks, op0=ALU.mult, op1=ALU.add))
            step(v.tensor_tensor(tmp_be[:], tmp_be[:], one_hot[:], ALU.mult))
            with nc.allow_low_precision("whole numbers"):
                v.tensor_reduce(slot_i[:], tmp_be[:], X, ALU.add).then_inc(sem["slots_made"], 1)
            for b in range(4):
                add_shared(b)
            shared_act(2)
            step(v.tensor_tensor(end_tile[:], first[:], tiles_i[:], ALU.add))
            step(v.tensor_tensor(tmp_te[:], tile_no[:, :].unsqueeze(2).to_broadcast([P, LOADED, E1]),
                                 end_tile[:, :].unsqueeze(1).to_broadcast([P, LOADED, E1]), ALU.is_ge))
            shared_act(3)
            for b in range(4, B):
                add_shared(b)
            step(v.tensor_reduce(tile_expert_f[:], tmp_te[:], X, ALU.add))
            step(v.tensor_scalar(tile_expert[:], tile_expert_f[:], float(E1 - 1), None, ALU.min))
            step(v.tensor_scalar(inner_i[:], end_tile[:, E1 - 1:E1], -2.0, float(4 * MIN_INNER), ALU.add, ALU.max))
            v.tensor_scalar(inner_i[:], inner_i[:], 2, None, ALU.logical_shift_right).then_inc(sem["tiles_made"], 1)

            v.wait_ge(sem["tiles_made"], 1)
            inner = v.value_load(inner_i[0:1, 0:1], min_val=MIN_INNER, max_val=MAX_INNER)

            def tile_copy(k, t, first=False):
                if not first:
                    v.wait_ge(sem["tile_T"], t - 1)
                v.tensor_copy(xs_in[k % 2][:], sorted_in[:, bass.ds(t, 1), 0:D].rearrange("p a d -> p (a d)")
                              ).then_inc(sem["tile_copied"], 1)

            def tile_act(k, t):
                v.wait_ge(sem["tile_silu"], t + 1)
                v.wait_ge(sem["tile_up"], t + 1)
                v.tensor_tensor(act_T[k % 2].rearrange("p c t -> p (c t)"), bank[4 + k % 2][:, 0:F1], silu_g[k % 2],
                                ALU.mult).then_inc(sem["tile_act"], 1)

            def y_scaled(k, t, scattered):
                if scattered is not None:
                    v.wait_ge(y_scattered[k], scattered)
                v.tensor_copy(token_of[k][:], sorted_in[:, bass.ds(t, 1), D:ROW].rearrange("p a d -> p (a d)").bitcast(I32)).then_inc(sem["y_ready"], 1)
                v.wait_ge(sem["tile_y"], t + 1)
                v.scalar_tensor_tensor(out=y_out[k], in0=bank[6 + k % 2][:, 0:P], scalar=tgate[:, 3:4],
                                       in1=acc_in[:, bass.ds(t, 1), :].rearrange("p a d -> p (a d)"),
                                       op0=ALU.mult, op1=ALU.add).then_inc(sem["y_ready"], 1)

            def four(i, first=False, last=False):
                for k in range(4):
                    t = 4 * i + k
                    tile_act(k + 1, t + 1)
                    if first and k == 1:
                        v.wait_ge(sem["tiles_loaded2"], 16)
                    if not last or k == 0:
                        tile_copy(k + 4, t + 4)
                    if first and k == 0:
                        v.wait_ge(sem["acc_loaded0"], 16)
                    if first and k == 2:
                        v.wait_ge(sem["acc_loaded1"], 16)
                    y_scaled(k, t, None if first else 16 * i)

            v.wait_ge(sem["tiles_loaded0"], 16)
            tile_copy(0, 0, first=True)
            tile_copy(1, 1, first=True)
            v.wait_ge(sem["tiles_loaded1"], 16)
            tile_copy(2, 2)
            tile_act(0, 0)
            tile_copy(3, 3)
            four(0, first=True)
            v.wait_ge(sem["acc_loaded2"], 16)
            with v.Fori(1, inner) as i:
                four(i)
            four(inner, last=True)
            y_scaled(0, 4 * inner + 4, 16 * inner + 16)

        @block.tensor
        def _(pe):
            mm = pe.matmul

            def transpose(to, rows):
                n = rows.shape[0]
                return pe.transpose(to, rows, ident[0:n, 0:n])

            def col(i, n=1):
                return slice(i * P, (i + n) * P)

            def run_groups(s):
                for n, what, j, at, e in groups_at(s):
                    before_it = [g for g in GROUPS[:n] if g[3] == at]
                    if at == 7 and before_it:
                        pe.wait_ge(*pre_emptied(*before_it[-1][1:3]))
                    if at < 7 and s > 0:
                        if at in (3, 4):
                            pe.wait_ge(sem["probs_T_out"], UNITS)
                        elif before_it[-1][0] > 0:
                            pe.wait_ge(*pre_emptied(*before_it[-1][1:3]))
                        else:
                            pe.wait_ge(sem["probs_made"], UNITS)
                    to = bank[at]
                    if what == "cT":
                        pe.wait_ge(sem[f"c_loaded{j}"], 16)
                        for m in range(4):
                            i = transpose(to[:, col(m)], c[:, 4 * j + m, :])
                    elif what == "xn":
                        pe.wait_ge(sem["xn_written"], 4 * j + 4)
                        for m in range(4):
                            i = transpose(to[:, col(m)], xn[:, 4 * j + m, :])
                    elif what == "w":
                        pe.wait_ge(sem["w_loaded"], 12 * 16)
                        lo, hi = W_GROUPS[j]
                        for m in range(hi - lo):
                            i = transpose(to[:, col(m)], w_raw[:, lo + m, :])
                    elif what == "small":
                        transpose(to[:, 0:E0], w_small[0:E0, 0, :])
                        i = transpose(to[:, E0:E0 + E1], w_small[0:E1, 1, :])
                    elif what == "k":
                        pe.wait_ge(*pre_emptied("w", 1))
                        i = mm(to[:], w_t[:, WK, :], cT[:, 4 * j:4 * j + 4, :], start=True, stop=True)
                    else:
                        for m in range(4):
                            i = mm(to[:, col(m)], cT[:, 4 * j + m, :], w_t[:, WV, :], start=True, stop=True)
                    i.then_inc(sem["pre_ready"], 1)

            pe.wait_ge(sem["ident_made"], 1)
            run_groups(-1)
            pe.wait_ge(*pre_emptied("cT", 1))
            pe.wait_ge(*pre_emptied("xn", 0))
            pe.wait_ge(sem["mask_made"], 1)
            pe.wait_ge(sem["consts_bf16"], 1)

            for s in range(STEPS):
                if s < UNITS:
                    b, g = divmod(s, UB)
                    pe.wait_ge(sem["keys_made"], g + 1 if b == 0 else UB + b)
                    if s == UNITS // 2:
                        pe.wait_ge(*pre_emptied("xn", 1))
                        pe.wait_ge(sem["mask_made"], 2)
                    if s >= 3:
                        pe.wait_ge(sem["probs_made"], s - 2)
                    mm(bank[s % 3][:], xnT[:, b, :], keys[b % 2][:, HG * g:HG * g + HG, :], start=True, stop=False)
                    mm(bank[s % 3][:], ident_b[:], mask_b[:, b:b + 1, :].to_broadcast([P, HG, P]), start=False,
                       stop=True).then_inc(sem["scores"], 1)
                b = chain_row(s, 2 * UB)
                if b is not None:
                    pe.wait_ge(sem["o_normed"], b + 1)
                    if b == 0:
                        pe.wait_ge(*pre_emptied("xn", 1))
                    else:
                        pe.wait_ge(sem["gate_summed"], b)
                    transpose(bank[7][:, 0:P], o_rows[b % 2][:, :, :].rearrange("p h d -> p (h d)")
                              ).then_inc(sem["o_T"], 1)
                b = chain_row(s, 2 * UB + 2)
                if b is not None:
                    pe.wait_ge(sem["xn2_made"], b + 1)
                    transpose(bank[7][:, 0:P], xn[:, b, :]).then_inc(sem["xn2_T"], 1)
                if 2 <= s < UNITS + 2:
                    u = s - 2
                    pe.wait_ge(sem["probs_made"], u + 1)
                    if u >= 2:
                        pe.wait_ge(sem["probs_T_out"], u - 1)
                    for h in range(HG):
                        n = transpose(bank[3 + u % 2][:, col(h)], probs[u % 3][:, h, :])
                    n.then_inc(sem["probs_T"], 1)
                b = chain_row(s, 2 * UB - 1)
                if b is not None:
                    pe.wait_ge(sem["heads_T_out"], b + 1)
                    for g in range(UB):
                        n = transpose(bank[5 + b % 2][:, col(g)], o_headsT[:, g, :])
                    n.then_inc(sem["heads_back"], 1)
                if 3 <= s < UNITS + 3:
                    u = s - 3
                    b, g = divmod(u, UB)
                    pe.wait_ge(sem["probs_T_out"], u + 1)
                    pe.wait_ge(sem["vals_made"], b + 1)
                    if g == 0 and b >= 2:
                        pe.wait_ge(sem["o_normed"], b - 1)
                    for h in range(HG):
                        n = mm(bank[5 + b % 2][32 * h:32 * h + 32, col(g)], vals[b % 2][:, HG * g + h, :],
                               probsT[u % 2][:, h, :], start=True, stop=True)
                    n.then_inc(sem["heads_out"], 1)
                b = chain_row(s, 2 * UB)
                if b is not None:
                    pe.wait_ge(sem["o_T_out"], b + 1)
                    pe.wait_ge(sem["wout_scaled"], 1)
                    mm(bank[7][:, col(1)], oT[:], w_t[:, WO, :], start=True, stop=True).then_inc(sem["projected"], 1)
                b = chain_row(s, 2 * UB + 2)
                if b is not None:
                    pe.wait_ge(sem["xn2_T_out"], b + 1)
                    mm(bank[7][:, col(1)], w_t[:, GW1, :], xnT[:, b, :], start=True, stop=True).then_inc(sem["gate_hidden"], 1)

                run_groups(s)

            pe.wait_ge(sem["gate_summed"], B)
            mm(bank[2][0:E0, 0:B], gate2T[:], h_sum[:], start=True, stop=True).then_inc(sem["gate_out"], 1)
            run_groups(END)
            pe.wait_ge(sem["g_made"], 1)
            mm(bank[2][:, 16:16 + B], spread[:], gT[:], start=True, stop=True).then_inc(sem["g_spread"], 1)
            for f in range(FC):
                n = mm(bank[7][:, f * B:(f + 1) * B], tb1[:, col(f)], gT[:], start=True, stop=True)
            n.then_inc(sem["g_spread"], 1)
            run_groups(END + 1)
            pe.wait_ge(*pre_emptied("w", 3))
            pe.wait_ge(sem["g_mixed"], 1)
            pe.wait_ge(sem["tw1_loaded"], 16 * E0)
            pe.wait_ge(sem["tw2_loaded"], 16 * E0)

            def mix(m):
                if m >= 4:
                    pe.wait_ge(sem["mixed_out"], m - 3)
                for j in range(4):
                    f, h = divmod(m - 8, 2)
                    w = tw1[:, 4 * m + j, :] if m < 8 else tw2[:, 4 * h + j, col(f)]
                    n = mm(bank[3 + m % 4][:, col(j)], w, g_mix[:], start=True, stop=True)
                n.then_inc(sem["mixed"], 1)

            for m in range(10):
                mix(m)
            pe.wait_ge(*pre_emptied("w", 5))
            pe.wait_ge(sem["mixed_out"], 8)
            for b in range(B):
                if b >= 2:
                    pe.wait_ge(sem["gelu_made"], b - 1)
                for f in range(FC):
                    n = mm(bank[b % 2][:, col(f)], mW1T[:, b, :, :].rearrange("p q r -> p (q r)")[:, col(f)],
                           xnT[:, b, :], start=True, stop=True)
                n.then_inc(sem["hidden"], 1)
                if b < B - 2:
                    mix(10 + b)
            pe.wait_ge(sem["mixed_out"], 16)
            pe.wait_ge(sem["pad_made"], 1)
            pe.wait_ge(sem["vh_scaled"], 1)
            pe.wait_ge(sem["g_rows_made"], 1)

            def shared_part(w, h, at):
                mm(bank[at][:], w_t[:, w, :], xnT[:, 4 * h:4 * h + 4, :], start=True, stop=True
                   ).then_inc(sem["shared_hidden"], 1)

            for s in range(B + 8):
                if s < B:
                    pe.wait_ge(sem["gelu_made"], B - 1 + s if s < 2 else s + 1)
                    if s >= 2:
                        pe.wait_ge(sem["x2_made"], s - 1)
                    o = bank[s % 2][:, 0:P]
                    for f in range(FC):
                        mm(o, uT[:, s, f, :], mW2T[:, s, f, :, :].rearrange("p q r -> p (q r)"), start=(f == 0), stop=False)
                    mm(o, g_rows[:, s, :], tb2[:], start=False, stop=True).then_inc(sem["ffn_out"], 1)
                if 8 <= s:
                    b = s - 8
                    pe.wait_ge(sem["xn4_T_out"], b + 1)
                    n = mm(bank[7][:, P + b * E1:P + (b + 1) * E1], xnT[:, b, :], routerT[:], start=True, stop=True)
                    if b == B - 1:
                        n.then_inc(sem["logits"], 1)
                if 4 <= s < B + 4:
                    b = s - 4
                    pe.wait_ge(sem["probs1"], b + 1)
                    if b >= 1:
                        pe.wait_ge(sem["x3_made"], b)
                    transpose(bank[6][:, 0:P], p1[:, b, :]).then_inc(sem["probs1_T"], 1)
                if 2 <= s < B + 2:
                    b = s - 2
                    pe.wait_ge(sem["xn3_made"], b + 1)
                    if b >= 2:
                        pe.wait_ge(sem["q_out"], b - 1)
                    transpose(bank[2 + b % 2][:, 0:P], xn[:, b, :]).then_inc(sem["xn3_T"], 1)
                if 3 <= s < B + 3:
                    b = s - 3
                    pe.wait_ge(sem["q_out"], b + 1)
                    if b >= 2:
                        pe.wait_ge(sem["probs1"], b - 1)
                    o = bank[4 + b % 2][:, 0:P]
                    mm(o, q1T[b % 2][:], kT[:, b, :], start=True, stop=False)
                    mm(o, ident_b[:], pad_b[:, b, :], start=False, stop=True).then_inc(sem["scores1"], 1)
                if 7 <= s < B + 7:
                    b = s - 7
                    pe.wait_ge(sem["xn4_made"], b + 1)
                    transpose(bank[7][:, 0:P], xn[:, b, :]).then_inc(sem["xn4_T"], 1)
                if 4 <= s < B + 4:
                    b = s - 4
                    pe.wait_ge(sem["probs1_T_out"], b + 1)
                    mm(bank[6][:, col(1)], p1T[b % 2][:], vh[:, b, :], start=True, stop=True).then_inc(sem["attn1"], 1)
                if 2 <= s < B + 2:
                    b = s - 2
                    pe.wait_ge(sem["xn3_T_out"], b + 1)
                    mm(bank[2 + b % 2][:, col(1)], w_t[:, WQ, :], xnT[:, b, :], start=True, stop=True
                       ).then_inc(sem["q_ready"], 1)
                if s == B + 4:
                    pe.wait_ge(sem["x2_made"], B)
                    shared_part(WG, 0, 0)
                if s == B + 6:
                    shared_part(WU, 0, 1)

            def shared(i):
                f, h, gate_bank, up_bank = SHARED[i]
                for w, at in ((WG, gate_bank), (WU, up_bank)):
                    shared_part(w + f, h, at)

            pe.wait_ge(sem["q_out"], B)
            shared_part(WG + 1, 0, 2)
            pe.wait_ge(sem["one_hot_made"], 1)
            pe.wait_ge(sem["consts_bf16"], 3)
            mm(bank[6][:, P:P + B * E1], before[:], one_hot_b[:], start=True, stop=False, skip_group_check=True)
            for b in range(B - 1):
                mm(bank[6][:, P + (b + 1) * E1:P + B * E1], ones_b[:],
                   one_hot_b[:, b:b + 1, :].to_broadcast([P, B - 1 - b, E1]), start=False, stop=(b == B - 2),
                   skip_group_check=True)
            for b in range(B):
                n = mm(bank[6][:, 256:256 + E1], ones_b[:], one_hot_b[:, b, :], start=False, stop=(b == B - 1),
                       skip_group_check=True)
            n.then_inc(sem["ranks"], 1)

            def shared_down(h):
                for b in range(4 * h, 4 * h + 4):
                    if b == 3:
                        pe.wait_ge(sem["slots_made"], 1)
                    if b >= 4:
                        pe.wait_ge(sem["acc_made"], b - 3)
                    for f in range(C1):
                        n = mm(bank[OUT_BANKS[b % 4]][:, 0:P], sharedT[:, f, b, :], w_t[:, WD + f, :],
                               start=(f == 0), stop=(f == C1 - 1))
                    n.then_inc(sem["shared_out"], 1)

            shared_part(WU + 1, 0, 3)
            shared(2)
            pe.wait_ge(sem["shared_act"], 2)
            shared_down(0)
            shared(3)
            pe.wait_ge(sem["shared_act"], 4)
            shared_down(1)

            for _ in range(9):
                mm(bank[0][:], ident[:], w_t[:, WG:WG + 4, :], start=True, stop=True)

            pe.wait_ge(sem["experts_loaded"], 32)
            pe.wait_ge(sem["acc_made"], B)
            pe.wait_ge(sem["tiles_made"], 1)
            inner = pe.value_load(inner_i[0:1, 0:1], min_val=MIN_INNER, max_val=MAX_INNER)

            def experts_of(t, n):
                _, e = nc.values_load_multi_w_load_instructions(
                    tile_expert[0:1, bass.ds(t, n)], engines=(mybir.EngineType.PE,), min_val=0, max_val=E1 - 1,
                    skip_runtime_bounds_check_because="a count, and clamped to the last expert where it is computed")
                return e

            def tile_transpose(k, t):
                pe.wait_ge(sem["tile_copied"], t + 1)
                transpose(bank[k % 2][:, 0:P], xs_in[k % 2][:]).then_inc(sem["tile_T"], 1)

            def tile_hidden(k, t):
                pe.wait_ge(sem["tile_T_out"], t + 1)
                pe.wait_ge(sem["w_copied"], t + 1)
                for at, half, done in ((2, 0, "tile_gate"), (4, C1, "tile_up")):
                    for f in range(C1):
                        n = mm(bank[at + k % 2][:, col(f)], w_tile[k % 2][:, half + f, :], xs_T[k % 2], start=True, stop=True)
                    n.then_inc(sem[done], 1)

            def tile_down(k, t, e, first=False):
                pe.wait_ge(sem["tile_act"], t + 1)
                if not first:
                    pe.wait_ge(sem["y_ready"], 2 * t)
                for f in range(C1):
                    n = mm(bank[6 + k % 2][:, 0:P], act_T[k % 2][:, f, :],
                           down[:, bass.ds(e, 1), f, :].rearrange("p a h -> p (a h)"), start=(f == 0), stop=(f == C1 - 1))
                n.then_inc(sem["tile_y"], 1)

            tile_transpose(0, 0)
            tile_transpose(1, 1)
            tile_hidden(0, 0)
            tile_transpose(2, 2)
            tile_hidden(1, 1)

            def four(i, first=False, last=False):
                e = experts_of(4 * i, 5 if last else 4)
                for k in range(4):
                    t = 4 * i + k
                    tile_down(k, t, e[k], first and k == 0)
                    if not last or k < 2:
                        tile_transpose(k + 3, t + 3)
                    if not last or k < 3:
                        tile_hidden(k + 2, t + 2)
                if last:
                    tile_down(0, t + 1, e[4])

            four(0, first=True)
            with pe.Fori(1, inner) as i:
                four(i)
            four(inner, last=True)


_INS = ['x', 'ctx_1024', 'mask_Bx1xSxS2_ik1', 'mask_BxS2_if1', 'g_xattn', 'g_ffn', 'L0_xattn_w_out', 'L0_xattn_b_out',
        'L0_ffn_gate_w1', 'L0_ffn_gate_b1', 'L0_ffn_gate_w2', 'L0_ffn_gate_b2', 'L0_ffn_W1', 'L0_ffn_b1', 'L0_ffn_W2',
        'L0_ffn_b2', 'L0_ffn_TW1', 'L0_ffn_Tb1', 'L0_ffn_TW2', 'L0_ffn_Tb2', 'L1_xattn_Wq_w', 'L1_xattn_Wq_b',
        'L1_xattn_Wk_w', 'L1_xattn_Wk_b', 'L1_xattn_Wv_w', 'L1_xattn_Wv_b', 'L1_ffn_w_router', 'L1_ffn_gate_up_proj',
        'L1_ffn_down_proj', 'L1_ffn_w_gate', 'L1_ffn_w_up', 'L1_ffn_w_down']


def kernel(**inputs):
    import numpy as _np
    import concourse.bacc as _bacc
    from concourse import mybir as _mybir
    from concourse.bass_utils import run_bass_kernel_spmd as _run

    nc = _bacc.Bacc("TRN2", target_bir_lowering=False, num_devices=1)
    arrays, args = {}, {}
    for name in _INS:
        arr = _np.ascontiguousarray(inputs[name])
        arrays[f"in_{name}"] = arr
        args[name] = nc.dram_tensor(f"in_{name}", arr.shape, _mybir.dt.from_np(arr.dtype), kind="ExternalInput").ap()
    out = nc.dram_tensor("out_x", inputs["x"].shape, _mybir.dt.float32, kind="ExternalOutput").ap()
    flamingo_gated_blocks(nc, args, out)
    r = _run(nc, [arrays], core_ids=[0])
    return r.results[0]["out_x"]
```
